# Optimizing a Trainium2 kernel written in Bass

```python
import numpy as np
import jax
import jax.numpy as jnp

def _softmax(x, axis=-1):
    return jax.nn.softmax(x, axis=axis)

def _gelu(x):
    return jax.nn.gelu(x, approximate=True)

def _silu(x):
    return jax.nn.silu(x)

def _sigmoid(x):
    return jax.nn.sigmoid(x)

def _layernorm(x, axis=-1, eps=1e-05):
    m = jnp.mean(x, axis=axis, keepdims=True)
    v = jnp.var(x, axis=axis, keepdims=True)
    return (x - m) / jnp.sqrt(v + eps)

def _scatter_add(tgt, idx, src, axis=0):
    return tgt.at[idx].add(src)

def _segment_sum(src, seg, n):
    return jax.ops.segment_sum(src, seg, n)
kernel_name = 'mk_audio_tower_d1_tok_audfeat256_r4_e3303e'

def setup_inputs(seed: int=0):
    np.random.seed(seed)
    _w = jnp.asarray

    def _rec_inputs():
        import jax
        import jax.numpy as jnp
        _rk = jax.random.key(seed)
        x = -0.00197248 + 1.00072 * jax.random.normal(jax.random.fold_in(_rk, 1), (32, 1, 10240), jnp.float32)
        return x
    x = _rec_inputs()

    def _L0_tok_setup():
        import jax, jax.numpy as jnp
        import numpy as np
        B, L = (4, 10240)
        C = 128
        DMLP = 512
        TEMP = 1e-05
        EPS = 1e-05
        FACTOR = 2

        def _conv(x, w, b, stride, pad):
            x = jnp.pad(x, ((0, 0), (0, 0), (pad, pad)), mode='reflect')
            y = jax.lax.conv_general_dilated(x, w, (stride,), 'VALID', dimension_numbers=('NCH', 'OIH', 'NCH'))
            return y + b[None, :, None]

        def _cnorm(x, g, b):
            m = jnp.mean(x, axis=1, keepdims=True)
            v = jnp.var(x, axis=1, keepdims=True, ddof=1)
            return (x - m) * jax.lax.rsqrt(v + EPS) * g[None, :, None] + b[None, :, None]

        def _forward(x, conv0_w, conv0_b, conv1_w, conv1_b, conv2_w, conv2_b, conv3_w, conv3_b, n0_w, n0_b, n1_w, n1_b, n2_w, n2_b, n3_w, n3_b, n4_w, n4_b, mlp_w1, mlp_b1, mlp_w2, mlp_b2, mlp_w3, mlp_b3):
            h = jax.nn.relu(_cnorm(_conv(x, conv0_w, conv0_b, 5, 3), n0_w, n0_b))
            h = jax.nn.relu(_cnorm(_conv(h, conv1_w, conv1_b, 4, 2), n1_w, n1_b))
            h = jax.nn.relu(_cnorm(_conv(h, conv2_w, conv2_b, 2, 1), n2_w, n2_b))
            h = jax.nn.relu(_cnorm(_conv(h, conv3_w, conv3_b, 2, 1), n3_w, n3_b))
            f = jnp.transpose(h, (0, 2, 1))
            T = f.shape[1]
            z = jax.nn.gelu(f @ mlp_w1 + mlp_b1, approximate=False)
            z = jax.nn.gelu(z @ mlp_w2 + mlp_b2, approximate=False)
            imp = jax.nn.sigmoid((z @ mlp_w3 + mlp_b3)[..., 0]) + TEMP
            imp = imp / jnp.sum(imp, axis=1, keepdims=True) * (T / FACTOR)
            Tn = T // FACTOR
            cs = jnp.cumsum(imp, axis=1)
            p = jnp.maximum(cs[:, :, None] - jnp.arange(Tn, dtype=cs.dtype)[None, None, :], 0.0)
            pc = jnp.pad(p, ((0, 0), (0, 0), (0, 1)))
            d = pc[:, :, :-1] - pc[:, :, 1:]
            wmat = d - jnp.pad(d, ((0, 0), (1, 0), (0, 0)))[:, :-1, :]
            pooled = jnp.einsum('btn,btc->bnc', wmat, f)
            out = jnp.transpose(pooled, (0, 2, 1))
            return jax.nn.relu(_cnorm(out, n4_w, n4_b))
        key = jax.random.key(seed)
        ks = jax.random.split(key, 8)

        def w(k, shape, fan_in):
            return jax.random.normal(k, shape, jnp.float32) / np.float32(np.sqrt(fan_in))
        inp = {'x': jax.random.normal(ks[0], (B, 1, L), jnp.float32), 'conv0_w': w(ks[1], (C, 1, 10), 10), 'conv0_b': jnp.zeros(C, jnp.float32), 'conv1_w': w(ks[2], (C, C, 8), C * 8), 'conv1_b': jnp.zeros(C, jnp.float32), 'conv2_w': w(ks[3], (C, C, 4), C * 4), 'conv2_b': jnp.zeros(C, jnp.float32), 'conv3_w': w(ks[4], (C, C, 4), C * 4), 'conv3_b': jnp.zeros(C, jnp.float32), 'mlp_w1': w(ks[5], (C, DMLP), C), 'mlp_b1': jnp.zeros(DMLP, jnp.float32), 'mlp_w2': w(ks[6], (DMLP, DMLP), DMLP), 'mlp_b2': jnp.zeros(DMLP, jnp.float32), 'mlp_w3': w(ks[7], (DMLP, 1), DMLP), 'mlp_b3': jnp.zeros(1, jnp.float32)}
        for i in range(5):
            inp[f'n{i}_w'] = jnp.ones(C, jnp.float32)
            inp[f'n{i}_b'] = jnp.zeros(C, jnp.float32)
        return inp
    _L0_tok_all = _L0_tok_setup()
    _L0_tok_in = {k: v for k, v in _L0_tok_all.items() if k in ('conv0_w', 'conv0_b', 'conv1_w', 'conv1_b', 'conv2_w', 'conv2_b', 'conv3_w', 'conv3_b', 'n0_w', 'n0_b', 'n1_w', 'n1_b', 'n2_w', 'n2_b', 'n3_w', 'n3_b', 'n4_w', 'n4_b', 'mlp_w1', 'mlp_b1', 'mlp_w2', 'mlp_b2', 'mlp_w3', 'mlp_b3')}
    del _L0_tok_all

    def _L0_attn_setup():
        import jax, jax.numpy as jnp
        import numpy as np
        D_K = 64
        SPARSITY = 0.5
        key = jax.random.key(seed)
        k1, k2, k3, k4, k5 = jax.random.split(key, 5)
        B, N, d_model, d_k, d_v = (4, 1024, 64, 64, 64)
        x = jax.random.normal(k1, (B, N, d_model), dtype=jnp.float32)
        W_qkv = jax.random.normal(k2, (d_model, 2 * d_k + d_v), dtype=jnp.float32) * 0.02
        b_qkv = jnp.zeros((2 * d_k + d_v,), dtype=jnp.float32)
        W_out = jax.random.normal(k3, (d_v, d_model), dtype=jnp.float32) * 0.02
        b_out = jnp.zeros((d_model,), dtype=jnp.float32)
        return {'x': x, 'W_qkv': W_qkv, 'b_qkv': b_qkv, 'W_out': W_out, 'b_out': b_out}
    _L0_attn_all = _L0_attn_setup()
    _L0_attn_in = {k: v for k, v in _L0_attn_all.items() if k in ('W_qkv', 'b_qkv', 'W_out', 'b_out')}
    del _L0_attn_all

    def _L0_ffn_setup():
        import jax, jax.numpy as jnp
        import numpy as np
        B, T, IN_DIM = (64, 64, 64)
        HID, OUT_DIM = (128, 64)
        N_LAYERS, N_EXPERTS, N_SHARED = (2, 16, 1)
        key = jax.random.key(seed)
        ks = jax.random.split(key, 10)
        s = 0.02
        x = jax.random.normal(ks[0], (B, T, IN_DIM), dtype=jnp.float32)
        route_id = jax.random.randint(ks[1], (B,), 0, N_EXPERTS)
        Wi = jax.random.normal(ks[2], (HID, IN_DIM), dtype=jnp.float32) * s
        bi = jnp.zeros((HID,), dtype=jnp.float32)
        Wr = jax.random.normal(ks[3], (N_LAYERS, N_EXPERTS, HID, HID), dtype=jnp.float32) * s
        br = jax.random.normal(ks[4], (N_LAYERS, N_EXPERTS, HID), dtype=jnp.float32) * s
        Ws = jax.random.normal(ks[5], (N_LAYERS, N_SHARED, HID, HID), dtype=jnp.float32) * s
        bs = jax.random.normal(ks[6], (N_LAYERS, N_SHARED, HID), dtype=jnp.float32) * s
        Wo = jax.random.normal(ks[7], (OUT_DIM, HID), dtype=jnp.float32) * s
        bo = jnp.zeros((OUT_DIM,), dtype=jnp.float32)
        return {'x': x, 'route_id': route_id, 'Wi': Wi, 'bi': bi, 'Wr': Wr, 'br': br, 'Ws': Ws, 'bs': bs, 'Wo': Wo, 'bo': bo}
    _L0_ffn_all = _L0_ffn_setup()
    _L0_ffn_in = {k: v for k, v in _L0_ffn_all.items() if k in ('route_id', 'Wi', 'bi', 'Wr', 'br', 'Ws', 'bs', 'Wo', 'bo')}
    del _L0_ffn_all
    return {'x': x, 'L0_tok_conv0_w': _L0_tok_in['conv0_w'], 'L0_tok_conv0_b': _L0_tok_in['conv0_b'], 'L0_tok_conv1_w': _L0_tok_in['conv1_w'], 'L0_tok_conv1_b': _L0_tok_in['conv1_b'], 'L0_tok_conv2_w': _L0_tok_in['conv2_w'], 'L0_tok_conv2_b': _L0_tok_in['conv2_b'], 'L0_tok_conv3_w': _L0_tok_in['conv3_w'], 'L0_tok_conv3_b': _L0_tok_in['conv3_b'], 'L0_tok_n0_w': _L0_tok_in['n0_w'], 'L0_tok_n0_b': _L0_tok_in['n0_b'], 'L0_tok_n1_w': _L0_tok_in['n1_w'], 'L0_tok_n1_b': _L0_tok_in['n1_b'], 'L0_tok_n2_w': _L0_tok_in['n2_w'], 'L0_tok_n2_b': _L0_tok_in['n2_b'], 'L0_tok_n3_w': _L0_tok_in['n3_w'], 'L0_tok_n3_b': _L0_tok_in['n3_b'], 'L0_tok_n4_w': _L0_tok_in['n4_w'], 'L0_tok_n4_b': _L0_tok_in['n4_b'], 'L0_tok_mlp_w1': _L0_tok_in['mlp_w1'], 'L0_tok_mlp_b1': _L0_tok_in['mlp_b1'], 'L0_tok_mlp_w2': _L0_tok_in['mlp_w2'], 'L0_tok_mlp_b2': _L0_tok_in['mlp_b2'], 'L0_tok_mlp_w3': _L0_tok_in['mlp_w3'], 'L0_tok_mlp_b3': _L0_tok_in['mlp_b3'], 'L0_attn_W_qkv': _L0_attn_in['W_qkv'], 'L0_attn_b_qkv': _L0_attn_in['b_qkv'], 'L0_attn_W_out': _L0_attn_in['W_out'], 'L0_attn_b_out': _L0_attn_in['b_out'], 'L0_ffn_route_id': _L0_ffn_in['route_id'], 'L0_ffn_Wi': _L0_ffn_in['Wi'], 'L0_ffn_bi': _L0_ffn_in['bi'], 'L0_ffn_Wr': _L0_ffn_in['Wr'], 'L0_ffn_br': _L0_ffn_in['br'], 'L0_ffn_Ws': _L0_ffn_in['Ws'], 'L0_ffn_bs': _L0_ffn_in['bs'], 'L0_ffn_Wo': _L0_ffn_in['Wo'], 'L0_ffn_bo': _L0_ffn_in['bo']}

def reference(x, L0_tok_conv0_w, L0_tok_conv0_b, L0_tok_conv1_w, L0_tok_conv1_b, L0_tok_conv2_w, L0_tok_conv2_b, L0_tok_conv3_w, L0_tok_conv3_b, L0_tok_n0_w, L0_tok_n0_b, L0_tok_n1_w, L0_tok_n1_b, L0_tok_n2_w, L0_tok_n2_b, L0_tok_n3_w, L0_tok_n3_b, L0_tok_n4_w, L0_tok_n4_b, L0_tok_mlp_w1, L0_tok_mlp_b1, L0_tok_mlp_w2, L0_tok_mlp_b2, L0_tok_mlp_w3, L0_tok_mlp_b3, L0_attn_W_qkv, L0_attn_b_qkv, L0_attn_W_out, L0_attn_b_out, L0_ffn_route_id, L0_ffn_Wi, L0_ffn_bi, L0_ffn_Wr, L0_ffn_br, L0_ffn_Ws, L0_ffn_bs, L0_ffn_Wo, L0_ffn_bo):
    import jax
    import jax.numpy as jnp

    def _L0_tok_ref(x, conv0_w, conv0_b, conv1_w, conv1_b, conv2_w, conv2_b, conv3_w, conv3_b, n0_w, n0_b, n1_w, n1_b, n2_w, n2_b, n3_w, n3_b, n4_w, n4_b, mlp_w1, mlp_b1, mlp_w2, mlp_b2, mlp_w3, mlp_b3):
        import jax, jax.numpy as jnp
        import numpy as np
        B, L = (4, 10240)
        C = 128
        DMLP = 512
        TEMP = 1e-05
        EPS = 1e-05
        FACTOR = 2

        def _conv(x, w, b, stride, pad):
            x = jnp.pad(x, ((0, 0), (0, 0), (pad, pad)), mode='reflect')
            y = jax.lax.conv_general_dilated(x, w, (stride,), 'VALID', dimension_numbers=('NCH', 'OIH', 'NCH'))
            return y + b[None, :, None]

        def _cnorm(x, g, b):
            m = jnp.mean(x, axis=1, keepdims=True)
            v = jnp.var(x, axis=1, keepdims=True, ddof=1)
            return (x - m) * jax.lax.rsqrt(v + EPS) * g[None, :, None] + b[None, :, None]

        def _forward(x, conv0_w, conv0_b, conv1_w, conv1_b, conv2_w, conv2_b, conv3_w, conv3_b, n0_w, n0_b, n1_w, n1_b, n2_w, n2_b, n3_w, n3_b, n4_w, n4_b, mlp_w1, mlp_b1, mlp_w2, mlp_b2, mlp_w3, mlp_b3):
            h = jax.nn.relu(_cnorm(_conv(x, conv0_w, conv0_b, 5, 3), n0_w, n0_b))
            h = jax.nn.relu(_cnorm(_conv(h, conv1_w, conv1_b, 4, 2), n1_w, n1_b))
            h = jax.nn.relu(_cnorm(_conv(h, conv2_w, conv2_b, 2, 1), n2_w, n2_b))
            h = jax.nn.relu(_cnorm(_conv(h, conv3_w, conv3_b, 2, 1), n3_w, n3_b))
            f = jnp.transpose(h, (0, 2, 1))
            T = f.shape[1]
            z = jax.nn.gelu(f @ mlp_w1 + mlp_b1, approximate=False)
            z = jax.nn.gelu(z @ mlp_w2 + mlp_b2, approximate=False)
            imp = jax.nn.sigmoid((z @ mlp_w3 + mlp_b3)[..., 0]) + TEMP
            imp = imp / jnp.sum(imp, axis=1, keepdims=True) * (T / FACTOR)
            Tn = T // FACTOR
            cs = jnp.cumsum(imp, axis=1)
            p = jnp.maximum(cs[:, :, None] - jnp.arange(Tn, dtype=cs.dtype)[None, None, :], 0.0)
            pc = jnp.pad(p, ((0, 0), (0, 0), (0, 1)))
            d = pc[:, :, :-1] - pc[:, :, 1:]
            wmat = d - jnp.pad(d, ((0, 0), (1, 0), (0, 0)))[:, :-1, :]
            pooled = jnp.einsum('btn,btc->bnc', wmat, f)
            out = jnp.transpose(pooled, (0, 2, 1))
            return jax.nn.relu(_cnorm(out, n4_w, n4_b))
        return _forward(x, conv0_w, conv0_b, conv1_w, conv1_b, conv2_w, conv2_b, conv3_w, conv3_b, n0_w, n0_b, n1_w, n1_b, n2_w, n2_b, n3_w, n3_b, n4_w, n4_b, mlp_w1, mlp_b1, mlp_w2, mlp_b2, mlp_w3, mlp_b3)

    def _L0_attn_ref(x, W_qkv, b_qkv, W_out, b_out):
        import jax, jax.numpy as jnp
        import numpy as np
        D_K = 64
        SPARSITY = 0.5
        d_k = D_K
        qkv = x @ W_qkv + b_qkv
        q = qkv[..., :d_k]
        k = qkv[..., d_k:2 * d_k]
        v = qkv[..., 2 * d_k:]
        scores = jnp.einsum('bqd,bkd->bqk', q, k) / jnp.sqrt(jnp.float32(d_k))
        topk = int(SPARSITY * scores.shape[-1])
        thr = jax.lax.top_k(scores, topk)[0][..., -1:]
        sparse_mask = (scores >= thr).astype(scores.dtype)
        attn = jax.nn.softmax(scores * sparse_mask, axis=-1)
        out = jnp.einsum('bqk,bkd->bqd', attn, v)
        return out @ W_out + b_out

    def _L0_ffn_ref(x, route_id, Wi, bi, Wr, br, Ws, bs, Wo, bo):
        import jax, jax.numpy as jnp
        import numpy as np
        B, T, IN_DIM = (64, 64, 64)
        HID, OUT_DIM = (128, 64)
        N_LAYERS, N_EXPERTS, N_SHARED = (2, 16, 1)
        flat = x.reshape(-1, x.shape[-1])
        n_tok = flat.shape[0]
        route = jnp.repeat(route_id, n_tok // route_id.shape[0])
        h = jax.nn.relu(flat @ Wi.T + bi)
        n_layers, n_experts = (Wr.shape[0], Wr.shape[1])
        for l in range(n_layers):
            shared = (jnp.einsum('nd,shd->snh', h, Ws[l]) + bs[l][:, None, :]).mean(axis=0)
            routed = jnp.zeros_like(h)
            for e in range(n_experts):
                ye = h @ Wr[l, e].T + br[l, e]
                routed = routed + jnp.where((route == e)[:, None], ye, 0.0)
            h = jax.nn.relu(shared + routed + h)
        out = h @ Wo.T + bo
        return out.reshape(*x.shape[:-1], out.shape[-1])
    h = _L0_tok_ref(x, L0_tok_conv0_w, L0_tok_conv0_b, L0_tok_conv1_w, L0_tok_conv1_b, L0_tok_conv2_w, L0_tok_conv2_b, L0_tok_conv3_w, L0_tok_conv3_b, L0_tok_n0_w, L0_tok_n0_b, L0_tok_n1_w, L0_tok_n1_b, L0_tok_n2_w, L0_tok_n2_b, L0_tok_n3_w, L0_tok_n3_b, L0_tok_n4_w, L0_tok_n4_b, L0_tok_mlp_w1, L0_tok_mlp_b1, L0_tok_mlp_w2, L0_tok_mlp_b2, L0_tok_mlp_w3, L0_tok_mlp_b3)
    h = h + _L0_attn_ref(_layernorm(h, axis=-1), L0_attn_W_qkv, L0_attn_b_qkv, L0_attn_W_out, L0_attn_b_out)
    h = h + _L0_ffn_ref(_layernorm(h, axis=-1), L0_ffn_route_id, L0_ffn_Wi, L0_ffn_bi, L0_ffn_Wr, L0_ffn_br, L0_ffn_Ws, L0_ffn_bs, L0_ffn_Wo, L0_ffn_bo)
    return h

_drawn_inputs = setup_inputs


def setup_inputs(seed=0):
    import zlib

    import numpy as np

    out = dict(_drawn_inputs(seed))
    spreads = {'L0_tok_conv0_b': (0.0, 0.1),
     'L0_tok_conv1_b': (0.0, 0.1),
     'L0_tok_conv2_b': (0.0, 0.1),
     'L0_tok_conv3_b': (0.0, 0.1),
     'L0_tok_n0_w': (1.0, 0.2),
     'L0_tok_n0_b': (0.0, 0.1),
     'L0_tok_n1_w': (1.0, 0.2),
     'L0_tok_n1_b': (0.0, 0.1),
     'L0_tok_n2_w': (1.0, 0.2),
     'L0_tok_n2_b': (0.0, 0.1),
     'L0_tok_n3_w': (1.0, 0.2),
     'L0_tok_n3_b': (0.0, 0.1),
     'L0_tok_n4_w': (1.0, 0.2),
     'L0_tok_n4_b': (0.0, 0.1),
     'L0_tok_mlp_b1': (0.0, 0.48),
     'L0_tok_mlp_b2': (0.0, 0.355),
     'L0_attn_b_qkv': (0.0, 0.369),
     'L0_attn_b_out': (0.0, 0.1),
     'L0_ffn_bi': (0.0, 0.452),
     'L0_ffn_bo': (0.0, 0.1)}
    factors = {'L0_attn_W_qkv': 8.0,
     'L0_ffn_Wr': 5.976,
     'L0_ffn_br': 8.0,
     'L0_ffn_Ws': 6.049,
     'L0_ffn_bs': 8.0}
    for name, (base, spread) in spreads.items():
        noise = np.random.default_rng([zlib.crc32(name.encode()), seed]).standard_normal(out[name].shape)
        drawn = base * np.exp(spread * noise) if base else spread * noise
        out[name] = jnp.asarray(drawn.astype(out[name].dtype))
    for name, factor in factors.items():
        out[name] = (out[name] * factor).astype(out[name].dtype)
    return out
```

```python
from contextlib import ExitStack

import numpy as np

import concourse.bass as bass
from concourse import mybir

F32 = mybir.dt.float32
F32R = mybir.dt.float32r
I32 = mybir.dt.int32
ALU = mybir.AluOpType
ACT = mybir.ActivationFunctionType
AX = mybir.AxisListType.X

B, L = 32, 10240
C = 128
GB = 4
NG = B // GB
T0, T1, T2, T3 = 2048, 512, 256, 128
PH = 8
NW = T0 // PH
TAPS0, STRIDE0, PAD0 = 10, 5, 3
KX = TAPS0 * PH
KQ = KX + PH
K0 = KQ + 1
N = 2 * NW
W1P = T1 // 2 + 2
W2P = T2 + 2
DM = 512
MC = DM // C
TN = T3 // 2
D = 64
TOPK = T3 // 2
RG = 2
NR = GB * RG
TOK = 64
E = 16
EPS, TEMP = 1e-5, 1e-5
NEG = -3.0e38

IDENT, TRI, SHIFT, MEANS, ONES = 0, 128, 256, 384, 512
RAMP = 640
PHASE = RAMP + TN + 1
SAME = PHASE + PH
HALF = SAME + KQ
ROWNO = HALF + 32
NCONST = ROWNO + 1
CEN = TAPS0 + 4
GAIN, OFFS = CEN, CEN + 5
MB1, MB2, MW3 = CEN + 10, CEN + 14, CEN + 18
BS, BI, B3 = CEN + 22, CEN + 24, CEN + 25
NVEC = CEN + 26


def at(group, per, k):
    i, off = group
    c = off * per + k
    return c if i is None else i * per + c


def build(nc, a):
    with ExitStack() as ctx:
        def sb(name, shape, dt=F32):
            return ctx.enter_context(nc.sbuf_tensor(name, shape, dt))

        def ps(name):
            return ctx.enter_context(nc.psum_tensor(name, [128, 512], F32))

        def sem(name):
            return ctx.enter_context(nc.semaphore(name))

        cst = sb("cst", [128, NCONST])
        vec = sb("vec", [128, NVEC])
        cen = sb("cen", [128, CEN])
        neg3 = sb("neg3", [128, 1])
        ident = cst[:, IDENT:IDENT + 128]
        w0rep = sb("w0rep", [128, KQ])
        w0gain = sb("w0gain", [128, KQ])
        w0t = sb("w0t", [KQ, 128])
        gram = sb("gram", [KQ, KQ])
        w0h, w0l = sb("w0h", [K0, PH, 128], F32R), sb("w0l", [K0, PH, 128], F32R)
        wc_mean = sb("wc_mean", [128, 16])
        wch, wcl = sb("wch", [128, 16, 128], F32R), sb("wcl", [128, 16, 128], F32R)
        m1h, m1l = sb("m1h", [128, DM], F32R), sb("m1l", [128, DM], F32R)
        m2h, m2l = sb("m2h", [128, MC, DM], F32R), sb("m2l", [128, MC, DM], F32R)
        wqkv = sb("wqkv", [D + 1, 3 * D])
        wout = sb("wout", [D, D])
        bout = sb("bout", [128, D])
        wi = sb("wi", [D, 128])
        ws = sb("ws", [128, 2, 128])
        brt = sb("brt", [E, 2, 128])
        wo = sb("wo", [128, D])
        bo = sb("bo", [128, D])
        route_i = sb("route_i", [E, B * RG], I32)
        route_f = sb("route_f", [E, B * RG])
        route_c = sb("route_c", [1, B * RG])
        route_in = sb("route_in", [1, B * RG])
        pick = sb("pick", [1, B * RG], I32)
        onehot = sb("onehot", [E, B * RG])

        xt = [sb(f"xt{k}", [KQ, N]) for k in range(2)]
        quad = sb("quad", [KQ, N])
        eps0, rstd0 = sb("eps0", [128, 32]), sb("rstd0", [128, 32])
        rst0w = sb("rst0w", [128, 4, KQ])
        xs = sb("xs", [K0, N])
        xh, xl = sb("xh", [K0, N], F32R), sb("xl", [K0, N], F32R)
        h0 = sb("h0", [128, 2, PH, 2, NW + 2], F32R)
        h1 = sb("h1", [128, 2, 2, 2, W1P], F32R)
        h2 = sb("h2", [128, 2, GB, W2P], F32R)
        KINDS = (1, 2, 3, 4)
        WIDE = {1: 512, 2: 512, 3: 512, 4: GB * TN}
        y = {n: [sb(f"y{n}_{r}", [128, WIDE[n]]) for r in range(2 if n == 1 else 1)] for n in KINDS}
        sq = {n: [sb(f"sq{n}_{r}", [128, WIDE[n]]) for r in range(2 if n == 1 else 1)] for n in KINDS}
        vare = {n: sb(f"vare{n}", [128, 4]) for n in KINDS}
        rstd = {n: sb(f"rstd{n}", [128, 4]) for n in KINDS}
        f = y[3][0]
        fh, fl = sb("fh", [128, 512], F32R), sb("fl", [128, 512], F32R)
        fsum = sb("fsum", [128, GB])
        fmean = sb("fmean", [128, GB])
        ftc = sb("ftc", [128, GB, 128])
        g1 = [sb(f"g1_{m}", [128, 512]) for m in range(2)]
        g1h, g1l = sb("g1h", [128, MC, 512], F32R), sb("g1l", [128, MC, 512], F32R)
        g2 = sb("g2", [128, MC, 512])
        sig = sb("sig", [128, 3, GB])
        imp = sb("imp", [128, GB])
        rtot = sb("rtot", [128, GB])
        impn = sb("impn", [128, GB])
        cums = sb("cums", [128, GB])
        over = sb("over", [128, GB, TN + 1])
        diff = sb("diff", [128, GB, TN])
        wmat = sb("wmat", [128, GB, TN])
        h = y[4][0]
        bn = sb("bn", [128, GB, 6])
        mv = sb("mv", [128, GB, 2])
        lv = sb("lv", [128, GB])
        lr = sb("lr", [128, GB])
        lx = sb("lx", [128, GB, D])
        lxt = sb("lxt", [D + 1, 512])
        hb = sb("hb", [128, GB, D])
        qT, kT = sb("qT", [D, 512]), sb("kT", [D, 512])
        v = sb("v", [128, GB, D])
        s = sb("s", [128, GB, 128])
        swork = sb("swork", [128, GB, 128])
        top = sb("top", [128, GB, 8])
        smax = sb("smax", [128, GB])
        nmax = sb("nmax", [128, GB])
        e = swork
        den = sb("den", [128, GB])
        rden = sb("rden", [128, GB])
        eT, oT = s, qT
        ha = sb("ha", [128, GB, D])
        hc = sb("hc", [128, GB, D])
        l2x = sb("l2x", [128, GB, D])
        l2t = lxt[0:D, :]
        ub = sb("ub", [128, 3, 512])
        u = [ub[:, n, :] for n in range(3)]
        wr = sb("wr", [128, NR, 2, 128])
        res = sb("res", [128, GB, D])
        w0 = ub[0:K0, 0:2, :].rearrange("p a (j c) -> p (a j) c", c=128)
        wc_raw = g2[:, :, :].rearrange("p m (t c) -> p (m t) c", c=128)
        m1raw = y[1][0]
        m2raw = wr[:, :, :, :].rearrange("p (k n) l c -> p k (n l c)", k=MC)

        pF, pC, pS = ps("pF"), [ps("pC0"), ps("pC1")], ps("pS")
        pM = [ps("pM0"), ps("pM1")]
        pT = [ps("pT0"), ps("pT1")]
        var_bank = {1: pC, 2: [pC[1]], 3: [pM[0]], 4: [pT[1]]}

        s_const, s_setup, s_row = sem("const_loaded"), sem("setup_pe"), sem("ones_rows_set")
        s_w0row, s_mlpw = sem("w0_row_loaded"), sem("mlp_weights_loaded")
        s_dset, s_ready = sem("setup_dve"), sem("setup_done")
        s_x = [sem(f"x_loaded{k}") for k in range(2)]
        s_quad, s_quadx, s_var0, s_eps0 = sem("quad"), sem("quad_times_x"), sem("var0"), sem("eps0")
        s_rstd0, s_rst0w, s_rb0 = sem("rstd0"), sem("rstd0_spread"), sem("rstd0_on_rows")
        s_xs, s_xh, s_xl = sem("x_scaled"), sem("x_high"), sem("x_low")
        s_c0, s_h0h, s_h0l, s_pad0 = sem("conv0"), sem("h0_high"), sem("h0_low"), sem("h0_pads")
        s_c1, s_c2, s_c3 = sem("conv1"), sem("conv2"), sem("conv3")
        s_conv = {1: s_c1, 2: s_c2, 3: s_c3}
        s_pad1, s_pad2 = sem("h1_pads"), sem("h2_pads")
        ns = {n: {x: sem(f"n{n}_{x}") for x in ("y", "sq", "var", "eps", "rstd", "rb", "z", "act", "hi", "lo")}
              for n in KINDS}
        PER = {1: 4, 2: 2, 3: 1, 4: 1}
        s_ft, s_fsum, s_fmean, s_ftc = sem("fT"), sem("f_sum"), sem("f_mean"), sem("fT_centred")
        s_m1, s_g1, s_g1h, s_g1l = sem("mlp1"), sem("gelu1"), sem("gelu1_high"), sem("gelu1_low")
        s_m2, s_g2, s_m3, s_exp3, s_sig = sem("mlp2"), sem("gelu2"), sem("mlp3"), sem("exp3"), sem("sigmoid")
        s_tot, s_impn, s_cum, s_over, s_wm = sem("total"), sem("imp_normed"), sem("cumsum"), sem("over"), sem("wmat_product")
        s_wmat, s_pool, s_hb = sem("wmat"), sem("pooled"), sem("h_plus_bout")
        s_ln, s_lr, s_lx, s_lxp, s_lxt = (sem(x) for x in ("ln_stats", "ln_rstd", "ln_x", "ln_xT_product", "ln_xT"))
        s_qkvp, s_qk, s_v, s_sp, s_s = (sem(x) for x in ("qkv_product", "qk", "v", "score_product", "scores"))
        s_top, s_sm, s_e, s_etp, s_et = (sem(x) for x in ("topk", "masked", "exp", "expT_product", "expT"))
        s_op, s_oT, s_wop, s_ha = (sem(x) for x in ("attn_product", "attnT", "attn_out_product", "attn_added"))
        s_hc = sem("ha_plus_bo")
        s_fp, s_u, s_res, s_out, s_wr = (sem(x) for x in ("ffn_product", "ffn_relu", "result", "stored", "experts_loaded"))

        s_chain = {x: sem(f"chain_{x}") for x in ("sigmoid", "total", "over", "ln1", "ln2", "mask", "den")}

        LOADS = [(cst[:, :], a["consts"]), (vec[:, :], a["vecs"]), (wc_raw[:, :, :], a["wconv"]),
                 (wqkv[:, :], a["wqkv"]), (wout[:, :], a["wout"]), (bout[:, :], a["bout"]),
                 (wi[:, :], a["wi"]), (ws[:, :, :], a["ws"]), (brt[:, :, :], a["brt"]), (wo[:, :], a["wo"]),
                 (bo[:, :], a["bo"]), (route_i[:, :], a["route"])]
        LOADED = 16 * len(LOADS)
        block = ctx.enter_context(nc.Block())

        def wait_apart(engine, semaphore, value):
            if not isinstance(value, int):
                value = engine.to_reg(value)
            engine.wait_ge(s_ready, 2)
            engine.wait_ge(semaphore, value)

        PRE, FIRST = (None, 0), (None, 1)
        LOOPS = NG - 2

        def nxt(group):
            return group[0], group[1] + 1

        @block.sync
        def _(sp):
            for dst, src in LOADS:
                sp.dma_start(dst, src).then_inc(s_const, 16)
            sp.dma_start(m1raw[:, :], a["m1"]).then_inc(s_mlpw, 16)
            sp.dma_start(m2raw[:, :, :], a["m2"]).then_inc(s_mlpw, 16)
            sp.wait_ge(s_ready, 1)
            for j in range(PH):
                sp.dma_start(w0[KQ:K0, j, :], a["off0"]).then_inc(s_w0row, 16)
            sp.wait_ge(s_row, 2)

            def load_x(group, k, first=False):
                i, off = group
                if not first:
                    sp.wait_ge(s_xs, at(group, 2, k + 1 - 2))
                n = off * 2 + k if i is None else i * 2 + (off * 2 + k)
                src = a["x"][n, :, :] if i is None else a["x"][bass.ds(n, 1), :, :].rearrange("a r n -> (a r) n")
                sp.dma_start(xt[k][0:KX, :], src).then_inc(s_x[k], 16)

            def load_experts(group):
                i, off = group
                for n in range(NR):
                    c = off * NR + n if i is None else i * NR + (off * NR + n)
                    src = pick[0:1, c:c + 1] if i is None else pick[0:1, bass.ds(c, 1)]
                    x = sp.value_load(src, min_val=0, max_val=E)
                    sp.dma_start(wr[:, n, :, :], a["wr"][bass.ds(x, 1), :, :, :].rearrange("e p l o -> (e p) l o"))\
                      .then_inc(s_wr, 16)

            def store(group):
                i, off = group
                sp.wait_ge(s_res, at(group, 1, 1))
                src = res[:, :, :]
                n = off * GB if i is None else i * GB + off * GB
                o = a["out"][bass.ds(n, GB), :, :] if i is not None else a["out"][n:n + GB, :, :]
                sp.dma_start(o.rearrange("b c n -> c b n"), src).then_inc(s_out, 16)
                sp.wait_ge(s_out, at(group, 16, 16))

            load_x(PRE, 0, True)
            load_x(PRE, 1, True)
            load_x(FIRST, 0)
            load_x(FIRST, 1)

            def body(gf, gb, gc):
                if gf:
                    load_x(nxt(gf), 0)
                    load_x(nxt(gf), 1)
                if gc:
                    store(gc)
                if gb:
                    load_experts(gb)
            load_x((None, 2), 0)
            load_x((None, 2), 1)
            load_experts(PRE)
            with sp.Fori(0, LOOPS) as i:
                body((i, 2), (i, 1), (i, 0))
            body(None, (None, NG - 1), (None, NG - 2))
            body(None, None, (None, NG - 1))
            sp.wait_ge(s_x[1], 16 * (NG + 1))
            sp.wait_ge(s_out, 16 * NG)

        @block.tensor
        def _(pe):
            def mm(out, lhs, rhs, start=True, stop=True):
                return nc.tensor.matmul(out, lhs, rhs, start=start, stop=stop)

            pe.wait_ge(s_const, LOADED)
            mm(pS[:, 0:CEN], cst[:, MEANS:MEANS + 128], vec[:, 0:CEN]).then_inc(s_setup, 1)
            pe.wait_ge(s_dset, 2)
            mm(pF[0:KQ, 0:KQ], w0rep[:, :], w0rep[:, :]).then_inc(s_setup, 1)
            pe.wait_ge(s_dset, 3)
            nc.tensor.transpose(pC[0][0:KQ, 0:128], w0gain[:, :], ident).then_inc(s_setup, 1)

            def quad_form(group, k):
                pe.wait_ge(s_x[k], at(group, 16, 16))
                mm(pF[0:KQ, :], gram[:, :], xt[k][:, :]).then_inc(s_quad, 1)

            def var0(group, k):
                pe.wait_ge(s_quadx, at(group, 2, k + 1))
                for b in range(4):
                    m = mm(pS[:, PH * b:PH * b + PH], quad[:, 128 * b:128 * b + 128],
                           cst[0:KQ, PHASE:PHASE + PH])
                m.then_inc(s_var0, 1)

            def spread0(group, k, first=False):
                pe.wait_ge(s_rst0w, at(group, 2, k + 1))
                if not first:
                    pe.wait_ge(ns[2]["z"], z2_before[0])
                for b in range(4):
                    m = mm(pF[0:KQ, 128 * b:128 * b + 128], rst0w[:, b, :], ident)
                m.then_inc(s_rb0, 1)

            z2_before = [None]

            def split3(out, wh, wl, xhi, xlo, first=True, last=True):
                mm(out, wh, xhi, first, False)
                mm(out, wh, xlo, False, False)
                return mm(out, wl, xhi, False, last)

            def conv0(group, k, js, first=False):
                if js[0] == 0:
                    pe.wait_ge(s_xh, at(group, 2, k + 1))
                    pe.wait_ge(s_xl, at(group, 2, k + 1))
                    if not first:
                        pe.wait_ge(ns[1]["sq"], at(group, 4, 2 * k))
                for j in js:
                    if j >= 2:
                        pe.wait_ge(s_h0l, at(group, 2 * PH, PH * k + j - 1))
                    split3(pC[j % 2][:, :], w0h[:, j, :], w0l[:, j, :], xh[:, :], xl[:, :]).then_inc(s_c0, 1)

            def conv1(group, k, r):
                if r == 0:
                    pe.wait_ge(s_h0l, at(group, 2 * PH, PH * k + PH))
                    pe.wait_ge(s_h0h, at(group, 2 * PH, PH * k + PH))
                    pe.wait_ge(s_pad0, at(group, 2, k + 1))
                elif n2_before[0] is not None:
                    pe.wait_ge(ns[2]["eps"], n2_before[0])
                for t in range(8):
                    p = 4 * r - 2 + t
                    o = 1 + p // PH
                    m = split3(pC[r][:, :], wch[:, t, :], wcl[:, t, :], h0[:, 0, p % PH, :, o:o + NW],
                               h0[:, 1, p % PH, :, o:o + NW], t == 0, t == 7)
                m.then_inc(s_c1, 1)

            n2_before = [None]

            def conv2(group, k):
                pe.wait_ge(ns[1]["lo"], at(group, 4, 2 * k + 2))
                pe.wait_ge(s_pad1, at(group, 2, k + 1))
                if h0l_before[0] is not None:
                    pe.wait_ge(s_h0l, h0l_before[0])
                for t in range(4):
                    r, o = (t + 1) % 2, (0 if t == 0 else 2 if t == 3 else 1)
                    m = split3(pC[1][:, :], wch[:, 8 + t, :], wcl[:, 8 + t, :], h1[:, 0, r, :, o:o + T2],
                               h1[:, 1, r, :, o:o + T2], t == 0, t == 3)
                m.then_inc(s_c2, 1)

            h0l_before = [None]

            def var(n, group, idx, buf=0, blocks=4):
                pe.wait_ge(ns[n]["sq"], at(group, PER[n], idx))
                for b in range(blocks):
                    m = mm(var_bank[n][buf][:, b:b + 1], sq[n][buf][:, 128 * b:128 * b + 128], cst[:, ONES:ONES + 1])
                m.then_inc(ns[n]["var"], 1)

            def spread(n, group, idx, bank, blocks=4):
                pe.wait_ge(ns[n]["rstd"], at(group, PER[n], idx))
                for b in range(blocks):
                    m = mm(bank[:, 128 * b:128 * b + 128], rstd[n][:, b:b + 1].to_broadcast([128, 128]), ident)
                m.then_inc(ns[n]["rb"], 1)

            def conv3(group):
                pe.wait_ge(ns[2]["lo"], at(group, 2, 2))
                pe.wait_ge(s_pad2, at(group, 2, 2))
                if group is not PRE:
                    pe.wait_ge(s_exp3, at(group, 1, 0))
                for t in range(4):
                    m = split3(pM[0][:, :], wch[:, 12 + t, :], wcl[:, 12 + t, :], h2[:, 0, :, t:t + 2 * T3 - 1:2],
                               h2[:, 1, :, t:t + 2 * T3 - 1:2], t == 0, t == 3)
                m.then_inc(s_c3, 1)

            def f_transposes(group):
                pe.wait_ge(ns[3]["act"], at(group, 1, 1))
                for b in range(GB):
                    m = nc.tensor.transpose(pM[1][:, 128 * b:128 * b + 128], f[:, 128 * b:128 * b + 128], ident)
                m.then_inc(s_ft, 1)

            def mlp1(group, ms):
                pe.wait_ge(ns[3]["lo"], at(group, 1, 1))
                for m_ in ms:
                    if m_ == 1:
                        pe.wait_ge(s_ftc, at(group, 1, 1))
                    if m_ >= 2:
                        pe.wait_ge(s_g1, at(group, MC, m_ - 1))
                    w = slice(128 * m_, 128 * m_ + 128)
                    split3(pM[m_ % 2][:, :], m1h[:, w], m1l[:, w], fh[:, :], fl[:, :]).then_inc(s_m1, 1)

            def mlp2(group, ms):
                if ms[0] == 0:
                    pe.wait_ge(s_g1l, at(group, MC, MC))
                for m_ in ms:
                    if m_ >= 2:
                        pe.wait_ge(s_g2, at(group, MC, m_ - 1))
                    w = slice(128 * m_, 128 * m_ + 128)
                    for kc in range(MC):
                        m = split3(pM[m_ % 2][:, :], m2h[:, kc, w], m2l[:, kc, w], g1h[:, kc, :], g1l[:, kc, :],
                                   kc == 0, kc == MC - 1)
                    m.then_inc(s_m2, 1)

            def mlp3(group):
                pe.wait_ge(s_g2, at(group, MC, MC))
                for b in range(GB):
                    for kc in range(MC):
                        m = mm(pM[0][:, b:b + 1], g2[:, kc, 128 * b:128 * b + 128],
                               vec[:, MW3 + kc:MW3 + kc + 1], kc == 0, kc == MC - 1)
                m.then_inc(s_m3, 1)

            def total(group):
                pe.wait_ge(s_sig, at(group, 1, 1))
                mm(pT[0][:, 0:GB], cst[:, ONES:ONES + 128], imp[:, :]).then_inc(s_tot, 1)

            def cumsum(group):
                pe.wait_ge(s_impn, at(group, 1, 1))
                mm(pT[0][:, 0:GB], cst[:, TRI:TRI + 128], impn[:, :]).then_inc(s_cum, 1)

            def shares(group):
                pe.wait_ge(s_over, at(group, 1, 1))
                mm(pT[0][:, 0:GB * TN], cst[:, SHIFT:SHIFT + 128], diff[:, :, :]).then_inc(s_wm, 1)

            def pool(group):
                pe.wait_ge(s_wmat, at(group, 1, 1))
                for b in range(GB):
                    m = mm(pT[1][:, TN * b:TN * b + TN], ftc[:, b, :], wmat[:, b, :])
                m.then_inc(s_pool, 1)

            def x_transposes(group):
                wait_apart(pe, s_lx, at(group, 2, 1))
                for b in range(GB):
                    m = nc.tensor.transpose(pT[1][0:D, 128 * b:128 * b + 128], lx[:, b, :], ident)
                m.then_inc(s_lxp, 1)

            def qkv(group):
                pe.wait_ge(s_lxt, at(group, 2, 1))
                mm(pT[0][0:D, :], wqkv[:, 0:D], lxt[:, :]).then_inc(s_qkvp, 1)
                mm(pT[1][0:D, :], wqkv[:, D:2 * D], lxt[:, :]).then_inc(s_qkvp, 1)
                pe.wait_ge(s_qk, at(group, 2, 1))
                for b in range(GB):
                    m = mm(pT[0][:, D * b:D * b + D], lxt[:, 128 * b:128 * b + 128], wqkv[:, 2 * D:3 * D])
                m.then_inc(s_qkvp, 1)

            def scores(group):
                pe.wait_ge(s_qk, at(group, 2, 2))
                for b in range(GB):
                    w = slice(128 * b, 128 * b + 128)
                    m = mm(pT[1][:, w], qT[:, w], kT[:, w])
                m.then_inc(s_sp, 1)

            def e_transposes(group):
                pe.wait_ge(s_e, at(group, 1, 1))
                pe.wait_ge(s_v, at(group, 1, 1))
                for b in range(GB):
                    m = nc.tensor.transpose(pT[0][:, 128 * b:128 * b + 128], e[:, b, :], ident)
                m.then_inc(s_etp, 1)

            def attend(group):
                pe.wait_ge(s_et, at(group, 1, 1))
                for b in range(GB):
                    m = mm(pT[1][0:D, 128 * b:128 * b + 128], v[:, b, :], eT[:, b, :])
                m.then_inc(s_op, 1)

            def attn_out(group):
                pe.wait_ge(s_oT, at(group, 1, 1))
                for b in range(GB):
                    m = mm(pT[0][:, D * b:D * b + D], oT[:, 128 * b:128 * b + 128], wout[:, :])
                m.then_inc(s_wop, 1)

            def x2_transposes(group):
                wait_apart(pe, s_lx, at(group, 2, 2))
                for b in range(GB):
                    m = nc.tensor.transpose(pT[1][0:D, 128 * b:128 * b + 128], l2x[:, b, :], ident)
                m.then_inc(s_lxp, 1)

            def ffn_in(group):
                pe.wait_ge(s_lxt, at(group, 2, 2))
                mm(pT[0][:, :], wi[:, :], l2t[:, :]).then_inc(s_fp, 1)

            def ffn_layer(group, l):
                i, off = group
                pe.wait_ge(s_u, at(group, 3, l + 1))
                if l == 0:
                    pe.wait_ge(s_wr, at(group, 16 * NR, 16 * NR))
                p = pT[1 - l]
                mm(p[:, :], ws[:, l, :], u[l][:, :], True, False)
                hot = onehot[:, off * NR:off * NR + NR] if i is None else onehot[:, bass.ds(i * NR + off * NR, NR)]
                for n in range(NR):
                    w = slice(TOK * n, TOK * n + TOK)
                    nc.tensor.matmul(p[:, w], wr[:, n, l, :], u[l][:, w], start=False, stop=False,
                                     skip_group_check=True)
                nc.tensor.matmul(p[:, :], brt[:, l, :], hot.unsqueeze(2).to_broadcast([E, NR, TOK]),
                                 start=False, stop=True).then_inc(s_fp, 1)

            def ffn_out(group):
                pe.wait_ge(s_u, at(group, 3, 3))
                for b in range(GB):
                    m = mm(pT[1][:, D * b:D * b + D], u[2][:, 128 * b:128 * b + 128], wo[:, :])
                m.then_inc(s_fp, 1)

            def body(gf, gb, gc):
                ng = gf and nxt(gf)
                n2_before[0] = gb and at(gb, 2, 2)
                h0l_before[0] = gf and at(gf, 2 * PH, PH)
                z2_before[0] = gb and at(gb, 2, 2)
                if gc: total(gc)
                if gf: conv0(gf, 0, range(0, 4), gf is PRE)
                if gc: cumsum(gc)
                if gf: conv0(gf, 0, range(4, 8))
                if gc: shares(gc)
                if gb: conv2(gb, 1)
                if gc: pool(gc)
                if gf: conv1(gf, 0, 0)
                if gb: var(2, gb, 2)
                if gc: var(4, gc, 1, blocks=2)
                if gf: quad_form(gf, 1)
                if gf: conv1(gf, 0, 1)
                if gb:
                    if gf: pe.wait_ge(s_quadx, at(gf, 2, 2))
                    spread(2, gb, 2, pF)
                if gc: spread(4, gc, 1, pT[0], 2)
                if gf: var0(gf, 1)
                if gf: var(1, gf, 1, 0)
                if gf: var(1, gf, 2, 1)
                if gf:
                    spread0(gf, 1, gf is PRE)
                    pe.wait_ge(s_xs, at(gf, 2, 2))
                    spread(1, gf, 1, pF)
                if gc: x_transposes(gc)
                if gb: conv3(gb)
                if gf:
                    pe.wait_ge(ns[1]["z"], at(gf, 4, 1))
                    spread(1, gf, 2, pF)
                if gc: qkv(gc)
                if gf: conv0(gf, 1, range(0, 4))
                if gb: var(3, gb, 1)
                if gc: scores(gc)
                if gf: conv0(gf, 1, range(4, 8))
                if gb: spread(3, gb, 1, pM[1])
                h0l_before[0] = gf and at(gf, 2 * PH, 2 * PH)
                n2_before[0] = gf and at(gf, 2, 1)
                if gf: conv2(gf, 0)
                if gf: conv1(gf, 1, 0)
                if gb: f_transposes(gb)
                if gb: mlp1(gb, range(MC))
                if gf: var(2, gf, 1)
                if gf: quad_form(ng, 0)
                if gc: e_transposes(gc)
                if gb: mlp2(gb, range(0, 2))
                if gc: attend(gc)
                if gf:
                    pe.wait_ge(s_quadx, at(ng, 2, 1))
                    spread(2, gf, 1, pF)
                    var0(ng, 0)
                if gb: mlp2(gb, range(2, 4))
                if gc: attn_out(gc)
                if gf: conv1(gf, 1, 1)
                if gc: x2_transposes(gc)
                if gb: mlp3(gb)
                if gf:
                    z2_before[0] = at(gf, 2, 1)
                    var(1, gf, 3, 0)
                    var(1, gf, 4, 1)
                if gc: ffn_in(gc)
                if gf:
                    spread0(ng, 0)
                    pe.wait_ge(s_xs, at(ng, 2, 1))
                    spread(1, gf, 3, pF)
                if gc: ffn_layer(gc, 0)
                if gf:
                    pe.wait_ge(ns[1]["z"], at(gf, 4, 3))
                    spread(1, gf, 4, pF)
                if gc: ffn_layer(gc, 1)
                if gc: ffn_out(gc)

            pe.wait_ge(s_ready, 2)
            quad_form(PRE, 0)
            var0(PRE, 0)
            spread0(PRE, 0, True)
            body(PRE, None, None)
            body(FIRST, PRE, None)
            with pe.Fori(0, LOOPS) as i:
                body((i, 2), (i, 1), (i, 0))
            body(None, (None, NG - 1), (None, NG - 2))
            body(None, None, (None, NG - 1))

        @block.scalar
        def _(sc):
            def do(out, in_, func, **k):
                return nc.scalar.activation(out, in_, func, **k)

            def x_high(group, k):
                sc.wait_ge(s_xs, at(group, 2, k + 1))
                do(xh[0:KQ, :], xs[0:KQ, :], ACT.Copy).then_inc(s_xh, 1)

            def relu0(group, k, js):
                for j in js:
                    sc.wait_ge(s_c0, at(group, 2 * PH, PH * k + j + 1))
                    do(h0[:, 0, j, :, 1:1 + NW], pC[j % 2][:, :].rearrange("p (b w) -> p b w", b=2), ACT.Relu)\
                        .then_inc(s_h0h, 1)

            def squares(n, group, idx, src, buf=0, cols=512):
                sc.wait_ge(s_pool if n == 4 else s_conv[n], at(group, PER[n], idx))
                nb = len(y[n])
                if n < 3 and not (group[0] is None and group[1] * PER[n] + idx <= nb):
                    sc.wait_ge(ns[n]["lo"], at(group, PER[n], idx - nb))
                bias = {} if n == 4 else {"bias": cen[:, TAPS0 + n:TAPS0 + n + 1]}
                do(y[n][buf][:, 0:cols], src, ACT.Identity, **bias).then_inc(ns[n]["y"], 1)
                do(sq[n][buf][:, 0:cols], src, ACT.Square, **bias).then_inc(ns[n]["sq"], 1)

            def relu(n, group, idx, cols=512):
                sc.wait_ge(ns[n]["z"], at(group, PER[n], idx))
                x = y[n][(idx - 1) % len(y[n])][:, 0:cols]
                do(x, x, ACT.Relu, bias=vec[:, OFFS + n:OFFS + n + 1],
                   scale=vec[:, GAIN + n:GAIN + n + 1]).then_inc(ns[n]["act"], 1)

            def gelu1(group, ms):
                for m in ms:
                    sc.wait_ge(s_m1, at(group, MC, m + 1))
                    if m >= 2:
                        sc.wait_ge(s_g1l, at(group, MC, m - 1))
                    do(g1[m % 2][:, :], pM[m % 2][:, :], ACT.Gelu, bias=vec[:, MB1 + m:MB1 + m + 1]).then_inc(s_g1, 1)

            def gelu2(group, ms):
                for m in ms:
                    sc.wait_ge(s_m2, at(group, MC, m + 1))
                    do(g2[:, m, :], pM[m % 2][:, :], ACT.Gelu, bias=vec[:, MB2 + m:MB2 + m + 1]).then_inc(s_g2, 1)

            def exp3(group):
                sc.wait_ge(s_m3, at(group, 1, 1))
                do(sig[:, 0, :], pM[0][:, 0:GB], ACT.Exp, bias=neg3[:, :], scale=-1.0).then_inc(s_exp3, 1)

            def x_rows(group, second):
                sc.wait_ge(s_lxp, at(group, 2, 1 + second))
                do((l2t if second else lxt)[0:D, :], pT[1][0:D, :], ACT.Copy).then_inc(s_lxt, 1)

            def qk(group):
                sc.wait_ge(s_qkvp, at(group, 3, 1))
                do(qT[:, :], pT[0][0:D, :], ACT.Copy).then_inc(s_qk, 1)
                sc.wait_ge(s_qkvp, at(group, 3, 2))
                do(kT[:, :], pT[1][0:D, :], ACT.Copy).then_inc(s_qk, 1)
                sc.wait_ge(s_qkvp, at(group, 3, 3))
                do(v[:, :, :], pT[0][:, 0:GB * D].rearrange("p (b d) -> p b d", b=GB), ACT.Copy).then_inc(s_v, 1)

            def copy_scores(group):
                sc.wait_ge(s_sp, at(group, 1, 1))
                do(s[:, :, :], pT[1][:, :].rearrange("p (b d) -> p b d", b=GB), ACT.Copy, scale=float(D) ** -0.5)\
                    .then_inc(s_s, 1)

            def exps(group):
                sc.wait_ge(s_sm, at(group, 1, 1))
                for b in range(GB):
                    x = do(e[:, b, :], s[:, b, :], ACT.Exp, bias=nmax[:, b:b + 1], accum_out=den[:, b:b + 1])
                x.then_inc(s_e, 1)

            def e_rows(group):
                sc.wait_ge(s_etp, at(group, 1, 1))
                do(eT[:, :, :], pT[0][:, :].rearrange("p (b d) -> p b d", b=GB), ACT.Copy).then_inc(s_et, 1)

            def o_rows(group):
                sc.wait_ge(s_op, at(group, 1, 1))
                do(oT[:, :], pT[1][0:D, :], ACT.Copy).then_inc(s_oT, 1)

            def ffn_relu(group, l):
                sc.wait_ge(s_fp, at(group, 4, l + 1))
                b = vec[:, BI:BI + 1] if l == 0 else vec[:, BS + l - 1:BS + l]
                do(u[l][:, :], pT[l % 2][:, :], ACT.Relu, bias=b).then_inc(s_u, 1)

            def body(gf, gb, gc):
                ng = gf and nxt(gf)
                if gf: relu0(gf, 0, range(0, 4))
                if gf: relu0(gf, 0, range(4, 8))
                if gb: squares(2, gb, 2, pC[1][:, :])
                if gc: squares(4, gc, 1, pT[1][:, 0:GB * TN], cols=GB * TN)
                if gf: squares(1, gf, 1, pC[0][:, :], 0)
                if gf: squares(1, gf, 2, pC[1][:, :], 1)
                if gb: relu(2, gb, 2)
                if gc: relu(4, gc, 1, GB * TN)
                if gf: x_high(gf, 1)
                if gf: relu(1, gf, 1)
                if gc: x_rows(gc, 0)
                if gb: squares(3, gb, 1, pM[0][:, :])
                if gf: relu(1, gf, 2)
                if gc: qk(gc)
                if gf: relu0(gf, 1, range(0, 4))
                if gc: copy_scores(gc)
                if gf: relu0(gf, 1, range(4, 8))
                if gb: relu(3, gb, 1)
                if gf: squares(2, gf, 1, pC[1][:, :])
                if gf: squares(1, gf, 3, pC[0][:, :], 0)
                if gb: gelu1(gb, range(MC))
                if gc: exps(gc)
                if gc: e_rows(gc)
                if gb: gelu2(gb, range(0, 2))
                if gc: o_rows(gc)
                if gf: relu(2, gf, 1)
                if gb: gelu2(gb, range(2, 4))
                if gf: squares(1, gf, 4, pC[1][:, :], 1)
                if gc: x_rows(gc, 1)
                if gb: exp3(gb)
                if gc: ffn_relu(gc, 0)
                if gf: x_high(ng, 0)
                if gf: relu(1, gf, 3)
                if gc: ffn_relu(gc, 1)
                if gf: relu(1, gf, 4)
                if gc: ffn_relu(gc, 2)

            sc.wait_ge(s_ready, 2)
            x_high(PRE, 0)
            body(PRE, None, None)
            body(FIRST, PRE, None)
            with sc.Fori(0, LOOPS) as i:
                body((i, 2), (i, 1), (i, 0))
            body(None, (None, NG - 1), (None, NG - 2))
            body(None, None, (None, NG - 1))

        @block.vector
        def _(ve):
            V = nc.vector
            count = [0]

            def step(ins):
                count[0] += 1
                ins.then_inc(s_dset, 1)
                ve.wait_ge(s_dset, count[0])

            ve.wait_ge(s_setup, 1)
            step(V.tensor_tensor(cen[:, :], vec[:, 0:CEN], pS[:, 0:CEN], ALU.subtract))
            step(V.tensor_copy(w0rep[:, :].rearrange("p (t j) -> p t j", j=PH),
                               cen[:, 0:TAPS0 + 1].unsqueeze(2).to_broadcast([128, TAPS0 + 1, PH])))
            step(V.tensor_scalar(w0gain[:, :], w0rep[:, :], vec[:, GAIN:GAIN + 1], None, ALU.mult))
            ve.wait_ge(s_setup, 2)
            step(V.tensor_tensor(gram[:, :], pF[0:KQ, 0:KQ], cst[0:KQ, SAME:SAME + KQ], ALU.mult))
            ve.wait_ge(s_setup, 3)
            step(V.tensor_copy(w0t[:, :], pC[0][0:KQ, 0:128]))
            for j in range(PH):
                ins = V.tensor_scalar(w0[0:KQ, j, :], w0t[:, :], cst[0:KQ, PHASE + j:PHASE + j + 1], None, ALU.mult)
            ins.then_inc(s_ready, 1)
            V.memset(xt[0][64:KQ, :], 1.0).then_inc(s_row, 1)
            V.memset(xt[1][64:KQ, :], 1.0).then_inc(s_row, 1)
            step(V.memset(xs[:, :], 1.0))
            step(V.tensor_copy(xh[:, :], xs[:, :]))
            step(V.memset(xs[:, :], 0.0))
            step(V.tensor_copy(xl[:, :], xs[:, :]))
            step(V.memset(lxt[D:D + 1, :], 1.0))
            step(V.tensor_scalar(neg3[:, :], vec[:, B3:B3 + 1], -1.0, None, ALU.mult))
            step(V.tensor_copy(route_f[:, :], route_i[:, :]))
            step(V.tensor_scalar(onehot[:, :], route_f[:, :], cst[0:E, ROWNO:ROWNO + 1], None, ALU.is_equal))
            step(V.tensor_scalar(route_in[:, :], route_f[0:1, :], 0.0, None, ALU.is_ge))
            step(V.tensor_scalar(route_c[:, :], route_f[0:1, :], float(E), None, ALU.is_lt))
            step(V.tensor_tensor(route_in[:, :], route_in[:, :], route_c[:, :], ALU.mult))
            step(V.tensor_scalar(route_c[:, :], route_f[0:1, :], 0.0, float(E), ALU.max, ALU.min))
            step(V.tensor_scalar(route_c[:, :], route_c[:, :], -float(E), None, ALU.add))
            step(V.tensor_tensor(route_c[:, :], route_c[:, :], route_in[:, :], ALU.mult))
            step(V.tensor_scalar(pick[:, :], route_c[:, :], float(E), None, ALU.add))
            for l in range(2):
                step(V.tensor_tensor(ws[:, l, :], ws[:, l, :], ident, ALU.add))
            step(V.tensor_reduce(wc_mean[:, :], wc_raw[:, :, :], AX, ALU.add))
            step(V.tensor_scalar(wc_mean[:, :], wc_mean[:, :], 1.0 / C, None, ALU.mult))
            step(V.tensor_tensor(wc_raw[:, :, :], wc_raw[:, :, :],
                                 wc_mean[:, :].unsqueeze(2).to_broadcast([128, 16, 128]), ALU.subtract))

            def split(hi, lo, x):
                step(V.tensor_copy(hi, x))
                step(V.tensor_tensor(lo, x, hi.bitcast(F32), ALU.subtract))

            split(wch[:, :, :], wcl[:, :, :], wc_raw[:, :, :])
            ve.wait_ge(s_mlpw, 32)
            split(m1h[:, :], m1l[:, :], m1raw[:, :])
            split(m2h[:, :, :], m2l[:, :, :], m2raw[:, :, :])
            ve.wait_ge(s_w0row, 16 * PH)
            split(w0h[:, :, :], w0l[:, :, :], w0[:, :, :])
            V.memset(lv[:, :], 1.0).then_inc(s_ready, 1)

            def quad_x(group, k):
                ve.wait_ge(s_quad, at(group, 2, k + 1))
                V.tensor_tensor(quad[:, :], pF[0:KQ, :], xt[k][:, :], ALU.mult).then_inc(s_quadx, 1)

            def eps_0(group, k):
                ve.wait_ge(s_var0, at(group, 2, k + 1))
                V.tensor_scalar(eps0[:, :], pS[:, 0:32], 1.0 / (C - 1), EPS, ALU.mult, ALU.add)\
                    .then_inc(s_eps0, 1)

            def spread_0(group, k):
                ve.wait_ge(s_rstd0, at(group, 2, k + 1))
                V.tensor_copy(rst0w[:, :, :].rearrange("p b (t j) -> p b t j", j=PH),
                              rstd0[:, :].rearrange("p (b j) -> p b j", j=PH).unsqueeze(2)
                              .to_broadcast([128, 4, TAPS0 + 1, PH])).then_inc(s_rst0w, 1)

            def scale_x(group, k):
                ve.wait_ge(s_rb0, at(group, 2, k + 1))
                V.tensor_tensor(xs[0:KQ, :], xt[k][:, :], pF[0:KQ, :], ALU.mult).then_inc(s_xs, 1)

            def low0(group, k, js):
                for j in js:
                    ve.wait_ge(s_h0h, at(group, 2 * PH, PH * k + j + 1))
                    V.scalar_tensor_tensor(out=h0[:, 1, j, :, 1:1 + NW],
                                           in0=pC[j % 2][:, :].rearrange("p (b w) -> p b w", b=2), scalar=0.0,
                                           in1=h0[:, 0, j, :, 1:1 + NW].bitcast(F32), op0=ALU.max,
                                           op1=ALU.subtract).then_inc(s_h0l, 1)

            def eps(n, group, idx, buf=0, blocks=4):
                ve.wait_ge(ns[n]["var"], at(group, PER[n], idx))
                V.tensor_scalar(vare[n][:, 0:blocks], var_bank[n][buf][:, 0:blocks], 1.0 / (C - 1), EPS, ALU.mult, ALU.add)\
                    .then_inc(ns[n]["eps"], 1)

            def norm(n, group, idx, bank, buf=0, cols=512):
                ve.wait_ge(ns[n]["rb"], at(group, PER[n], idx))
                V.tensor_tensor(y[n][buf][:, 0:cols], y[n][buf][:, 0:cols], bank[:, 0:cols], ALU.mult)\
                    .then_inc(ns[n]["z"], 1)

            def centre_f(group):
                ve.wait_ge(s_ft, at(group, 1, 1))
                p = pM[1][:, :].rearrange("p (b c) -> p b c", b=GB)
                V.tensor_reduce(fsum[:, :], p, AX, ALU.add).then_inc(s_fsum, 1)
                ve.wait_ge(s_fsum, at(group, 1, 1))
                V.tensor_scalar(fmean[:, :], fsum[:, :], 1.0 / C, None, ALU.mult).then_inc(s_fmean, 1)
                ve.wait_ge(s_fmean, at(group, 1, 1))
                V.tensor_tensor(ftc[:, :, :], p, fmean[:, :].unsqueeze(2).to_broadcast([128, GB, 128]),
                                ALU.subtract).then_inc(s_ftc, 1)

            def low1(group, ms):
                for m in ms:
                    ve.wait_ge(s_g1h, at(group, MC, m + 1))
                    V.tensor_tensor(g1l[:, m, :], g1[m % 2][:, :], g1h[:, m, :].bitcast(F32), ALU.subtract)\
                        .then_inc(s_g1l, 1)

            def chain(s_done, per):
                k = [0]

                def link(group, ins, wait=True):
                    k[0] += 1
                    ins.then_inc(s_done, 1)
                    if wait:
                        ve.wait_ge(s_done, at(group, per, k[0]))
                return link

            def sigmoid(group):
                ve.wait_ge(s_exp3, at(group, 1, 1))
                link = chain(s_chain["sigmoid"], 2)
                link(group, V.tensor_scalar(sig[:, 1, :], sig[:, 0, :], 1.0, None, ALU.add))
                link(group, V.reciprocal(sig[:, 2, :], sig[:, 1, :]))
                V.tensor_scalar(imp[:, :], sig[:, 2, :], TEMP, None, ALU.add).then_inc(s_sig, 1)

            def normalise(group):
                ve.wait_ge(s_tot, at(group, 1, 1))
                link = chain(s_chain["total"], 1)
                link(group, V.reciprocal(rtot[:, :], pT[0][:, 0:GB]))
                V.scalar_tensor_tensor(out=impn[:, :], in0=imp[:, :], scalar=float(TN), in1=rtot[:, :],
                                       op0=ALU.mult, op1=ALU.mult).then_inc(s_impn, 1)

            def overs(group):
                ve.wait_ge(s_cum, at(group, 1, 1))
                link = chain(s_chain["over"], 1 + GB)
                link(group, V.tensor_copy(cums[:, :], pT[0][:, 0:GB]))
                for b in range(GB):
                    link(group, V.tensor_scalar(over[:, b, :], cst[:, RAMP:RAMP + TN + 1], cums[:, b:b + 1], 0.0,
                                                ALU.add, ALU.max), b == GB - 1)
                V.tensor_tensor(diff[:, :, :], over[:, :, 0:TN], over[:, :, 1:TN + 1], ALU.subtract)\
                    .then_inc(s_over, 1)

            def copy_shares(group):
                ve.wait_ge(s_wm, at(group, 1, 1))
                V.tensor_copy(wmat[:, :, :], pT[0][:, 0:GB * TN].rearrange("p (b n) -> p b n", b=GB))\
                    .then_inc(s_wmat, 1)

            def ln(group, src, dst, which):
                link = chain(s_chain[f"ln{which}"], 2 * GB)
                for b in range(GB):
                    link(group, V.bn_stats(bn[:, b, :], src[:, b, :]), False)
                wait_apart(ve, s_chain[f"ln{which}"], at(group, 2 * GB, GB))
                for b in range(GB):
                    link(group, V.bn_aggr(mv[:, b, :], bn[:, b, :]), b == GB - 1)
                V.tensor_scalar(lv[:, :], mv[:, :, 1], EPS, None, ALU.add).then_inc(s_ln, 1)
                ve.wait_ge(s_lr, at(group, 2, which))
                for b in range(GB):
                    x = V.tensor_scalar(dst[:, b, :], src[:, b, :], mv[:, b, 0:1], lr[:, b:b + 1],
                                        ALU.subtract, ALU.mult)
                x.then_inc(s_lx, 1)

            def ln1(group):
                ve.wait_ge(ns[4]["act"], at(group, 1, 1))
                ln(group, h[:, 0:GB * D].rearrange("p (b n) -> p b n", b=GB), lx, 1)

            NTOP = TOPK // 8

            def topk(group, rounds):
                for r in rounds:
                    if r == 0:
                        wait_apart(ve, s_s, at(group, 1, 1))
                    src = s if r == 0 else swork
                    for b in range(GB):
                        if r:
                            wait_apart(ve, s_top, at(group, TOPS, (2 * r - 1) * GB + b + 1))
                        V.max(top[:, b, :], src[:, b, :]).then_inc(s_top, 1)
                    if r < NTOP - 1:
                        for b in range(GB):
                            wait_apart(ve, s_top, at(group, TOPS, 2 * r * GB + b + 1))
                            V.match_replace(swork[:, b, :], top[:, b, :], src[:, b, :], NEG).then_inc(s_top, 1)
            TOPS = (2 * NTOP - 1) * GB

            def mask(group):
                ve.wait_ge(s_top, at(group, TOPS, TOPS))
                link = chain(s_chain["mask"], GB + 1)
                for b in range(GB):
                    link(group, V.scalar_tensor_tensor(out=s[:, b, :], in0=s[:, b, :], scalar=top[:, b, 7:8],
                                                       in1=s[:, b, :], op0=ALU.is_ge, op1=ALU.mult), b == GB - 1)
                link(group, V.tensor_reduce(smax[:, :], s[:, :, :], AX, ALU.max))
                V.tensor_scalar(nmax[:, :], smax[:, :], -1.0, None, ALU.mult).then_inc(s_sm, 1)

            def add_attn(group):
                ve.wait_ge(s_e, at(group, 1, 1))
                link = chain(s_chain["den"], 1)
                link(group, V.reciprocal(rden[:, :], den[:, :]), False)
                ve.wait_ge(s_hb, at(group, 1, 1))
                ve.wait_ge(s_wop, at(group, 1, 1))
                ve.wait_ge(s_chain["den"], at(group, 1, 1))
                for b in range(GB):
                    x = V.scalar_tensor_tensor(out=ha[:, b, :], in0=pT[0][:, D * b:D * b + D], scalar=rden[:, b:b + 1],
                                               in1=hb[:, b, :], op0=ALU.mult, op1=ALU.add)
                x.then_inc(s_ha, 1)

            def ln2(group):
                ve.wait_ge(s_ha, at(group, 1, 1))
                ln(group, ha[:, :, :], l2x, 2)

            def result(group):
                ve.wait_ge(s_hc, at(group, 1, 1))
                ve.wait_ge(s_fp, at(group, 4, 4))
                V.tensor_tensor(res[:, :, :], pT[1][:, 0:GB * D].rearrange("p (b d) -> p b d", b=GB), hc[:, :, :],
                                ALU.add).then_inc(s_res, 1)

            def body(gf, gb, gc):
                ng = gf and nxt(gf)
                if gc: normalise(gc)
                if gf: low0(gf, 0, range(0, 4))
                if gc: overs(gc)
                if gf: low0(gf, 0, range(4, 8))
                if gc: copy_shares(gc)
                if gb: eps(2, gb, 2)
                if gc: eps(4, gc, 1, blocks=2)
                if gf: quad_x(gf, 1)
                if gb: norm(2, gb, 2, pF)
                if gc: norm(4, gc, 1, pT[0], cols=GB * TN)
                if gf: eps_0(gf, 1)
                if gf: spread_0(gf, 1)
                if gf: eps(1, gf, 1, 0)
                if gf: scale_x(gf, 1)
                if gf: norm(1, gf, 1, pF, 0)
                if gf: eps(1, gf, 2, 1)
                if gc: ln1(gc)
                if gf: norm(1, gf, 2, pF, 1)
                if gf: low0(gf, 1, range(0, 4))
                if gb: eps(3, gb, 1)
                if gc: topk(gc, range(0, 1))
                if gf: low0(gf, 1, range(4, 8))
                if gb: norm(3, gb, 1, pM[1])
                if gc: topk(gc, range(1, 4))
                if gb: centre_f(gb)
                if gc: topk(gc, range(4, 8))
                if gb: low1(gb, range(MC))
                if gf: eps(2, gf, 1)
                if gc: mask(gc)
                if gf: quad_x(ng, 0)
                if gf: norm(2, gf, 1, pF)
                if gf: eps_0(ng, 0)
                if gf: spread_0(ng, 0)
                if gc: add_attn(gc)
                if gc: ln2(gc)
                if gb: sigmoid(gb)
                if gf: eps(1, gf, 3, 0)
                if gf: scale_x(ng, 0)
                if gf: norm(1, gf, 3, pF, 0)
                if gf: eps(1, gf, 4, 1)
                if gf: norm(1, gf, 4, pF, 1)
                if gc: result(gc)

            quad_x(PRE, 0)
            eps_0(PRE, 0)
            spread_0(PRE, 0)
            scale_x(PRE, 0)
            body(PRE, None, None)
            body(FIRST, PRE, None)
            with ve.Fori(0, LOOPS) as i:
                body((i, 2), (i, 1), (i, 0))
            body(None, (None, NG - 1), (None, NG - 2))
            body(None, None, (None, NG - 1))

        @block.gpsimd
        def _(po):
            G = nc.gpsimd

            def root(out, in_):
                return G.tensor_tensor(out, in_, cst[:, HALF:HALF + in_.shape[1]], ALU.pow)

            def keep(out, in_):
                return G.tensor_scalar(out, in_, 1.0, 0.0, ALU.mult, ALU.add)

            def root0(group, k):
                po.wait_ge(s_eps0, at(group, 2, k + 1))
                root(rstd0[:, :], eps0[:, :]).then_inc(s_rstd0, 1)

            def x_low(group, k):
                po.wait_ge(s_xh, at(group, 2, k + 1))
                G.tensor_tensor(xl[0:KQ, :], xs[0:KQ, :], xh[0:KQ, :].bitcast(F32), ALU.subtract).then_inc(s_xl, 1)

            def rootn(n, group, idx, blocks=4):
                po.wait_ge(ns[n]["eps"], at(group, PER[n], idx))
                root(rstd[n][:, 0:blocks], vare[n][:, 0:blocks]).then_inc(ns[n]["rstd"], 1)

            def pads0(group, k):
                wait_apart(po, s_h0l, at(group, 2 * PH, PH * k + PH))
                for dj, dw, sj, sw in ((6, 0, 2, 1), (7, 0, 1, 1), (0, NW + 1, 6, NW), (1, NW + 1, 5, NW)):
                    x = keep(h0[:, :, dj, :, dw:dw + 1], h0[:, :, sj, :, sw:sw + 1].bitcast(F32))
                x.then_inc(s_pad0, 1)

            def splitn(n, group, idx, hi, lo, src):
                wait_apart(po, ns[n]["act"], at(group, PER[n], idx))
                keep(hi, src).then_inc(ns[n]["hi"], 1)
                po.wait_ge(ns[n]["hi"], at(group, PER[n], idx))
                G.tensor_tensor(lo, src, hi.bitcast(F32), ALU.subtract).then_inc(ns[n]["lo"], 1)

            def split1(group, k, r):
                splitn(1, group, 2 * k + r + 1, h1[:, 0, r, :, 1:1 + T2], h1[:, 1, r, :, 1:1 + T2],
                       y[1][r][:, :].rearrange("p (b w) -> p b w", b=2))

            def pads1(group, k):
                wait_apart(po, ns[1]["lo"], at(group, 4, 2 * k + 2))
                for dr, dw, sr, sw in ((1, 0, 1, 1), (0, T2 + 1, 0, T2)):
                    x = keep(h1[:, :, dr, :, dw:dw + 1], h1[:, :, sr, :, sw:sw + 1].bitcast(F32))
                x.then_inc(s_pad1, 1)

            def split2(group, k):
                b = slice(2 * k, 2 * k + 2)
                splitn(2, group, k + 1, h2[:, 0, b, 1:1 + T2], h2[:, 1, b, 1:1 + T2],
                       y[2][0][:, :].rearrange("p (b w) -> p b w", b=2))
                wait_apart(po, ns[2]["lo"], at(group, 2, k + 1))
                for dw, sw in ((0, 2), (T2 + 1, T2 - 1)):
                    x = keep(h2[:, :, b, dw:dw + 1], h2[:, :, b, sw:sw + 1].bitcast(F32))
                x.then_inc(s_pad2, 1)

            def split3(group):
                splitn(3, group, 1, fh[:, :], fl[:, :], f[:, :])

            def high1(group, ms):
                for m in ms:
                    wait_apart(po, s_g1, at(group, MC, m + 1))
                    keep(g1h[:, m, :], g1[m % 2][:, :]).then_inc(s_g1h, 1)

            def add_bout(group):
                po.wait_ge(ns[4]["act"], at(group, 1, 1))
                G.tensor_tensor(hb[:, :, :], h[:, 0:GB * D].rearrange("p (b n) -> p b n", b=GB),
                                bout[:, :].unsqueeze(1).to_broadcast([128, GB, D]), ALU.add).then_inc(s_hb, 1)

            def add_bo(group):
                po.wait_ge(s_ha, at(group, 1, 1))
                G.tensor_tensor(hc[:, :, :], ha[:, :, :], bo[:, :].unsqueeze(1).to_broadcast([128, GB, D]),
                                ALU.add).then_inc(s_hc, 1)

            def ln_root(group, which):
                po.wait_ge(s_ln, at(group, 2, which))
                root(lr[:, :], lv[:, :]).then_inc(s_lr, 1)

            def body(gf, gb, gc):
                ng = gf and nxt(gf)
                if gf: pads0(gf, 0)
                if gb: rootn(2, gb, 2)
                if gc: rootn(4, gc, 1, 2)
                if gf: root0(gf, 1)
                if gf: rootn(1, gf, 1)
                if gb: split2(gb, 1)
                if gf: x_low(gf, 1)
                if gf: rootn(1, gf, 2)
                if gf: split1(gf, 0, 0)
                if gc: ln_root(gc, 1)
                if gc: add_bout(gc)
                if gf: split1(gf, 0, 1)
                if gf: pads1(gf, 0)
                if gb: rootn(3, gb, 1)
                if gb: split3(gb)
                if gf: pads0(gf, 1)
                if gb: high1(gb, range(MC))
                if gf: rootn(2, gf, 1)
                if gf: root0(ng, 0)
                if gf: split2(gf, 0)
                if gc: ln_root(gc, 2)
                if gc: add_bo(gc)
                if gf: rootn(1, gf, 3)
                if gf: x_low(ng, 0)
                if gf: rootn(1, gf, 4)
                if gf: split1(gf, 1, 0)
                if gf: split1(gf, 1, 1)
                if gf: pads1(gf, 1)

            po.wait_ge(s_ready, 2)
            root0(PRE, 0)
            x_low(PRE, 0)
            body(PRE, None, None)
            body(FIRST, PRE, None)
            with po.Fori(0, LOOPS) as i:
                body((i, 2), (i, 1), (i, 0))
            body(None, (None, NG - 1), (None, NG - 2))
            body(None, None, (None, NG - 1))


def shape_constants():
    c = np.zeros((128, NCONST), np.float32)
    r = np.arange(128)
    c[:, IDENT:IDENT + 128] = np.eye(128)
    c[:, TRI:TRI + 128] = r[:, None] <= r[None, :]
    c[:, SHIFT:SHIFT + 128] = np.eye(128) - np.eye(128, k=1)
    c[:, MEANS:MEANS + 128] = 1.0 / C
    c[:, ONES:ONES + 128] = 1.0
    c[:, RAMP:RAMP + TN] = -np.arange(TN)
    c[:, RAMP + TN] = -1e30
    c[:, PHASE:PHASE + PH] = r[:, None] % PH == np.arange(PH)
    c[:, SAME:SAME + KQ] = r[:, None] % PH == np.arange(KQ)[None, :] % PH
    c[:, HALF:HALF + 32] = -0.5
    c[:, ROWNO] = r
    return c


def kernel(**inputs):
    import concourse.bacc as bacc
    from concourse.bass_utils import run_bass_kernel_spmd

    p = {k.replace("L0_", ""): np.asarray(x) for k, x in inputs.items()}
    x = np.pad(p["x"][:, 0, :], ((0, 0), (PAD0, PAD0)), mode="reflect")
    at_ = (STRIDE0 * PH * np.arange(NW)[None, None, :] + STRIDE0 * np.arange(PH)[None, :, None]
           + np.arange(TAPS0)[:, None, None])
    win = x[:, at_].reshape(B // 2, 2, KX, NW).transpose(0, 2, 1, 3).reshape(B // 2, KX, N)
    win = np.pad(win, ((0, 2), (0, 0), (0, 0)))
    col = lambda v: v.reshape(-1, 128).T
    vecs = np.concatenate(
        [p["tok_conv0_w"][:, 0, :]] + [p[f"tok_conv{n}_b"][:, None] for n in range(4)]
        + [p[f"tok_n{n}_w"][:, None] for n in range(5)] + [p[f"tok_n{n}_b"][:, None] for n in range(5)]
        + [col(p["tok_mlp_b1"]), col(p["tok_mlp_b2"]), col(p["tok_mlp_w3"]), col(p["ffn_bs"][0, 0]),
           col(p["ffn_bs"][1, 0]), col(p["ffn_bi"]), np.broadcast_to(p["tok_mlp_b3"][None, :], (128, 1))], axis=1)
    wconv = np.concatenate([p[f"tok_conv{n}_w"].transpose(1, 2, 0) for n in (1, 2, 3)], axis=1)
    arrays = {
        "consts": shape_constants(),
        "vecs": vecs,
        "wconv": wconv,
        "m1": p["tok_mlp_w1"],
        "m2": p["tok_mlp_w2"].reshape(MC, 128, DM).transpose(1, 0, 2),
        "off0": p["tok_n0_b"][None, :],
        "wqkv": np.concatenate([p["attn_W_qkv"], p["attn_b_qkv"][None, :]]),
        "wout": p["attn_W_out"],
        "bout": np.broadcast_to(p["attn_b_out"][None, :], (128, D)),
        "wi": p["ffn_Wi"].T,
        "ws": p["ffn_Ws"][:, 0].transpose(2, 0, 1),
        "brt": p["ffn_br"].transpose(1, 0, 2),
        "wo": p["ffn_Wo"].T,
        "bo": np.broadcast_to(p["ffn_bo"][None, :], (128, D)),
        "route": np.broadcast_to(p["ffn_route_id"][None, :], (E, B * RG)),
        "wr": np.pad(p["ffn_Wr"].transpose(1, 3, 0, 2), ((0, 1), (0, 0), (0, 0), (0, 0))),
        "x": win,
    }
    arrays = {k: np.ascontiguousarray(v) for k, v in arrays.items()}
    nc = bacc.Bacc("TRN2", target_bir_lowering=False, num_devices=1)
    a = {k: nc.dram_tensor(f"in_{k}", v.shape, mybir.dt.from_np(v.dtype), kind="ExternalInput").ap()
         for k, v in arrays.items()}
    a["out"] = nc.dram_tensor("out", (B, C, TN), F32, kind="ExternalOutput").ap()
    build(nc, a)
    r = run_bass_kernel_spmd(nc, [{f"in_{k}": v for k, v in arrays.items()}], core_ids=[0])
    return r.results[0]["out"]
```

```python
from contextlib import ExitStack

import numpy as np

import concourse.bass as bass
from concourse import mybir

F32 = mybir.dt.float32
F32R = mybir.dt.float32r
I32 = mybir.dt.int32
ALU = mybir.AluOpType
ACT = mybir.ActivationFunctionType
AX = mybir.AxisListType.X

B, L = 32, 10240
C = 128
GB = 4
NG = B // GB
T0, T1, T2, T3 = 2048, 512, 256, 128
PH = 8
NW = T0 // PH
TAPS0, STRIDE0, PAD0 = 10, 5, 3
KX = TAPS0 * PH
KQ = KX + PH
K0 = KQ + 1
N = 2 * NW
W1P = T1 // 2 + 2
W2P = T2 + 2
DM = 512
MC = DM // C
TN = T3 // 2
D = 64
TOPK = T3 // 2
RG = 2
NR = GB * RG
TOK = 64
E = 16
EPS, TEMP = 1e-5, 1e-5
NEG = -3.0e38

IDENT, TRI, SHIFT, MEANS, ONES = 0, 128, 256, 384, 512
RAMP = 640
PHASE = RAMP + TN + 1
SAME = PHASE + PH
HALF = SAME + KQ
ROWNO = HALF + 32
NCONST = ROWNO + 1
CEN = TAPS0 + 4
GAIN, OFFS = CEN, CEN + 5
MB1, MB2, MW3 = CEN + 10, CEN + 14, CEN + 18
BS, BI, B3 = CEN + 22, CEN + 24, CEN + 25
NVEC = CEN + 26


def at(group, per, k):
    i, off = group
    c = off * per + k
    return c if i is None else i * per + c


def build(nc, a):
    with ExitStack() as ctx:
        def sb(name, shape, dt=F32):
            return ctx.enter_context(nc.sbuf_tensor(name, shape, dt))

        def ps(name):
            return ctx.enter_context(nc.psum_tensor(name, [128, 512], F32))

        def sem(name):
            return ctx.enter_context(nc.semaphore(name))

        cst = sb("cst", [128, NCONST])
        vec = sb("vec", [128, NVEC])
        cen = sb("cen", [128, CEN])
        neg3 = sb("neg3", [128, 1])
        ident = cst[:, IDENT:IDENT + 128]
        w0rep = sb("w0rep", [128, KQ])
        w0gain = sb("w0gain", [128, KQ])
        w0t = sb("w0t", [KQ, 128])
        gram = sb("gram", [KQ, KQ])
        w0h, w0l = sb("w0h", [K0, PH, 128], F32R), sb("w0l", [K0, PH, 128], F32R)
        wc_mean = sb("wc_mean", [128, 16])
        wch, wcl = sb("wch", [128, 16, 128], F32R), sb("wcl", [128, 16, 128], F32R)
        m1h, m1l = sb("m1h", [128, DM], F32R), sb("m1l", [128, DM], F32R)
        m2h, m2l = sb("m2h", [128, MC, DM], F32R), sb("m2l", [128, MC, DM], F32R)
        wqkv = sb("wqkv", [D + 1, 3 * D])
        wout = sb("wout", [D, D])
        bout = sb("bout", [128, D])
        wi = sb("wi", [D, 128])
        ws = sb("ws", [128, 2, 128])
        brt = sb("brt", [E, 2, 128])
        wo = sb("wo", [128, D])
        bo = sb("bo", [128, D])
        route_i = sb("route_i", [E, B * RG], I32)
        route_f = sb("route_f", [E, B * RG])
        route_c = sb("route_c", [1, B * RG])
        route_in = sb("route_in", [1, B * RG])
        pick = sb("pick", [1, B * RG], I32)
        onehot = sb("onehot", [E, B * RG])

        xt = [sb(f"xt{k}", [KQ, N]) for k in range(2)]
        quad = sb("quad", [KQ, N])
        eps0, rstd0, newt = (sb(x, [128, 32]) for x in ("eps0", "rstd0", "newt"))
        rst0w = sb("rst0w", [128, 4, KQ])
        xs = sb("xs", [K0, N])
        xh, xl = sb("xh", [K0, N], F32R), sb("xl", [K0, N], F32R)
        h0 = sb("h0", [128, 2, PH, 2, NW + 2], F32R)
        h1 = sb("h1", [128, 2, 2, 2, W1P], F32R)
        h2 = sb("h2", [128, 2, GB, W2P], F32R)
        KINDS = (1, 2, 3, 4)
        WIDE = {1: 512, 2: 512, 3: 512, 4: GB * TN}
        y = {n: [sb(f"y{n}_{r}", [128, WIDE[n]]) for r in range(2 if n == 1 else 1)] for n in KINDS}
        sq = {n: [sb(f"sq{n}_{r}", [128, WIDE[n]]) for r in range(2 if n == 1 else 1)] for n in KINDS}
        vare = {n: sb(f"vare{n}", [128, 4]) for n in KINDS}
        rstd = {n: sb(f"rstd{n}", [128, 4]) for n in KINDS}
        f = y[3][0]
        fh, fl = sb("fh", [128, 512], F32R), sb("fl", [128, 512], F32R)
        fsum = sb("fsum", [128, GB])
        fmean = sb("fmean", [128, GB])
        ftc = sb("ftc", [128, GB, 128])
        g1 = [sb(f"g1_{m}", [128, 512]) for m in range(2)]
        g1h, g1l = sb("g1h", [128, MC, 512], F32R), sb("g1l", [128, MC, 512], F32R)
        g2 = sb("g2", [128, MC, 512])
        sig = sb("sig", [128, 3, GB])
        imp = sb("imp", [128, GB])
        rtot = sb("rtot", [128, GB])
        impn = sb("impn", [128, GB])
        cums = sb("cums", [128, GB])
        over = sb("over", [128, GB, TN + 1])
        diff = sb("diff", [128, GB, TN])
        wmat = sb("wmat", [128, GB, TN])
        h = y[4][0]
        bn = sb("bn", [128, GB, 6])
        mv = sb("mv", [128, GB, 2])
        lv = sb("lv", [128, GB])
        lr = sb("lr", [128, GB])
        lx = sb("lx", [128, GB, D])
        lxt = sb("lxt", [D + 1, 512])
        hb = sb("hb", [128, GB, D])
        qT, kT = sb("qT", [D, 512]), sb("kT", [D, 512])
        v = sb("v", [128, GB, D])
        s = sb("s", [128, GB, 128])
        swork = sb("swork", [128, GB, 128])
        top = sb("top", [128, GB, 8])
        smax = sb("smax", [128, GB])
        nmax = sb("nmax", [128, GB])
        e = swork
        den = sb("den", [128, GB])
        rden = sb("rden", [128, GB])
        eT, oT = s, qT
        ha = sb("ha", [128, GB, D])
        hc = sb("hc", [128, GB, D])
        l2x = sb("l2x", [128, GB, D])
        l2t = lxt[0:D, :]
        ub = sb("ub", [128, 3, 512])
        u = [ub[:, n, :] for n in range(3)]
        wr = sb("wr", [128, NR, 2, 128])
        res = sb("res", [128, GB, D])
        w0 = ub[0:K0, 0:2, :].rearrange("p a (j c) -> p (a j) c", c=128)
        wc_raw = g2[:, :, :].rearrange("p m (t c) -> p (m t) c", c=128)
        m1raw = y[1][0]
        m2raw = wr[:, :, :, :].rearrange("p (k n) l c -> p k (n l c)", k=MC)

        pF, pC = ps("pF"), [ps(f"pC{n}") for n in range(3)]
        pM = [ps("pM0"), ps("pM1")]
        pT = [ps("pT0"), ps("pT1")]
        var_bank = {1: pC, 2: [pC[2]], 3: [pM[0]], 4: [pM[1]]}

        s_const, s_setup, s_row = sem("const_loaded"), sem("setup_pe"), sem("ones_rows_set")
        s_w0row, s_mlpw = sem("w0_row_loaded"), sem("mlp_weights_loaded")
        s_dset, s_ready = sem("setup_dve"), sem("setup_done")
        s_x = [sem(f"x_loaded{k}") for k in range(2)]
        s_quad, s_quadx, s_var0, s_eps0 = sem("quad"), sem("quad_times_x"), sem("var0"), sem("eps0")
        s_rstd0, s_rst0w, s_rb0 = sem("rstd0"), sem("rstd0_spread"), sem("rstd0_on_rows")
        s_xs, s_xh, s_xl = sem("x_scaled"), sem("x_high"), sem("x_low")
        s_c0, s_h0h, s_h0l, s_pad0 = sem("conv0"), sem("h0_high"), sem("h0_low"), sem("h0_pads")
        s_c1, s_c2, s_c3 = sem("conv1"), sem("conv2"), sem("conv3")
        s_conv = {1: s_c1, 2: s_c2, 3: s_c3}
        s_pad1, s_pad2 = sem("h1_pads"), sem("h2_pads")
        ns = {n: {x: sem(f"n{n}_{x}") for x in ("y", "sq", "var", "eps", "rstd", "rb", "z", "act", "hi", "lo")}
              for n in KINDS}
        PER = {1: 4, 2: 2, 3: 1, 4: 1}
        s_ft, s_fsum, s_fmean, s_ftc = sem("fT"), sem("f_sum"), sem("f_mean"), sem("fT_centred")
        s_m1, s_g1, s_g1h, s_g1l = sem("mlp1"), sem("gelu1"), sem("gelu1_high"), sem("gelu1_low")
        s_m2, s_g2, s_m3, s_exp3, s_sig = sem("mlp2"), sem("gelu2"), sem("mlp3"), sem("exp3"), sem("sigmoid")
        s_tot, s_impn, s_cum, s_over, s_wm = sem("total"), sem("imp_normed"), sem("cumsum"), sem("over"), sem("wmat_product")
        s_wmat, s_pool, s_hb = sem("wmat"), sem("pooled"), sem("h_plus_bout")
        s_ln, s_lr, s_lx, s_lxp, s_lxt = (sem(x) for x in ("ln_stats", "ln_rstd", "ln_x", "ln_xT_product", "ln_xT"))
        s_qkvp, s_qk, s_v, s_sp, s_s = (sem(x) for x in ("qkv_product", "qk", "v", "score_product", "scores"))
        s_top, s_sm, s_e, s_etp, s_et = (sem(x) for x in ("topk", "masked", "exp", "expT_product", "expT"))
        s_op, s_oT, s_wop, s_ha = (sem(x) for x in ("attn_product", "attnT", "attn_out_product", "attn_added"))
        s_hc = sem("ha_plus_bo")
        s_fp, s_u, s_res, s_out, s_wr = (sem(x) for x in ("ffn_product", "ffn_relu", "result", "stored", "experts_loaded"))

        s_chain = {x: sem(f"chain_{x}") for x in ("sigmoid", "total", "over", "ln1", "ln2", "mask", "den")}

        LOADS = [(cst[:, :], a["consts"]), (vec[:, :], a["vecs"]), (wc_raw[:, :, :], a["wconv"]),
                 (wqkv[:, :], a["wqkv"]), (wout[:, :], a["wout"]), (bout[:, :], a["bout"]),
                 (wi[:, :], a["wi"]), (ws[:, :, :], a["ws"]), (brt[:, :, :], a["brt"]), (wo[:, :], a["wo"]),
                 (bo[:, :], a["bo"]), (route_i[:, :], a["route"])]
        LOADED = 16 * len(LOADS)
        block = ctx.enter_context(nc.Block())

        def wait_apart(engine, semaphore, value):
            if not isinstance(value, int):
                value = engine.to_reg(value)
            engine.wait_ge(s_ready, 2)
            engine.wait_ge(semaphore, value)

        PRE, FIRST = (None, 0), (None, 1)
        LOOPS = NG - 3

        def nxt(group):
            return group[0], group[1] + 1

        @block.sync
        def _(sp):
            for dst, src in LOADS:
                sp.dma_start(dst, src).then_inc(s_const, 16)
            sp.dma_start(m1raw[:, :], a["m1"]).then_inc(s_mlpw, 16)
            sp.dma_start(m2raw[:, :, :], a["m2"]).then_inc(s_mlpw, 16)
            sp.wait_ge(s_ready, 1)
            for j in range(PH):
                sp.dma_start(w0[KQ:K0, j, :], a["off0"]).then_inc(s_w0row, 16)
            sp.wait_ge(s_row, 2)

            def load_x(group, k, first=False):
                i, off = group
                if not first:
                    sp.wait_ge(s_xs, at(group, 2, k + 1 - 2))
                n = off * 2 + k if i is None else i * 2 + (off * 2 + k)
                src = a["x"][n, :, :] if i is None else a["x"][bass.ds(n, 1), :, :].rearrange("a r n -> (a r) n")
                sp.dma_start(xt[k][0:KX, :], src).then_inc(s_x[k], 16)

            def load_experts(group):
                i, off = group
                for n in range(NR):
                    c = off * NR + n if i is None else i * NR + (off * NR + n)
                    src = pick[0:1, c:c + 1] if i is None else pick[0:1, bass.ds(c, 1)]
                    x = sp.value_load(src, min_val=0, max_val=E)
                    sp.dma_start(wr[:, n, :, :], a["wr"][bass.ds(x, 1), :, :, :].rearrange("e p l o -> (e p) l o"))\
                      .then_inc(s_wr, 16)

            def store(group):
                i, off = group
                sp.wait_ge(s_res, at(group, 1, 1))
                src = res[:, :, :]
                n = off * GB if i is None else i * GB + off * GB
                o = a["out"][bass.ds(n, GB), :, :] if i is not None else a["out"][n:n + GB, :, :]
                sp.dma_start(o.rearrange("b c n -> c b n"), src).then_inc(s_out, 16)
                sp.wait_ge(s_out, at(group, 16, 16))

            load_x(PRE, 0, True)
            load_x(PRE, 1, True)
            def body(gf, gb, gc, gd):
                if gf:
                    load_x(nxt(gf), 0)
                    load_x(nxt(gf), 1)
                if gd:
                    store(gd)
                if gc:
                    load_experts(gc)

            body(PRE, None, None, None)
            body(FIRST, PRE, None, None)
            body((None, 2), FIRST, PRE, None)
            with sp.Fori(0, LOOPS) as i:
                body((i, 3), (i, 2), (i, 1), (i, 0))
            body(None, (None, NG - 1), (None, NG - 2), (None, NG - 3))
            body(None, None, (None, NG - 1), (None, NG - 2))
            body(None, None, None, (None, NG - 1))
            sp.wait_ge(s_x[1], 16 * (NG + 1))
            sp.wait_ge(s_out, 16 * NG)

        @block.tensor
        def _(pe):
            def mm(out, lhs, rhs, start=True, stop=True):
                return nc.tensor.matmul(out, lhs, rhs, start=start, stop=stop)

            pe.wait_ge(s_const, LOADED)
            mm(pM[0][:, 0:CEN], cst[:, MEANS:MEANS + 128], vec[:, 0:CEN]).then_inc(s_setup, 1)
            pe.wait_ge(s_dset, 2)
            mm(pF[0:KQ, 0:KQ], w0rep[:, :], w0rep[:, :]).then_inc(s_setup, 1)
            pe.wait_ge(s_dset, 3)
            nc.tensor.transpose(pC[0][0:KQ, 0:128], w0gain[:, :], ident).then_inc(s_setup, 1)

            def quad_form(group, k):
                pe.wait_ge(s_x[k], at(group, 16, 16))
                if not (group is PRE and k == 0):
                    pe.wait_ge(s_xs, at(group, 2, k))
                mm(pF[0:KQ, :], gram[:, :], xt[k][:, :]).then_inc(s_quad, 1)

            def var0(group, k):
                pe.wait_ge(s_quadx, at(group, 2, k + 1))
                for b in range(4):
                    m = mm(pF[:, PH * b:PH * b + PH], quad[:, 128 * b:128 * b + 128],
                           cst[0:KQ, PHASE:PHASE + PH])
                m.then_inc(s_var0, 1)

            def spread0(group, k):
                pe.wait_ge(s_rst0w, at(group, 2, k + 1))
                for b in range(4):
                    m = mm(pF[0:KQ, 128 * b:128 * b + 128], rst0w[:, b, :], ident)
                m.then_inc(s_rb0, 1)

            def split3(out, wh, wl, xhi, xlo, first=True, last=True):
                mm(out, wh, xhi, first, False)
                mm(out, wh, xlo, False, False)
                return mm(out, wl, xhi, False, last)

            def conv0(group, k, js, before):
                if js[0] == 0:
                    pe.wait_ge(s_xh, at(group, 2, k + 1))
                    pe.wait_ge(s_xl, at(group, 2, k + 1))
                for j in js:
                    if j >= 3:
                        pe.wait_ge(s_h0l, at(group, 2 * PH, PH * k + j - 2))
                    elif before and before[j]:
                        n, value = before[j]
                        pe.wait_ge(ns[n]["z"], value)
                    split3(pC[j % 3][:, :], w0h[:, j, :], w0l[:, j, :], xh[:, :], xl[:, :]).then_inc(s_c0, 1)

            def conv1(group, k, r, taps):
                if r == 0 and taps[0] == 0:
                    pe.wait_ge(s_h0l, at(group, 2 * PH, PH * k + PH))
                    pe.wait_ge(s_pad0, at(group, 2, k + 1))
                for t in taps:
                    p = 4 * r - 2 + t
                    o = 1 + p // PH
                    m = split3(pC[r][:, :], wch[:, t, :], wcl[:, t, :], h0[:, 0, p % PH, :, o:o + NW],
                               h0[:, 1, p % PH, :, o:o + NW], t == 0, t == 7)
                if taps[-1] == 7:
                    m.then_inc(s_c1, 1)

            def conv2(group, k, front):
                pe.wait_ge(ns[1]["lo"], at(group, 4, 2 * k + 2))
                pe.wait_ge(s_pad1, at(group, 2, k + 1))
                if front:
                    pe.wait_ge(s_h0l, at(front[0], 2 * PH, PH * front[1] + 6))
                for t in range(4):
                    r, o = (t + 1) % 2, (0 if t == 0 else 2 if t == 3 else 1)
                    m = split3(pC[2][:, :], wch[:, 8 + t, :], wcl[:, 8 + t, :], h1[:, 0, r, :, o:o + T2],
                               h1[:, 1, r, :, o:o + T2], t == 0, t == 3)
                m.then_inc(s_c2, 1)

            def var(n, group, idx, buf=0, blocks=4):
                pe.wait_ge(ns[n]["sq"], at(group, PER[n], idx))
                for b in range(blocks):
                    m = mm(var_bank[n][buf][:, b:b + 1], sq[n][buf][:, 128 * b:128 * b + 128], cst[:, ONES:ONES + 1])
                m.then_inc(ns[n]["var"], 1)

            def spread(n, group, idx, bank, blocks=4):
                pe.wait_ge(ns[n]["rstd"], at(group, PER[n], idx))
                for b in range(blocks):
                    m = mm(bank[:, 128 * b:128 * b + 128], rstd[n][:, b:b + 1].to_broadcast([128, 128]), ident)
                m.then_inc(ns[n]["rb"], 1)

            def conv3(group, gc):
                pe.wait_ge(ns[2]["lo"], at(group, 2, 2))
                pe.wait_ge(s_pad2, at(group, 2, 2))
                if gc:
                    pe.wait_ge(ns[4]["z"], at(gc, 1, 1))
                for t in range(4):
                    m = split3(pM[0][:, :], wch[:, 12 + t, :], wcl[:, 12 + t, :], h2[:, 0, :, t:t + 2 * T3 - 1:2],
                               h2[:, 1, :, t:t + 2 * T3 - 1:2], t == 0, t == 3)
                m.then_inc(s_c3, 1)

            def f_transposes(group):
                pe.wait_ge(ns[3]["act"], at(group, 1, 1))
                for b in range(GB):
                    m = nc.tensor.transpose(pM[1][:, 128 * b:128 * b + 128], f[:, 128 * b:128 * b + 128], ident)
                m.then_inc(s_ft, 1)

            def mlp1(group, ms):
                pe.wait_ge(ns[3]["lo"], at(group, 1, 1))
                for m_ in ms:
                    if m_ == 1:
                        pe.wait_ge(s_ftc, at(group, 1, 1))
                    if m_ >= 2:
                        pe.wait_ge(s_g1, at(group, MC, m_ - 1))
                    w = slice(128 * m_, 128 * m_ + 128)
                    split3(pM[m_ % 2][:, :], m1h[:, w], m1l[:, w], fh[:, :], fl[:, :]).then_inc(s_m1, 1)

            def mlp2(group, ms):
                if ms[0] == 0:
                    pe.wait_ge(s_g1l, at(group, MC, MC))
                for m_ in ms:
                    if m_ >= 2:
                        pe.wait_ge(s_g2, at(group, MC, m_ - 1))
                    w = slice(128 * m_, 128 * m_ + 128)
                    for kc in range(MC):
                        m = split3(pM[m_ % 2][:, :], m2h[:, kc, w], m2l[:, kc, w], g1h[:, kc, :], g1l[:, kc, :],
                                   kc == 0, kc == MC - 1)
                    m.then_inc(s_m2, 1)

            def mlp3(group):
                pe.wait_ge(s_g2, at(group, MC, MC))
                for b in range(GB):
                    for kc in range(MC):
                        m = mm(pM[0][:, b:b + 1], g2[:, kc, 128 * b:128 * b + 128],
                               vec[:, MW3 + kc:MW3 + kc + 1], kc == 0, kc == MC - 1)
                m.then_inc(s_m3, 1)

            def total(group):
                pe.wait_ge(s_sig, at(group, 1, 1))
                mm(pM[1][:, 0:GB], cst[:, ONES:ONES + 128], imp[:, :]).then_inc(s_tot, 1)

            def cumsum(group):
                pe.wait_ge(s_impn, at(group, 1, 1))
                mm(pM[1][:, 0:GB], cst[:, TRI:TRI + 128], impn[:, :]).then_inc(s_cum, 1)

            def shares(group):
                pe.wait_ge(s_over, at(group, 1, 1))
                mm(pM[0][:, 0:GB * TN], cst[:, SHIFT:SHIFT + 128], diff[:, :, :]).then_inc(s_wm, 1)

            def pool(group):
                pe.wait_ge(s_wmat, at(group, 1, 1))
                for b in range(GB):
                    m = mm(pM[1][:, TN * b:TN * b + TN], ftc[:, b, :], wmat[:, b, :])
                m.then_inc(s_pool, 1)

            def x_transposes(group):
                wait_apart(pe, s_lx, at(group, 2, 1))
                for b in range(GB):
                    m = nc.tensor.transpose(pT[0][0:D, 128 * b:128 * b + 128], lx[:, b, :], ident)
                m.then_inc(s_lxp, 1)

            def qkv(group, gd):
                pe.wait_ge(s_lxt, at(group, 2, 1))
                if gd:
                    pe.wait_ge(s_res, at(gd, 1, 1))
                mm(pT[1][0:D, :], wqkv[:, 0:D], lxt[:, :]).then_inc(s_qkvp, 1)
                mm(pT[0][0:D, :], wqkv[:, D:2 * D], lxt[:, :]).then_inc(s_qkvp, 1)
                pe.wait_ge(s_qk, at(group, 2, 1))
                for b in range(GB):
                    m = mm(pT[1][:, D * b:D * b + D], lxt[:, 128 * b:128 * b + 128], wqkv[:, 2 * D:3 * D])
                m.then_inc(s_qkvp, 1)

            def scores(group):
                pe.wait_ge(s_qk, at(group, 2, 2))
                for b in range(GB):
                    w = slice(128 * b, 128 * b + 128)
                    m = mm(pT[0][:, w], qT[:, w], kT[:, w])
                m.then_inc(s_sp, 1)

            def e_transposes(group):
                pe.wait_ge(s_e, at(group, 1, 1))
                for b in range(GB):
                    m = nc.tensor.transpose(pT[0][:, 128 * b:128 * b + 128], e[:, b, :], ident)
                m.then_inc(s_etp, 1)

            def attend(group):
                pe.wait_ge(s_et, at(group, 1, 1))
                pe.wait_ge(s_v, at(group, 1, 1))
                for b in range(GB):
                    m = mm(pT[1][0:D, 128 * b:128 * b + 128], v[:, b, :], eT[:, b, :])
                m.then_inc(s_op, 1)

            def attn_out(group):
                pe.wait_ge(s_oT, at(group, 1, 1))
                for b in range(GB):
                    m = mm(pT[0][:, D * b:D * b + D], oT[:, 128 * b:128 * b + 128], wout[:, :])
                m.then_inc(s_wop, 1)

            def x2_transposes(group):
                wait_apart(pe, s_lx, at(group, 2, 2))
                for b in range(GB):
                    m = nc.tensor.transpose(pT[1][0:D, 128 * b:128 * b + 128], l2x[:, b, :], ident)
                m.then_inc(s_lxp, 1)

            def ffn_in(group):
                pe.wait_ge(s_lxt, at(group, 2, 2))
                mm(pT[0][:, :], wi[:, :], l2t[:, :]).then_inc(s_fp, 1)

            def ffn_layer(group, l):
                i, off = group
                pe.wait_ge(s_u, at(group, 3, l + 1))
                if l == 0:
                    pe.wait_ge(s_wr, at(group, 16 * NR, 16 * NR))
                p = pT[1 - l]
                mm(p[:, :], ws[:, l, :], u[l][:, :], True, False)
                hot = onehot[:, off * NR:off * NR + NR] if i is None else onehot[:, bass.ds(i * NR + off * NR, NR)]
                for n in range(NR):
                    w = slice(TOK * n, TOK * n + TOK)
                    nc.tensor.matmul(p[:, w], wr[:, n, l, :], u[l][:, w], start=False, stop=False,
                                     skip_group_check=True)
                nc.tensor.matmul(p[:, :], brt[:, l, :], hot.unsqueeze(2).to_broadcast([E, NR, TOK]),
                                 start=False, stop=True).then_inc(s_fp, 1)

            def ffn_out(group):
                pe.wait_ge(s_u, at(group, 3, 3))
                for b in range(GB):
                    m = mm(pT[1][:, D * b:D * b + D], u[2][:, 128 * b:128 * b + 128], wo[:, :])
                m.then_inc(s_fp, 1)

            def body(gf, gb, gc, gd):
                ng = gf and nxt(gf)
                before = gb and ((1, at(gb, 4, 3)), (1, at(gb, 4, 4)), (2, at(gb, 2, 1)))
                if gf: conv0(gf, 0, (0, 1, 2), before)
                if gf: quad_form(gf, 1)
                if gc: total(gc)
                if gd: e_transposes(gd)
                if gf: conv0(gf, 0, (3, 4, 5), None)
                if gc: cumsum(gc)
                if gd: attend(gd)
                if gf: conv0(gf, 0, (6, 7), None)
                if gc: shares(gc)
                if gd: attn_out(gd)
                if gf: var0(gf, 1)
                if gb: conv2(gb, 1, gf and (gf, 0))
                if gf: conv1(gf, 0, 0, range(0, 4))
                if gc: pool(gc)
                if gf: conv1(gf, 0, 0, range(4, 8))
                if gb: var(2, gb, 2)
                if gc: var(4, gc, 1, blocks=2)
                if gd: x2_transposes(gd)
                if gf: spread0(gf, 1)
                if gf: conv1(gf, 0, 1, range(0, 4))
                if gb: spread(2, gb, 2, pC[2])
                if gc: spread(4, gc, 1, pM[0], 2)
                if gd: ffn_in(gd)
                if gf: var(1, gf, 1, 0)
                if gf: conv1(gf, 0, 1, range(4, 8))
                if gf: spread(1, gf, 1, pC[0])
                if gd: ffn_layer(gd, 0)
                if gb: conv3(gb, gc)
                if gf: var(1, gf, 2, 1)
                if gd: ffn_layer(gd, 1)
                if gf: spread(1, gf, 2, pC[1])
                if gb: var(3, gb, 1)
                if gd: ffn_out(gd)

                before = gf and ((1, at(gf, 4, 1)), (1, at(gf, 4, 2)), gb and (2, at(gb, 2, 2)))
                if gf: conv0(gf, 1, (0, 1, 2), before)
                if gf: quad_form(ng, 0)
                if gc: x_transposes(gc)
                if gb: spread(3, gb, 1, pM[0])
                if gf: conv0(gf, 1, (3, 4, 5), None)
                if gc: qkv(gc, gd)
                if gb: f_transposes(gb)
                if gf: conv0(gf, 1, (6, 7), None)
                if gc: scores(gc)
                if gf: var0(ng, 0)
                if gf: conv2(gf, 0, (gf, 1))
                if gb: mlp1(gb, range(MC))
                if gf: conv1(gf, 1, 0, range(0, 8))
                if gf: var(2, gf, 1)
                if gf: spread0(ng, 0)
                if gb: mlp2(gb, (0,))
                if gf: conv1(gf, 1, 1, range(0, 4))
                if gf: spread(2, gf, 1, pC[2])
                if gf: var(1, gf, 3, 0)
                if gb: mlp2(gb, (1,))
                if gf: conv1(gf, 1, 1, range(4, 8))
                if gf: spread(1, gf, 3, pC[0])
                if gb: mlp2(gb, (2,))
                if gf: var(1, gf, 4, 1)
                if gb: mlp2(gb, (3,))
                if gf: spread(1, gf, 4, pC[1])
                if gb: mlp3(gb)

            pe.wait_ge(s_ready, 2)
            quad_form(PRE, 0)
            var0(PRE, 0)
            spread0(PRE, 0)
            body(PRE, None, None, None)
            body(FIRST, PRE, None, None)
            body((None, 2), FIRST, PRE, None)
            with pe.Fori(0, LOOPS) as i:
                body((i, 3), (i, 2), (i, 1), (i, 0))
            body(None, (None, NG - 1), (None, NG - 2), (None, NG - 3))
            body(None, None, (None, NG - 1), (None, NG - 2))
            body(None, None, None, (None, NG - 1))

        @block.scalar
        def _(sc):
            def do(out, in_, func, **k):
                return nc.scalar.activation(out, in_, func, **k)

            def x_high(group, k):
                sc.wait_ge(s_xs, at(group, 2, k + 1))
                do(xh[0:KQ, :], xs[0:KQ, :], ACT.Copy).then_inc(s_xh, 1)

            def relu0(group, k, js):
                for j in js:
                    sc.wait_ge(s_c0, at(group, 2 * PH, PH * k + j + 1))
                    do(h0[:, 0, j, :, 1:1 + NW], pC[j % 3][:, :].rearrange("p (b w) -> p b w", b=2), ACT.Relu)\
                        .then_inc(s_h0h, 1)

            def squares(n, group, idx, src, buf=0, cols=512):
                sc.wait_ge(s_pool if n == 4 else s_conv[n], at(group, PER[n], idx))
                nb = len(y[n])
                if n < 3 and not (group[0] is None and group[1] * PER[n] + idx <= nb):
                    sc.wait_ge(ns[n]["lo"], at(group, PER[n], idx - nb))
                bias = {} if n == 4 else {"bias": cen[:, TAPS0 + n:TAPS0 + n + 1]}
                do(y[n][buf][:, 0:cols], src, ACT.Identity, **bias).then_inc(ns[n]["y"], 1)
                do(sq[n][buf][:, 0:cols], src, ACT.Square, **bias).then_inc(ns[n]["sq"], 1)

            def relu(n, group, idx, cols=512):
                sc.wait_ge(ns[n]["z"], at(group, PER[n], idx))
                x = y[n][(idx - 1) % len(y[n])][:, 0:cols]
                do(x, x, ACT.Relu, bias=vec[:, OFFS + n:OFFS + n + 1],
                   scale=vec[:, GAIN + n:GAIN + n + 1]).then_inc(ns[n]["act"], 1)

            def gelu1(group, ms):
                for m in ms:
                    sc.wait_ge(s_m1, at(group, MC, m + 1))
                    if m >= 2:
                        sc.wait_ge(s_g1l, at(group, MC, m - 1))
                    do(g1[m % 2][:, :], pM[m % 2][:, :], ACT.Gelu, bias=vec[:, MB1 + m:MB1 + m + 1]).then_inc(s_g1, 1)

            def gelu2(group, ms):
                for m in ms:
                    sc.wait_ge(s_m2, at(group, MC, m + 1))
                    do(g2[:, m, :], pM[m % 2][:, :], ACT.Gelu, bias=vec[:, MB2 + m:MB2 + m + 1]).then_inc(s_g2, 1)

            def exp3(group):
                sc.wait_ge(s_m3, at(group, 1, 1))
                do(sig[:, 0, :], pM[0][:, 0:GB], ACT.Exp, bias=neg3[:, :], scale=-1.0).then_inc(s_exp3, 1)

            def x_rows(group, second):
                sc.wait_ge(s_lxp, at(group, 2, 1 + second))
                do((l2t if second else lxt)[0:D, :], pT[second][0:D, :], ACT.Copy).then_inc(s_lxt, 1)

            def qk(group):
                sc.wait_ge(s_qkvp, at(group, 3, 1))
                do(qT[:, :], pT[1][0:D, :], ACT.Copy).then_inc(s_qk, 1)
                sc.wait_ge(s_qkvp, at(group, 3, 2))
                do(kT[:, :], pT[0][0:D, :], ACT.Copy).then_inc(s_qk, 1)
                sc.wait_ge(s_qkvp, at(group, 3, 3))
                do(v[:, :, :], pT[1][:, 0:GB * D].rearrange("p (b d) -> p b d", b=GB), ACT.Copy).then_inc(s_v, 1)

            def copy_scores(group):
                sc.wait_ge(s_sp, at(group, 1, 1))
                do(s[:, :, :], pT[0][:, :].rearrange("p (b d) -> p b d", b=GB), ACT.Copy, scale=float(D) ** -0.5)\
                    .then_inc(s_s, 1)

            def exps(group):
                sc.wait_ge(s_sm, at(group, 1, 1))
                for b in range(GB):
                    x = do(e[:, b, :], s[:, b, :], ACT.Exp, bias=nmax[:, b:b + 1], accum_out=den[:, b:b + 1])
                x.then_inc(s_e, 1)

            def e_rows(group):
                sc.wait_ge(s_etp, at(group, 1, 1))
                do(eT[:, :, :], pT[0][:, :].rearrange("p (b d) -> p b d", b=GB), ACT.Copy).then_inc(s_et, 1)

            def o_rows(group):
                sc.wait_ge(s_op, at(group, 1, 1))
                do(oT[:, :], pT[1][0:D, :], ACT.Copy).then_inc(s_oT, 1)

            def ffn_relu(group, l):
                sc.wait_ge(s_fp, at(group, 4, l + 1))
                b = vec[:, BI:BI + 1] if l == 0 else vec[:, BS + l - 1:BS + l]
                do(u[l][:, :], pT[l % 2][:, :], ACT.Relu, bias=b).then_inc(s_u, 1)

            def body(gf, gb, gc, gd):
                ng = gf and nxt(gf)
                if gf: relu0(gf, 0, (0, 1, 2))
                if gd: e_rows(gd)
                if gf: relu0(gf, 0, (3, 4, 5))
                if gd: o_rows(gd)
                if gf: relu0(gf, 0, (6, 7))
                if gb: squares(2, gb, 2, pC[2][:, :])
                if gc: squares(4, gc, 1, pM[1][:, 0:GB * TN], cols=GB * TN)
                if gf: squares(1, gf, 1, pC[0][:, :], 0)
                if gd: x_rows(gd, 1)
                if gf: x_high(gf, 1)
                if gb: relu(2, gb, 2)
                if gc: relu(4, gc, 1, GB * TN)
                if gd: ffn_relu(gd, 0)
                if gf: squares(1, gf, 2, pC[1][:, :], 1)
                if gf: relu(1, gf, 1)
                if gd: ffn_relu(gd, 1)
                if gb: squares(3, gb, 1, pM[0][:, :])
                if gd: ffn_relu(gd, 2)
                if gf: relu(1, gf, 2)

                if gf: relu0(gf, 1, (0, 1, 2))
                if gc: x_rows(gc, 0)
                if gb: relu(3, gb, 1)
                if gf: relu0(gf, 1, (3, 4, 5))
                if gc: qk(gc)
                if gf: relu0(gf, 1, (6, 7))
                if gc: copy_scores(gc)
                if gf: squares(2, gf, 1, pC[2][:, :])
                if gb: gelu1(gb, range(MC))
                if gf: squares(1, gf, 3, pC[0][:, :], 0)
                if gf: x_high(ng, 0)
                if gb: gelu2(gb, (0,))
                if gf: relu(2, gf, 1)
                if gb: gelu2(gb, (1,))
                if gf: squares(1, gf, 4, pC[1][:, :], 1)
                if gf: relu(1, gf, 3)
                if gb: gelu2(gb, (2, 3))
                if gf: relu(1, gf, 4)
                if gc: exps(gc)
                if gb: exp3(gb)

            sc.wait_ge(s_ready, 2)
            x_high(PRE, 0)
            body(PRE, None, None, None)
            body(FIRST, PRE, None, None)
            body((None, 2), FIRST, PRE, None)
            with sc.Fori(0, LOOPS) as i:
                body((i, 3), (i, 2), (i, 1), (i, 0))
            body(None, (None, NG - 1), (None, NG - 2), (None, NG - 3))
            body(None, None, (None, NG - 1), (None, NG - 2))
            body(None, None, None, (None, NG - 1))

        @block.vector
        def _(ve):
            V = nc.vector
            count = [0]

            def step(ins):
                count[0] += 1
                ins.then_inc(s_dset, 1)
                ve.wait_ge(s_dset, count[0])

            ve.wait_ge(s_setup, 1)
            step(V.tensor_tensor(cen[:, :], vec[:, 0:CEN], pM[0][:, 0:CEN], ALU.subtract))
            step(V.tensor_copy(w0rep[:, :].rearrange("p (t j) -> p t j", j=PH),
                               cen[:, 0:TAPS0 + 1].unsqueeze(2).to_broadcast([128, TAPS0 + 1, PH])))
            step(V.tensor_scalar(w0gain[:, :], w0rep[:, :], vec[:, GAIN:GAIN + 1], None, ALU.mult))
            ve.wait_ge(s_setup, 2)
            step(V.tensor_tensor(gram[:, :], pF[0:KQ, 0:KQ], cst[0:KQ, SAME:SAME + KQ], ALU.mult))
            ve.wait_ge(s_setup, 3)
            step(V.tensor_copy(w0t[:, :], pC[0][0:KQ, 0:128]))
            for j in range(PH):
                ins = V.tensor_scalar(w0[0:KQ, j, :], w0t[:, :], cst[0:KQ, PHASE + j:PHASE + j + 1], None, ALU.mult)
            ins.then_inc(s_ready, 1)
            V.memset(xt[0][64:KQ, :], 1.0).then_inc(s_row, 1)
            V.memset(xt[1][64:KQ, :], 1.0).then_inc(s_row, 1)
            step(V.memset(xs[:, :], 1.0))
            step(V.tensor_copy(xh[:, :], xs[:, :]))
            step(V.memset(xs[:, :], 0.0))
            step(V.tensor_copy(xl[:, :], xs[:, :]))
            step(V.memset(lxt[D:D + 1, :], 1.0))
            step(V.tensor_scalar(neg3[:, :], vec[:, B3:B3 + 1], -1.0, None, ALU.mult))
            step(V.tensor_copy(route_f[:, :], route_i[:, :]))
            step(V.tensor_scalar(onehot[:, :], route_f[:, :], cst[0:E, ROWNO:ROWNO + 1], None, ALU.is_equal))
            step(V.tensor_scalar(route_in[:, :], route_f[0:1, :], 0.0, None, ALU.is_ge))
            step(V.tensor_scalar(route_c[:, :], route_f[0:1, :], float(E), None, ALU.is_lt))
            step(V.tensor_tensor(route_in[:, :], route_in[:, :], route_c[:, :], ALU.mult))
            step(V.tensor_scalar(route_c[:, :], route_f[0:1, :], 0.0, float(E), ALU.max, ALU.min))
            step(V.tensor_scalar(route_c[:, :], route_c[:, :], -float(E), None, ALU.add))
            step(V.tensor_tensor(route_c[:, :], route_c[:, :], route_in[:, :], ALU.mult))
            step(V.tensor_scalar(pick[:, :], route_c[:, :], float(E), None, ALU.add))
            for l in range(2):
                step(V.tensor_tensor(ws[:, l, :], ws[:, l, :], ident, ALU.add))
            step(V.tensor_reduce(wc_mean[:, :], wc_raw[:, :, :], AX, ALU.add))
            step(V.tensor_scalar(wc_mean[:, :], wc_mean[:, :], 1.0 / C, None, ALU.mult))
            step(V.tensor_tensor(wc_raw[:, :, :], wc_raw[:, :, :],
                                 wc_mean[:, :].unsqueeze(2).to_broadcast([128, 16, 128]), ALU.subtract))

            def split(hi, lo, x):
                step(V.tensor_copy(hi, x))
                step(V.tensor_tensor(lo, x, hi.bitcast(F32), ALU.subtract))

            split(wch[:, :, :], wcl[:, :, :], wc_raw[:, :, :])
            ve.wait_ge(s_mlpw, 32)
            split(m1h[:, :], m1l[:, :], m1raw[:, :])
            split(m2h[:, :, :], m2l[:, :, :], m2raw[:, :, :])
            ve.wait_ge(s_w0row, 16 * PH)
            split(w0h[:, :, :], w0l[:, :, :], w0[:, :, :])
            V.memset(lv[:, :], 1.0).then_inc(s_ready, 1)

            def quad_x(group, k):
                ve.wait_ge(s_quad, at(group, 2, k + 1))
                V.tensor_tensor(quad[:, :], pF[0:KQ, :], xt[k][:, :], ALU.mult).then_inc(s_quadx, 1)

            def eps_0(group, k):
                ve.wait_ge(s_var0, at(group, 2, k + 1))
                V.tensor_scalar(eps0[:, :], pF[:, 0:32], 1.0 / (C - 1), EPS, ALU.mult, ALU.add)\
                    .then_inc(s_eps0, 1)
                root0(group, k)

            STEPS = 10

            def root0(group, k):
                n = [k * STEPS]

                def link(ins):
                    n[0] += 1
                    ins.then_inc(s_rstd0, 1)
                    ve.wait_ge(s_rstd0, at(group, 2 * STEPS, n[0]))

                ve.wait_ge(s_eps0, at(group, 2, k + 1))
                link(V.tensor_scalar(rstd0[:, :].bitcast(I32), eps0[:, :].bitcast(I32), -0.5, float(0x5f3759df),
                                     ALU.mult, ALU.add))
                for _ in range(3):
                    link(V.tensor_tensor(newt[:, :], rstd0[:, :], rstd0[:, :], ALU.mult))
                    link(V.scalar_tensor_tensor(out=newt[:, :], in0=newt[:, :], scalar=-0.5, in1=eps0[:, :],
                                                op0=ALU.mult, op1=ALU.mult))
                    link(V.scalar_tensor_tensor(out=rstd0[:, :], in0=newt[:, :], scalar=1.5, in1=rstd0[:, :],
                                                op0=ALU.add, op1=ALU.mult))

            def spread_0(group, k):
                V.tensor_copy(rst0w[:, :, :].rearrange("p b (t j) -> p b t j", j=PH),
                              rstd0[:, :].rearrange("p (b j) -> p b j", j=PH).unsqueeze(2)
                              .to_broadcast([128, 4, TAPS0 + 1, PH])).then_inc(s_rst0w, 1)

            def scale_x(group, k):
                ve.wait_ge(s_rb0, at(group, 2, k + 1))
                V.tensor_tensor(xs[0:KQ, :], xt[k][:, :], pF[0:KQ, :], ALU.mult).then_inc(s_xs, 1)

            def low0(group, k, js):
                for j in js:
                    ve.wait_ge(s_h0h, at(group, 2 * PH, PH * k + j + 1))
                    V.scalar_tensor_tensor(out=h0[:, 1, j, :, 1:1 + NW],
                                           in0=pC[j % 3][:, :].rearrange("p (b w) -> p b w", b=2), scalar=0.0,
                                           in1=h0[:, 0, j, :, 1:1 + NW].bitcast(F32), op0=ALU.max,
                                           op1=ALU.subtract).then_inc(s_h0l, 1)

            def eps(n, group, idx, buf=0, blocks=4):
                ve.wait_ge(ns[n]["var"], at(group, PER[n], idx))
                V.tensor_scalar(vare[n][:, 0:blocks], var_bank[n][buf][:, 0:blocks], 1.0 / (C - 1), EPS, ALU.mult, ALU.add)\
                    .then_inc(ns[n]["eps"], 1)

            def norm(n, group, idx, bank, buf=0, cols=512):
                ve.wait_ge(ns[n]["rb"], at(group, PER[n], idx))
                V.tensor_tensor(y[n][buf][:, 0:cols], y[n][buf][:, 0:cols], bank[:, 0:cols], ALU.mult)\
                    .then_inc(ns[n]["z"], 1)

            def centre_f(group):
                ve.wait_ge(s_ft, at(group, 1, 1))
                p = pM[1][:, :].rearrange("p (b c) -> p b c", b=GB)
                V.tensor_reduce(fsum[:, :], p, AX, ALU.add).then_inc(s_fsum, 1)
                ve.wait_ge(s_fsum, at(group, 1, 1))
                V.tensor_scalar(fmean[:, :], fsum[:, :], 1.0 / C, None, ALU.mult).then_inc(s_fmean, 1)
                ve.wait_ge(s_fmean, at(group, 1, 1))
                V.tensor_tensor(ftc[:, :, :], p, fmean[:, :].unsqueeze(2).to_broadcast([128, GB, 128]),
                                ALU.subtract).then_inc(s_ftc, 1)

            def low1(group, ms):
                for m in ms:
                    ve.wait_ge(s_g1h, at(group, MC, m + 1))
                    V.tensor_tensor(g1l[:, m, :], g1[m % 2][:, :], g1h[:, m, :].bitcast(F32), ALU.subtract)\
                        .then_inc(s_g1l, 1)

            def chain(s_done, per):
                k = [0]

                def link(group, ins, wait=True):
                    k[0] += 1
                    ins.then_inc(s_done, 1)
                    if wait:
                        ve.wait_ge(s_done, at(group, per, k[0]))
                return link

            def sigmoid(group):
                ve.wait_ge(s_exp3, at(group, 1, 1))
                link = chain(s_chain["sigmoid"], 2)
                link(group, V.tensor_scalar(sig[:, 1, :], sig[:, 0, :], 1.0, None, ALU.add))
                link(group, V.reciprocal(sig[:, 2, :], sig[:, 1, :]))
                V.tensor_scalar(imp[:, :], sig[:, 2, :], TEMP, None, ALU.add).then_inc(s_sig, 1)

            def normalise(group):
                ve.wait_ge(s_tot, at(group, 1, 1))
                link = chain(s_chain["total"], 1)
                link(group, V.reciprocal(rtot[:, :], pM[1][:, 0:GB]))
                V.scalar_tensor_tensor(out=impn[:, :], in0=imp[:, :], scalar=float(TN), in1=rtot[:, :],
                                       op0=ALU.mult, op1=ALU.mult).then_inc(s_impn, 1)

            def overs(group):
                ve.wait_ge(s_cum, at(group, 1, 1))
                link = chain(s_chain["over"], 1 + GB)
                link(group, V.tensor_copy(cums[:, :], pM[1][:, 0:GB]))
                for b in range(GB):
                    link(group, V.tensor_scalar(over[:, b, :], cst[:, RAMP:RAMP + TN + 1], cums[:, b:b + 1], 0.0,
                                                ALU.add, ALU.max), b == GB - 1)
                V.tensor_tensor(diff[:, :, :], over[:, :, 0:TN], over[:, :, 1:TN + 1], ALU.subtract)\
                    .then_inc(s_over, 1)

            def copy_shares(group):
                ve.wait_ge(s_wm, at(group, 1, 1))
                V.tensor_copy(wmat[:, :, :], pM[0][:, 0:GB * TN].rearrange("p (b n) -> p b n", b=GB))\
                    .then_inc(s_wmat, 1)

            def ln_stats(group, src, which):
                link = chain(s_chain[f"ln{which}"], 2 * GB)
                for b in range(GB):
                    link(group, V.bn_stats(bn[:, b, :], src[:, b, :]), False)
                wait_apart(ve, s_chain[f"ln{which}"], at(group, 2 * GB, GB))
                for b in range(GB):
                    link(group, V.bn_aggr(mv[:, b, :], bn[:, b, :]), b == GB - 1)
                V.tensor_scalar(lv[:, :], mv[:, :, 1], EPS, None, ALU.add).then_inc(s_ln, 1)

            def ln_apply(group, src, dst, which):
                ve.wait_ge(s_lr, at(group, 2, which))
                for b in range(GB):
                    x = V.tensor_scalar(dst[:, b, :], src[:, b, :], mv[:, b, 0:1], lr[:, b:b + 1],
                                        ALU.subtract, ALU.mult)
                x.then_inc(s_lx, 1)

            h_rows = h[:, 0:GB * D].rearrange("p (b n) -> p b n", b=GB)

            def ln1_stats(group):
                ve.wait_ge(ns[4]["act"], at(group, 1, 1))
                ln_stats(group, h_rows, 1)

            def ln2_stats(group):
                ve.wait_ge(s_ha, at(group, 1, 1))
                ln_stats(group, ha[:, :, :], 2)

            NTOP = TOPK // 8

            def topk(group, rounds):
                for r in rounds:
                    if r == 0:
                        wait_apart(ve, s_s, at(group, 1, 1))
                    src = s if r == 0 else swork
                    for b in range(GB):
                        if r:
                            wait_apart(ve, s_top, at(group, TOPS, (2 * r - 1) * GB + b + 1))
                        V.max(top[:, b, :], src[:, b, :]).then_inc(s_top, 1)
                    if r < NTOP - 1:
                        for b in range(GB):
                            wait_apart(ve, s_top, at(group, TOPS, 2 * r * GB + b + 1))
                            V.match_replace(swork[:, b, :], top[:, b, :], src[:, b, :], NEG).then_inc(s_top, 1)
            TOPS = (2 * NTOP - 1) * GB

            def mask(group):
                ve.wait_ge(s_top, at(group, TOPS, TOPS))
                link = chain(s_chain["mask"], GB + 1)
                for b in range(GB):
                    link(group, V.scalar_tensor_tensor(out=s[:, b, :], in0=s[:, b, :], scalar=top[:, b, 7:8],
                                                       in1=s[:, b, :], op0=ALU.is_ge, op1=ALU.mult), b == GB - 1)
                link(group, V.tensor_reduce(smax[:, :], s[:, :, :], AX, ALU.max))
                V.tensor_scalar(nmax[:, :], smax[:, :], -1.0, None, ALU.mult).then_inc(s_sm, 1)

            def add_attn(group):
                ve.wait_ge(s_e, at(group, 1, 1))
                link = chain(s_chain["den"], 1)
                link(group, V.reciprocal(rden[:, :], den[:, :]), False)
                ve.wait_ge(s_hb, at(group, 1, 1))
                ve.wait_ge(s_wop, at(group, 1, 1))
                ve.wait_ge(s_chain["den"], at(group, 1, 1))
                for b in range(GB):
                    x = V.scalar_tensor_tensor(out=ha[:, b, :], in0=pT[0][:, D * b:D * b + D], scalar=rden[:, b:b + 1],
                                               in1=hb[:, b, :], op0=ALU.mult, op1=ALU.add)
                x.then_inc(s_ha, 1)

            def result(group):
                ve.wait_ge(s_hc, at(group, 1, 1))
                ve.wait_ge(s_fp, at(group, 4, 4))
                V.tensor_tensor(res[:, :, :], pT[1][:, 0:GB * D].rearrange("p (b d) -> p b d", b=GB), hc[:, :, :],
                                ALU.add).then_inc(s_res, 1)

            def body(gf, gb, gc, gd):
                ng = gf and nxt(gf)
                if gf: low0(gf, 0, (0, 1, 2))
                if gf: quad_x(gf, 1)
                if gc: normalise(gc)
                if gf: low0(gf, 0, (3, 4, 5))
                if gc: overs(gc)
                if gf: low0(gf, 0, (6, 7))
                if gc: copy_shares(gc)
                if gd: add_attn(gd)
                if gd: ln2_stats(gd)
                if gf: eps_0(gf, 1)
                if gf: spread_0(gf, 1)
                if gd: ln_apply(gd, ha, l2x, 2)
                if gb: eps(2, gb, 2)
                if gc: eps(4, gc, 1, blocks=2)
                if gf: scale_x(gf, 1)
                if gb: norm(2, gb, 2, pC[2])
                if gc: norm(4, gc, 1, pM[0], cols=GB * TN)
                if gf: eps(1, gf, 1, 0)
                if gc: ln1_stats(gc)
                if gf: norm(1, gf, 1, pC[0], 0)
                if gc: ln_apply(gc, h_rows, lx, 1)
                if gf: eps(1, gf, 2, 1)
                if gf: norm(1, gf, 2, pC[1], 1)
                if gb: eps(3, gb, 1)
                if gd: result(gd)

                if gf: low0(gf, 1, (0, 1, 2))
                if gf: quad_x(ng, 0)
                if gb: norm(3, gb, 1, pM[0])
                if gf: low0(gf, 1, (3, 4, 5))
                if gb: centre_f(gb)
                if gf: low0(gf, 1, (6, 7))
                if gf: eps_0(ng, 0)
                if gf: spread_0(ng, 0)
                if gc: topk(gc, range(0, 2))
                if gb: low1(gb, range(MC))
                if gc: topk(gc, range(2, 4))
                if gf: eps(2, gf, 1)
                if gf: scale_x(ng, 0)
                if gc: topk(gc, range(4, 5))
                if gf: norm(2, gf, 1, pC[2])
                if gf: eps(1, gf, 3, 0)
                if gc: topk(gc, range(5, 7))
                if gf: norm(1, gf, 3, pC[0], 0)
                if gf: eps(1, gf, 4, 1)
                if gc: topk(gc, range(7, 8))
                if gc: mask(gc)
                if gf: norm(1, gf, 4, pC[1], 1)
                if gb: sigmoid(gb)

            quad_x(PRE, 0)
            eps_0(PRE, 0)
            spread_0(PRE, 0)
            scale_x(PRE, 0)
            body(PRE, None, None, None)
            body(FIRST, PRE, None, None)
            body((None, 2), FIRST, PRE, None)
            with ve.Fori(0, LOOPS) as i:
                body((i, 3), (i, 2), (i, 1), (i, 0))
            body(None, (None, NG - 1), (None, NG - 2), (None, NG - 3))
            body(None, None, (None, NG - 1), (None, NG - 2))
            body(None, None, None, (None, NG - 1))

        @block.gpsimd
        def _(po):
            G = nc.gpsimd

            def root(out, in_):
                return G.tensor_tensor(out, in_, cst[:, HALF:HALF + in_.shape[1]], ALU.pow)

            def keep(out, in_):
                return G.tensor_scalar(out, in_, 1.0, 0.0, ALU.mult, ALU.add)

            def x_low(group, k):
                po.wait_ge(s_xh, at(group, 2, k + 1))
                G.tensor_tensor(xl[0:KQ, :], xs[0:KQ, :], xh[0:KQ, :].bitcast(F32), ALU.subtract).then_inc(s_xl, 1)

            def rootn(n, group, idx, blocks=4):
                po.wait_ge(ns[n]["eps"], at(group, PER[n], idx))
                root(rstd[n][:, 0:blocks], vare[n][:, 0:blocks]).then_inc(ns[n]["rstd"], 1)

            def pads0(group, k):
                wait_apart(po, s_h0l, at(group, 2 * PH, PH * k + PH))
                for dj, dw, sj, sw in ((6, 0, 2, 1), (7, 0, 1, 1), (0, NW + 1, 6, NW), (1, NW + 1, 5, NW)):
                    x = keep(h0[:, :, dj, :, dw:dw + 1], h0[:, :, sj, :, sw:sw + 1].bitcast(F32))
                x.then_inc(s_pad0, 1)

            def splitn(n, group, idx, hi, lo, src):
                wait_apart(po, ns[n]["act"], at(group, PER[n], idx))
                keep(hi, src).then_inc(ns[n]["hi"], 1)
                po.wait_ge(ns[n]["hi"], at(group, PER[n], idx))
                G.tensor_tensor(lo, src, hi.bitcast(F32), ALU.subtract).then_inc(ns[n]["lo"], 1)

            def split1(group, k, r):
                splitn(1, group, 2 * k + r + 1, h1[:, 0, r, :, 1:1 + T2], h1[:, 1, r, :, 1:1 + T2],
                       y[1][r][:, :].rearrange("p (b w) -> p b w", b=2))

            def pads1(group, k):
                wait_apart(po, ns[1]["lo"], at(group, 4, 2 * k + 2))
                for dr, dw, sr, sw in ((1, 0, 1, 1), (0, T2 + 1, 0, T2)):
                    x = keep(h1[:, :, dr, :, dw:dw + 1], h1[:, :, sr, :, sw:sw + 1].bitcast(F32))
                x.then_inc(s_pad1, 1)

            def split2(group, k):
                b = slice(2 * k, 2 * k + 2)
                splitn(2, group, k + 1, h2[:, 0, b, 1:1 + T2], h2[:, 1, b, 1:1 + T2],
                       y[2][0][:, :].rearrange("p (b w) -> p b w", b=2))
                wait_apart(po, ns[2]["lo"], at(group, 2, k + 1))
                for dw, sw in ((0, 2), (T2 + 1, T2 - 1)):
                    x = keep(h2[:, :, b, dw:dw + 1], h2[:, :, b, sw:sw + 1].bitcast(F32))
                x.then_inc(s_pad2, 1)

            def split3(group):
                splitn(3, group, 1, fh[:, :], fl[:, :], f[:, :])

            def high1(group, ms):
                for m in ms:
                    wait_apart(po, s_g1, at(group, MC, m + 1))
                    keep(g1h[:, m, :], g1[m % 2][:, :]).then_inc(s_g1h, 1)

            def add_bout(group, gd):
                po.wait_ge(ns[4]["act"], at(group, 1, 1))
                if gd:
                    po.wait_ge(s_ha, at(gd, 1, 1))
                G.tensor_tensor(hb[:, :, :], h[:, 0:GB * D].rearrange("p (b n) -> p b n", b=GB),
                                bout[:, :].unsqueeze(1).to_broadcast([128, GB, D]), ALU.add).then_inc(s_hb, 1)

            def add_bo(group):
                po.wait_ge(s_ha, at(group, 1, 1))
                G.tensor_tensor(hc[:, :, :], ha[:, :, :], bo[:, :].unsqueeze(1).to_broadcast([128, GB, D]),
                                ALU.add).then_inc(s_hc, 1)

            def ln_root(group, which):
                po.wait_ge(s_ln, at(group, 2, which))
                root(lr[:, :], lv[:, :]).then_inc(s_lr, 1)

            def body(gf, gb, gc, gd):
                ng = gf and nxt(gf)
                if gf: pads0(gf, 0)
                if gd: ln_root(gd, 2)
                if gb: rootn(2, gb, 2)
                if gc: rootn(4, gc, 1, 2)
                if gf: x_low(gf, 1)
                if gb: split2(gb, 1)
                if gf: rootn(1, gf, 1)
                if gc: ln_root(gc, 1)
                if gc: add_bout(gc, gd)
                if gd: add_bo(gd)
                if gf: split1(gf, 0, 0)
                if gf: rootn(1, gf, 2)
                if gf: split1(gf, 0, 1)
                if gf: pads1(gf, 0)
                if gb: rootn(3, gb, 1)

                if gb: split3(gb)
                if gf: pads0(gf, 1)
                if gb: high1(gb, range(MC))
                if gf: rootn(2, gf, 1)
                if gf: x_low(ng, 0)
                if gf: split2(gf, 0)
                if gf: rootn(1, gf, 3)
                if gf: split1(gf, 1, 0)
                if gf: rootn(1, gf, 4)
                if gf: split1(gf, 1, 1)
                if gf: pads1(gf, 1)

            po.wait_ge(s_ready, 2)
            x_low(PRE, 0)
            body(PRE, None, None, None)
            body(FIRST, PRE, None, None)
            body((None, 2), FIRST, PRE, None)
            with po.Fori(0, LOOPS) as i:
                body((i, 3), (i, 2), (i, 1), (i, 0))
            body(None, (None, NG - 1), (None, NG - 2), (None, NG - 3))
            body(None, None, (None, NG - 1), (None, NG - 2))
            body(None, None, None, (None, NG - 1))


def shape_constants():
    c = np.zeros((128, NCONST), np.float32)
    r = np.arange(128)
    c[:, IDENT:IDENT + 128] = np.eye(128)
    c[:, TRI:TRI + 128] = r[:, None] <= r[None, :]
    c[:, SHIFT:SHIFT + 128] = np.eye(128) - np.eye(128, k=1)
    c[:, MEANS:MEANS + 128] = 1.0 / C
    c[:, ONES:ONES + 128] = 1.0
    c[:, RAMP:RAMP + TN] = -np.arange(TN)
    c[:, RAMP + TN] = -1e30
    c[:, PHASE:PHASE + PH] = r[:, None] % PH == np.arange(PH)
    c[:, SAME:SAME + KQ] = r[:, None] % PH == np.arange(KQ)[None, :] % PH
    c[:, HALF:HALF + 32] = -0.5
    c[:, ROWNO] = r
    return c


def kernel(**inputs):
    import concourse.bacc as bacc
    from concourse.bass_utils import run_bass_kernel_spmd

    p = {k.replace("L0_", ""): np.asarray(x) for k, x in inputs.items()}
    x = np.pad(p["x"][:, 0, :], ((0, 0), (PAD0, PAD0)), mode="reflect")
    at_ = (STRIDE0 * PH * np.arange(NW)[None, None, :] + STRIDE0 * np.arange(PH)[None, :, None]
           + np.arange(TAPS0)[:, None, None])
    win = x[:, at_].reshape(B // 2, 2, KX, NW).transpose(0, 2, 1, 3).reshape(B // 2, KX, N)
    win = np.pad(win, ((0, 2), (0, 0), (0, 0)))
    col = lambda v: v.reshape(-1, 128).T
    vecs = np.concatenate(
        [p["tok_conv0_w"][:, 0, :]] + [p[f"tok_conv{n}_b"][:, None] for n in range(4)]
        + [p[f"tok_n{n}_w"][:, None] for n in range(5)] + [p[f"tok_n{n}_b"][:, None] for n in range(5)]
        + [col(p["tok_mlp_b1"]), col(p["tok_mlp_b2"]), col(p["tok_mlp_w3"]), col(p["ffn_bs"][0, 0]),
           col(p["ffn_bs"][1, 0]), col(p["ffn_bi"]), np.broadcast_to(p["tok_mlp_b3"][None, :], (128, 1))], axis=1)
    wconv = np.concatenate([p[f"tok_conv{n}_w"].transpose(1, 2, 0) for n in (1, 2, 3)], axis=1)
    arrays = {
        "consts": shape_constants(),
        "vecs": vecs,
        "wconv": wconv,
        "m1": p["tok_mlp_w1"],
        "m2": p["tok_mlp_w2"].reshape(MC, 128, DM).transpose(1, 0, 2),
        "off0": p["tok_n0_b"][None, :],
        "wqkv": np.concatenate([p["attn_W_qkv"], p["attn_b_qkv"][None, :]]),
        "wout": p["attn_W_out"],
        "bout": np.broadcast_to(p["attn_b_out"][None, :], (128, D)),
        "wi": p["ffn_Wi"].T,
        "ws": p["ffn_Ws"][:, 0].transpose(2, 0, 1),
        "brt": p["ffn_br"].transpose(1, 0, 2),
        "wo": p["ffn_Wo"].T,
        "bo": np.broadcast_to(p["ffn_bo"][None, :], (128, D)),
        "route": np.broadcast_to(p["ffn_route_id"][None, :], (E, B * RG)),
        "wr": np.pad(p["ffn_Wr"].transpose(1, 3, 0, 2), ((0, 1), (0, 0), (0, 0), (0, 0))),
        "x": win,
    }
    arrays = {k: np.ascontiguousarray(v) for k, v in arrays.items()}
    nc = bacc.Bacc("TRN2", target_bir_lowering=False, num_devices=1)
    a = {k: nc.dram_tensor(f"in_{k}", v.shape, mybir.dt.from_np(v.dtype), kind="ExternalInput").ap()
         for k, v in arrays.items()}
    a["out"] = nc.dram_tensor("out", (B, C, TN), F32, kind="ExternalOutput").ap()
    build(nc, a)
    r = run_bass_kernel_spmd(nc, [{f"in_{k}": v for k, v in arrays.items()}], core_ids=[0])
    return r.results[0]["out"]
```

```python
from contextlib import ExitStack

import numpy as np

import concourse.bass as bass
from concourse import mybir

F32 = mybir.dt.float32
F32R = mybir.dt.float32r
I32 = mybir.dt.int32
ALU = mybir.AluOpType
ACT = mybir.ActivationFunctionType
AX = mybir.AxisListType.X

B, L = 32, 10240
C = 128
GB = 4
NG = B // GB
T0, T1, T2, T3 = 2048, 512, 256, 128
PH = 8
NW = T0 // PH
TAPS0, STRIDE0, PAD0 = 10, 5, 3
KX = TAPS0 * PH
KQ = KX + PH
K0 = KQ + 1
N = 2 * NW
W1P = T1 // 2 + 2
W2P = T2 + 2
DM = 512
MC = DM // C
TN = T3 // 2
D = 64
TOPK = T3 // 2
RG = 2
NR = GB * RG
TOK = 64
E = 16
EPS, TEMP = 1e-5, 1e-5
NEG = -3.0e38

IDENT, TRI, SHIFT, MEANS, ONES = 0, 128, 256, 384, 512
RAMP = 640
PHASE = RAMP + TN + 1
SAME = PHASE + PH
HALF = SAME + KQ
ROWNO = HALF + 32
NCONST = ROWNO + 1
CEN = TAPS0 + 4
GAIN, OFFS = CEN, CEN + 5
MB1, MB2, MW3 = CEN + 10, CEN + 14, CEN + 18
BS, BI, B3 = CEN + 22, CEN + 24, CEN + 25
NVEC = CEN + 26


def at(group, per, k):
    i, off = group
    c = off * per + k
    return c if i is None else i * per + c


def build(nc, a):
    with ExitStack() as ctx:
        def sb(name, shape, dt=F32):
            return ctx.enter_context(nc.sbuf_tensor(name, shape, dt))

        def ps(name):
            return ctx.enter_context(nc.psum_tensor(name, [128, 512], F32))

        def sem(name):
            return ctx.enter_context(nc.semaphore(name))

        cst = sb("cst", [128, NCONST])
        vec = sb("vec", [128, NVEC])
        cen = sb("cen", [128, CEN])
        neg3 = sb("neg3", [128, 1])
        ident = cst[:, IDENT:IDENT + 128]
        w0rep = sb("w0rep", [128, KQ])
        w0gain = sb("w0gain", [128, K0])
        w0th, w0tl = sb("w0th", [K0, 128], F32R), sb("w0tl", [K0, 128], F32R)
        gram = sb("gram", [KQ, KQ])
        w0h, w0l = sb("w0h", [K0, PH, 128], F32R), sb("w0l", [K0, PH, 128], F32R)
        wc_mean = sb("wc_mean", [128, 16])
        wch, wcl = sb("wch", [128, 16, 128], F32R), sb("wcl", [128, 16, 128], F32R)
        m1h, m1l = sb("m1h", [128, DM], F32R), sb("m1l", [128, DM], F32R)
        m2h, m2l = sb("m2h", [128, MC, DM], F32R), sb("m2l", [128, MC, DM], F32R)
        wqkvt = sb("wqkvt", [D, 3, D + 1])
        wqk = sb("wqk", [D + 1, D + 1])
        wvo = sb("wvo", [D + 1, D])
        wout = sb("wout", [D, D])
        bout = sb("bout", [128, D])
        wi = sb("wi", [D, 128])
        ws = sb("ws", [128, 2, 128])
        brt = sb("brt", [E, 2, 128])
        brh, brl = sb("brh", [E, 2, 128], F32R), sb("brl", [E, 2, 128], F32R)
        wo = sb("wo", [128, D])
        bo = sb("bo", [128, D])
        route_i = sb("route_i", [E, B * RG], I32)
        route_f = sb("route_f", [E, B * RG])
        route_c = sb("route_c", [1, B * RG])
        route_in = sb("route_in", [1, B * RG])
        pick = sb("pick", [1, B * RG], I32)
        onehot = sb("onehot", [E, B * RG], F32R)

        xt = [sb(f"xt{k}", [KQ, N]) for k in range(2)]
        quad = sb("quad", [KQ, N])
        eps0, rstd0, newt = (sb(x, [128, 32]) for x in ("eps0", "rstd0", "newt"))
        rst0w = sb("rst0w", [128, 4, KQ])
        xs = sb("xs", [K0, N])
        xh, xl = sb("xh", [K0, N], F32R), sb("xl", [K0, N], F32R)
        h0 = sb("h0", [128, 2, PH, 2, NW + 2], F32R)
        h1 = sb("h1", [128, 2, 2, 2, W1P], F32R)
        h2 = sb("h2", [128, 2, GB, W2P], F32R)
        KINDS = (1, 2, 3, 4)
        WIDE = {1: 512, 2: 512, 3: 512, 4: GB * TN}
        y = {n: [sb(f"y{n}_{r}", [128, WIDE[n]]) for r in range(2 if n == 1 else 1)] for n in KINDS}
        sq = {n: [sb(f"sq{n}_{r}", [128, WIDE[n]]) for r in range(2 if n == 1 else 1)] for n in KINDS}
        vare = {n: sb(f"vare{n}", [128, 4]) for n in KINDS}
        rstd = {n: sb(f"rstd{n}", [128, 4]) for n in KINDS}
        f = y[3][0]
        fh, fl = sb("fh", [128, 512], F32R), sb("fl", [128, 512], F32R)
        fsum = sb("fsum", [128, GB])
        fmean = sb("fmean", [128, GB])
        ftc = sb("ftc", [128, GB, 128])
        g1 = [sb(f"g1_{m}", [128, 512]) for m in range(2)]
        g1h, g1l = sb("g1h", [128, MC, 512], F32R), sb("g1l", [128, MC, 512], F32R)
        g2 = sb("g2", [128, MC, 512])
        g2sum = sb("g2sum", [128, 512])
        sig = sb("sig", [128, 3, GB])
        imp = sb("imp", [128, GB])
        rtot = sb("rtot", [128, GB])
        impn = sb("impn", [128, GB])
        cums = sb("cums", [128, GB])
        over = sb("over", [128, GB, TN + 1])
        diff = sb("diff", [128, GB, TN])
        wmat = sb("wmat", [128, GB, TN])
        h = y[4][0]
        bn = sb("bn", [128, GB, 6])
        mv = sb("mv", [128, GB, 2])
        lv = sb("lv", [128, GB])
        lr = sb("lr", [128, GB])
        lx = sb("lx", [128, GB, D])
        lxt = sb("lxt", [D + 1, 512])
        hb = sb("hb", [128, GB, D])
        qT = sb("qT", [D + 1, 512])
        v = sb("v", [128, GB, D])
        s = sb("s", [128, GB, 128])
        swork = sb("swork", [128, GB, 128])
        top = sb("top", [128, GB, 8])
        smax = sb("smax", [128, GB])
        nmax = sb("nmax", [128, GB])
        e = swork
        den = sb("den", [128, GB])
        rden = sb("rden", [128, GB])
        eT = s
        ha = sb("ha", [128, GB, D])
        hc = sb("hc", [128, GB, D])
        l2x = sb("l2x", [128, GB, D])
        l2t = lxt[0:D, :]
        ub = sb("ub", [128, 3, 512])
        u = [ub[:, n, :] for n in range(3)]
        wr = sb("wr", [128, NR, 2, 128])
        res = sb("res", [128, GB, D])
        wc_raw = g2[:, :, :].rearrange("p m (t c) -> p (m t) c", c=128)
        m1raw = g1[0]
        m2raw = wr[:, :, :, :].rearrange("p (k n) l c -> p k (n l c)", k=MC)

        pF, pC = ps("pF"), [ps(f"pC{n}") for n in range(3)]
        pM = [ps("pM0"), ps("pM1")]
        pT = [ps("pT0"), ps("pT1")]
        var_bank = {1: pC, 2: [pC[2]], 3: [pM[0]], 4: [pM[1]]}
        late3, lateT = pC[1], (pC[0], pC[1])

        s_const, s_wcload, s_small = sem("const_loaded"), sem("conv_weights_loaded"), sem("small_weights_loaded")
        s_mlpw, s_setup, s_dset = sem("mlp_weights_loaded"), sem("setup_pe"), sem("setup_dve")
        s_rows, s_ready = sem("ones_rows_set"), sem("buffers_set")
        s_w0l, s_wcc, s_wch, s_wcl = (sem(x) for x in ("w0_low", "conv_weights_centred", "conv_weights_high", "conv_weights_low"))
        s_rest = sem("later_weights_ready")
        s_raw, s_sum, s_kept = sem("raw_experts_loaded"), sem("shared_added"), sem("summed_experts_stored")
        s_x = [sem(f"x_loaded{k}") for k in range(2)]
        s_quad, s_quadx, s_var0, s_eps0 = sem("quad"), sem("quad_times_x"), sem("var0"), sem("eps0")
        s_rstd0, s_rst0w, s_rb0 = sem("rstd0"), sem("rstd0_spread"), sem("rstd0_on_rows")
        s_xs, s_xh, s_xl = sem("x_scaled"), sem("x_high"), sem("x_low")
        s_c0, s_h0h, s_h0l, s_pad0 = sem("conv0"), sem("h0_high"), sem("h0_low"), sem("h0_pads")
        s_c1, s_c2, s_c3 = sem("conv1"), sem("conv2"), sem("conv3")
        s_conv = {1: s_c1, 2: s_c2, 3: s_c3}
        s_pad1, s_pad2 = sem("h1_pads"), sem("h2_pads")
        ns = {n: {x: sem(f"n{n}_{x}") for x in ("y", "sq", "var", "eps", "rstd", "rb", "z", "act", "hi", "lo")}
              for n in KINDS}
        PER = {1: 4, 2: 2, 3: 1, 4: 1}
        s_ft, s_fsum, s_fmean, s_ftc = sem("fT"), sem("f_sum"), sem("f_mean"), sem("fT_centred")
        s_m1, s_g1, s_g1h, s_g1l = sem("mlp1"), sem("gelu1"), sem("gelu1_high"), sem("gelu1_low")
        s_m2, s_g2, s_g2sum, s_m3, s_exp3, s_sig = sem("mlp2"), sem("gelu2"), sem("gelu2_summed"), sem("mlp3"), sem("exp3"), sem("sigmoid")
        s_tot, s_impn, s_cum, s_over, s_wm = sem("total"), sem("imp_normed"), sem("cumsum"), sem("over"), sem("wmat_product")
        s_wmat, s_pool, s_hb = sem("wmat"), sem("pooled"), sem("h_plus_bout")
        s_ln, s_lr, s_lx, s_lxp, s_lxt = ({n: sem(f"ln{n}_{x}") for n in (1, 2)}
                                          for x in ("stats", "rstd", "x", "xT_product", "xT"))
        s_qkvp, s_q, s_v, s_sp, s_s = (sem(x) for x in ("qkv_product", "queries", "v", "score_product", "scores"))
        s_top, s_sm, s_e, s_etp, s_et = (sem(x) for x in ("topk", "masked", "exp", "expT_product", "expT"))
        s_op, s_ha = sem("attn_product"), sem("attn_added")
        s_hc = sem("ha_plus_bo")
        s_fp, s_u, s_res, s_out, s_wr = (sem(x) for x in ("ffn_product", "ffn_relu", "result", "stored", "experts_loaded"))

        s_chain = {x: sem(f"chain_{x}") for x in ("sigmoid", "total", "over", "ln1", "ln2", "mask", "den")}

        SMALL = [(wqkvt[:, :, :], a["wqkvt"]), (wout[:, :], a["wout"]), (bout[:, :], a["bout"]),
                 (wi[:, :], a["wi"]), (ws[:, :, :], a["ws"]), (brt[:, :, :], a["brt"]), (wo[:, :], a["wo"]),
                 (bo[:, :], a["bo"]), (route_i[:, :], a["route"])]
        CT1 = 8
        block = ctx.enter_context(nc.Block())

        def wait_apart(engine, semaphore, value):
            if not isinstance(value, int):
                value = engine.to_reg(value)
            engine.wait_ge(s_ready, 1)
            engine.wait_ge(semaphore, value)

        PRE, FIRST = (None, 0), (None, 1)
        LOOPS = NG - 3

        def nxt(group):
            return group[0], group[1] + 1

        @block.sync
        def _(sp):
            sp.dma_start(vec[:, :], a["vecs"]).then_inc(s_const, 16)
            sp.dma_start(cst[:, :], a["consts"]).then_inc(s_const, 16)
            sp.wait_ge(s_rows, 2)

            def load_x(group, k, first=False):
                i, off = group
                if not first:
                    sp.wait_ge(s_xs, at(group, 2, k + 1 - 2))
                n = off * 2 + k if i is None else i * 2 + (off * 2 + k)
                src = a["x"][n, :, :] if i is None else a["x"][bass.ds(n, 1), :, :].rearrange("a r n -> (a r) n")
                sp.dma_start(xt[k][0:KX, :], src).then_inc(s_x[k], 16)

            def load_experts(group):
                i, off = group
                for n in range(NR):
                    c = off * NR + n if i is None else i * NR + (off * NR + n)
                    src = pick[0:1, c:c + 1] if i is None else pick[0:1, bass.ds(c, 1)]
                    x = sp.value_load(src, min_val=0, max_val=E)
                    sp.dma_start(wr[:, n, :, :], a["sums"][bass.ds(x, 1), :, :, :].rearrange("e p l o -> (e p) l o"))\
                      .then_inc(s_wr, 16)

            def store(group):
                i, off = group
                sp.wait_ge(s_res, at(group, 1, 1))
                src = res[:, :, :]
                n = off * GB if i is None else i * GB + off * GB
                o = a["out"][bass.ds(n, GB), :, :] if i is not None else a["out"][n:n + GB, :, :]
                sp.dma_start(o.rearrange("b c n -> c b n"), src).then_inc(s_out, 16)
                sp.wait_ge(s_out, at(group, 16, 16))

            load_x(PRE, 0, True)
            sp.dma_start(wc_raw[:, :, :], a["wconv"]).then_inc(s_wcload, 16)
            load_x(PRE, 1, True)
            for dst, src in SMALL:
                sp.dma_start(dst, src).then_inc(s_small, 16)
            sp.dma_start(m1raw[:, :], a["m1"]).then_inc(s_mlpw, 16)
            sp.dma_start(m2raw[:, :, :], a["m2"]).then_inc(s_mlpw, 16)

            def body(gf, gb, gc, gd):
                if gf:
                    load_x(nxt(gf), 0)
                    load_x(nxt(gf), 1)
                if gd:
                    store(gd)
                if gc:
                    load_experts(gc)

            body(PRE, None, None, None)
            sp.wait_ge(s_rest, 3)

            def move(n, load):
                half = a["wr" if load else "sums"][NR * n:NR * n + NR, :, :, :].rearrange("e p l o -> p e l o")
                if load:
                    sp.dma_start(wr[:, :, :, :], half).then_inc(s_raw, 16)
                else:
                    sp.wait_ge(s_sum, n + 1)
                    sp.dma_start(half, wr[:, :, :, :]).then_inc(s_kept, 16)

            move(0, True)
            move(0, False)
            sp.wait_ge(s_kept, 16)
            move(1, True)
            body(FIRST, PRE, None, None)
            move(1, False)
            sp.dma_start(a["sums"][E, :, :, :], ws[:, :, :]).then_inc(s_kept, 16)
            sp.wait_ge(s_kept, 16 * 3)
            body((None, 2), FIRST, PRE, None)
            with sp.Fori(0, LOOPS) as i:
                body((i, 3), (i, 2), (i, 1), (i, 0))
            body(None, (None, NG - 1), (None, NG - 2), (None, NG - 3))
            body(None, None, (None, NG - 1), (None, NG - 2))
            body(None, None, None, (None, NG - 1))
            sp.wait_ge(s_x[1], 16 * (NG + 1))
            sp.wait_ge(s_out, 16 * NG)

        @block.tensor
        def _(pe):
            def mm(out, lhs, rhs, start=True, stop=True):
                return nc.tensor.matmul(out, lhs, rhs, start=start, stop=stop)

            pe.wait_ge(s_const, 32)
            mm(pM[0][:, 0:CEN], cst[:, MEANS:MEANS + 128], vec[:, 0:CEN]).then_inc(s_setup, 1)
            pe.wait_ge(s_dset, 3)
            mm(pF[0:KQ, 0:KQ], w0rep[:, :], w0rep[:, :]).then_inc(s_setup, 1)
            pe.wait_ge(s_dset, 4)
            nc.tensor.transpose(pC[0][0:K0, 0:128], w0gain[:, :], ident).then_inc(s_setup, 1)

            def fold_attention():
                pe.wait_ge(s_small, 16 * len(SMALL))
                mm(pT[0][0:D + 1, 0:D + 1], wqkvt[:, 0, :], wqkvt[:, 1, :])
                mm(pT[1][0:D + 1, 0:D], wqkvt[:, 2, :], wout[:, :]).then_inc(s_setup, 1)

            def quad_form(group, k):
                pe.wait_ge(s_x[k], at(group, 16, 16))
                if not (group is PRE and k == 0):
                    pe.wait_ge(s_xs, at(group, 2, k))
                mm(pF[0:KQ, :], gram[:, :], xt[k][:, :]).then_inc(s_quad, 1)

            def var0(group, k):
                pe.wait_ge(s_quadx, at(group, 2, k + 1))
                for b in range(4):
                    m = mm(pF[:, PH * b:PH * b + PH], quad[:, 128 * b:128 * b + 128],
                           cst[0:KQ, PHASE:PHASE + PH])
                m.then_inc(s_var0, 1)

            def spread0(group, k):
                pe.wait_ge(s_rst0w, at(group, 2, k + 1))
                for b in range(4):
                    m = mm(pF[0:KQ, 128 * b:128 * b + 128], rst0w[:, b, :], ident)
                m.then_inc(s_rb0, 1)

            def split3(out, wh, wl, xhi, xlo, first=True, last=True):
                mm(out, wh, xhi, first, False)
                mm(out, wh, xlo, False, False)
                return mm(out, wl, xhi, False, last)

            def conv0(group, k, js, before):
                if js[0] == 0:
                    pe.wait_ge(s_xh, at(group, 2, k + 1))
                    pe.wait_ge(s_xl, at(group, 2, k + 1))
                for j in js:
                    if j >= 3:
                        pe.wait_ge(s_h0l, at(group, 2 * PH, PH * k + j - 2))
                    elif before and before[j]:
                        n, value = before[j]
                        pe.wait_ge(ns[n]["z"], value)
                    split3(pC[j % 3][:, :], w0h[:, j, :], w0l[:, j, :], xh[:, :], xl[:, :]).then_inc(s_c0, 1)

            def conv1(group, k, r, taps):
                if group is PRE and k == r == 0 and taps[0] == 0:
                    pe.wait_ge(s_wcl, 1)
                if r == 0 and taps[0] == 0:
                    pe.wait_ge(s_h0l, at(group, 2 * PH, PH * k + PH))
                    pe.wait_ge(s_pad0, at(group, 2, k + 1))
                for t in taps:
                    p = 4 * r - 2 + t
                    o = 1 + p // PH
                    m = split3(pC[r][:, :], wch[:, t, :], wcl[:, t, :], h0[:, 0, p % PH, :, o:o + NW],
                               h0[:, 1, p % PH, :, o:o + NW], t == 0, t == 7)
                if taps[-1] == 7:
                    m.then_inc(s_c1, 1)

            def conv2(group, k, front):
                if group is PRE and k == 0:
                    pe.wait_ge(s_wcl, 2)
                pe.wait_ge(ns[1]["lo"], at(group, 4, 2 * k + 2))
                pe.wait_ge(s_pad1, at(group, 2, k + 1))
                if front:
                    pe.wait_ge(s_h0l, at(front[0], 2 * PH, PH * front[1] + 6))
                for t in range(4):
                    r, o = (t + 1) % 2, (0 if t == 0 else 2 if t == 3 else 1)
                    m = split3(pC[2][:, :], wch[:, 8 + t, :], wcl[:, 8 + t, :], h1[:, 0, r, :, o:o + T2],
                               h1[:, 1, r, :, o:o + T2], t == 0, t == 3)
                m.then_inc(s_c2, 1)

            def var(n, group, idx, buf=0, blocks=4, bank=None):
                bank = bank or var_bank[n][buf]
                pe.wait_ge(ns[n]["sq"], at(group, PER[n], idx))
                for b in range(blocks):
                    m = mm(bank[:, b:b + 1], sq[n][buf][:, 128 * b:128 * b + 128], cst[:, ONES:ONES + 1])
                m.then_inc(ns[n]["var"], 1)

            def spread(n, group, idx, bank, blocks=4):
                pe.wait_ge(ns[n]["rstd"], at(group, PER[n], idx))
                for b in range(blocks):
                    m = mm(bank[:, 128 * b:128 * b + 128], rstd[n][:, b:b + 1].to_broadcast([128, 128]), ident)
                m.then_inc(ns[n]["rb"], 1)

            def conv3(group, gc, bank=pM[0]):
                pe.wait_ge(ns[2]["lo"], at(group, 2, 2))
                pe.wait_ge(s_pad2, at(group, 2, 2))
                if gc:
                    pe.wait_ge(ns[4]["z"], at(gc, 1, 1))
                for t in range(4):
                    m = split3(bank[:, :], wch[:, 12 + t, :], wcl[:, 12 + t, :], h2[:, 0, :, t:t + 2 * T3 - 1:2],
                               h2[:, 1, :, t:t + 2 * T3 - 1:2], t == 0, t == 3)
                m.then_inc(s_c3, 1)

            def f_transposes(group, gc=None):
                pe.wait_ge(ns[3]["act"], at(group, 1, 1))
                if gc:
                    pe.wait_ge(ns[4]["z"], at(gc, 1, 1))
                for b in range(GB):
                    m = nc.tensor.transpose(pM[1][:, 128 * b:128 * b + 128], f[:, 128 * b:128 * b + 128], ident)
                m.then_inc(s_ft, 1)

            def mlp1(group, ms):
                pe.wait_ge(ns[3]["lo"], at(group, 1, 1))
                for m_ in ms:
                    if m_ == 1:
                        pe.wait_ge(s_ftc, at(group, 1, 1))
                    if m_ >= 2:
                        pe.wait_ge(s_g1, at(group, MC, m_ - 1))
                    w = slice(128 * m_, 128 * m_ + 128)
                    split3(pM[m_ % 2][:, :], m1h[:, w], m1l[:, w], fh[:, :], fl[:, :]).then_inc(s_m1, 1)

            def mlp2(group, ms):
                for m_ in ms:
                    if m_ == 0:
                        pe.wait_ge(s_g1, at(group, MC, MC - 1))
                    if m_ >= 2:
                        pe.wait_ge(s_g2, at(group, MC, m_ - 1))
                    w = slice(128 * m_, 128 * m_ + 128)
                    for kc in range(MC):
                        if m_ == 0:
                            pe.wait_ge(s_g1l, at(group, MC, kc + 1))
                        m = split3(pM[m_ % 2][:, :], m2h[:, kc, w], m2l[:, kc, w], g1h[:, kc, :], g1l[:, kc, :],
                                   kc == 0, kc == MC - 1)
                    m.then_inc(s_m2, 1)

            def mlp3(group):
                pe.wait_ge(s_g2sum, at(group, MC, MC))
                for b in range(GB):
                    m = mm(pM[0][:, b:b + 1], g2sum[:, 128 * b:128 * b + 128], cst[:, ONES:ONES + 1])
                m.then_inc(s_m3, 1)

            def total(group):
                pe.wait_ge(s_sig, at(group, 1, 1))
                mm(pM[1][:, 0:GB], cst[:, ONES:ONES + 128], imp[:, :]).then_inc(s_tot, 1)

            def cumsum(group):
                pe.wait_ge(s_impn, at(group, 1, 1))
                mm(pM[1][:, 0:GB], cst[:, TRI:TRI + 128], impn[:, :]).then_inc(s_cum, 1)

            def shares(group):
                pe.wait_ge(s_over, at(group, 1, 1))
                mm(pM[0][:, 0:GB * TN], cst[:, SHIFT:SHIFT + 128], diff[:, :, :]).then_inc(s_wm, 1)

            def pool(group):
                pe.wait_ge(s_wmat, at(group, 1, 1))
                for b in range(GB):
                    m = mm(pM[1][:, TN * b:TN * b + TN], ftc[:, b, :], wmat[:, b, :])
                m.then_inc(s_pool, 1)

            def x_transposes(group, banks=pT):
                wait_apart(pe, s_lx[1], at(group, 1, 1))
                for b in range(GB):
                    m = nc.tensor.transpose(banks[0][0:D, 128 * b:128 * b + 128], lx[:, b, :], ident)
                m.then_inc(s_lxp[1], 1)

            def qkv(group, gd, banks=pT):
                pe.wait_ge(s_lxt[1], at(group, 1, 1))
                if gd:
                    pe.wait_ge(s_res, at(gd, 1, 1))
                mm(banks[1][0:D + 1, :], wqk[:, :], lxt[:, :]).then_inc(s_qkvp, 1)
                for b in range(GB):
                    m = mm(banks[0][:, D * b:D * b + D], lxt[:, 128 * b:128 * b + 128], wvo[:, :])
                m.then_inc(s_qkvp, 1)

            def scores(group, banks=pT):
                pe.wait_ge(s_q, at(group, 1, 1))
                for b in range(GB):
                    w = slice(128 * b, 128 * b + 128)
                    m = mm(banks[1][:, w], qT[:, w], lxt[:, w])
                m.then_inc(s_sp, 1)

            def e_transposes(group):
                pe.wait_ge(s_e, at(group, 1, 1))
                for b in range(GB):
                    m = nc.tensor.transpose(pT[0][:, 128 * b:128 * b + 128], e[:, b, :], ident)
                m.then_inc(s_etp, 1)

            def attend(group):
                pe.wait_ge(s_et, at(group, 1, 1))
                for b in range(GB):
                    m = mm(pT[0][:, D * b:D * b + D], eT[:, b, :], v[:, b, :])
                m.then_inc(s_op, 1)

            def x2_transposes(group):
                wait_apart(pe, s_lx[2], at(group, 1, 1))
                for b in range(GB):
                    m = nc.tensor.transpose(pT[1][0:D, 128 * b:128 * b + 128], l2x[:, b, :], ident)
                m.then_inc(s_lxp[2], 1)

            def ffn_in(group):
                pe.wait_ge(s_lxt[2], at(group, 1, 1))
                mm(pT[0][:, :], wi[:, :], l2t[:, :]).then_inc(s_fp, 1)

            def ffn_layer(group, l):
                i, off = group
                if l == 0:
                    pe.wait_ge(s_wr, at(group, 16 * NR, 16 * NR))
                wait_apart(pe, s_u, at(group, 3, l + 1))
                p = pT[1 - l]
                hot = onehot[:, off * NR:off * NR + NR] if i is None else onehot[:, bass.ds(i * NR + off * NR, NR)]
                hot = hot.unsqueeze(2).to_broadcast([E, NR, TOK])
                mm(p[:, :], brl[:, l, :], hot, True, False)
                for n in range(NR):
                    w = slice(TOK * n, TOK * n + TOK)
                    nc.tensor.matmul(p[:, w], wr[:, n, l, :], u[l][:, w], start=False, stop=False,
                                     skip_group_check=True)
                mm(p[:, :], brh[:, l, :], hot, False, True).then_inc(s_fp, 1)

            def ffn_out(group):
                pe.wait_ge(s_u, at(group, 3, 3))
                for b in range(GB):
                    m = mm(pT[1][:, D * b:D * b + D], u[2][:, 128 * b:128 * b + 128], wo[:, :])
                m.then_inc(s_fp, 1)

            def middle_last(gb, gc, gd):
                conv2(gb, 1, None)
                mlp3(gc)
                e_transposes(gd)
                total(gc)
                var(2, gb, 2)
                attend(gd)
                cumsum(gc)
                spread(2, gb, 2, pC[2])
                shares(gc)
                pool(gc)
                conv3(gb, None, late3)
                x2_transposes(gd)
                var(4, gc, 1, blocks=2)
                ffn_in(gd)
                var(3, gb, 1, bank=late3)
                spread(4, gc, 1, pM[0], 2)
                spread(3, gb, 1, late3)
                ffn_layer(gd, 0)
                f_transposes(gb, gc)
                mlp1(gb, (0, 1))
                ffn_layer(gd, 1)
                mlp1(gb, (2, 3))
                ffn_out(gd)
                x_transposes(gc)
                qkv(gc, gd)
                mlp2(gb, (0,))
                scores(gc)
                mlp2(gb, (1, 2, 3))

            def tail_last(gc, gd):
                mlp3(gc)
                total(gc)
                cumsum(gc)
                shares(gc)
                pool(gc)
                var(4, gc, 1, blocks=2)
                spread(4, gc, 1, pM[0], 2)
                e_transposes(gd)
                x_transposes(gc, lateT)
                attend(gd)
                qkv(gc, None, lateT)
                scores(gc, lateT)
                x2_transposes(gd)
                ffn_in(gd)
                ffn_layer(gd, 0)
                ffn_layer(gd, 1)
                ffn_out(gd)

            def body(gf, gb, gc, gd):
                ng = gf and nxt(gf)
                before = gb and ((1, at(gb, 4, 3)), (1, at(gb, 4, 4)), (2, at(gb, 2, 1)))
                if gf: conv0(gf, 0, (0,), before)
                if gf: conv0(gf, 0, (1, 2), before)
                if gf: quad_form(gf, 1)
                if gf is PRE: fold_attention()
                if gc: mlp3(gc)
                if gf: conv0(gf, 0, (3, 4, 5), None)
                if gc: total(gc)
                if gd: e_transposes(gd)
                if gf: conv0(gf, 0, (6, 7), None)
                if gf: var0(gf, 1)
                if gc: cumsum(gc)
                if gd: attend(gd)
                if gb: conv2(gb, 1, gf and (gf, 0))
                if gc: shares(gc)
                if gf: conv1(gf, 0, 0, range(0, 4))
                if gb: var(2, gb, 2)
                if gf: conv1(gf, 0, 0, range(4, 8))
                if gd: x2_transposes(gd)
                if gc: pool(gc)
                if gf: spread0(gf, 1)
                if gb: spread(2, gb, 2, pC[2])
                if gc: var(4, gc, 1, blocks=2)
                if gf: conv1(gf, 0, 1, range(0, 4))
                if gd: ffn_in(gd)
                if gf: var(1, gf, 1, 0)
                if gf: conv1(gf, 0, 1, range(4, 8))
                if gc: spread(4, gc, 1, pM[0], 2)
                if gf: spread(1, gf, 1, pC[0])
                if gd: ffn_layer(gd, 0)
                if gb: conv3(gb, gc)
                if gf: var(1, gf, 2, 1)
                if gd: ffn_layer(gd, 1)
                if gf: spread(1, gf, 2, pC[1])
                if gb: var(3, gb, 1)
                if gd: ffn_out(gd)

                before = gf and ((1, at(gf, 4, 1)), (1, at(gf, 4, 2)), gb and (2, at(gb, 2, 2)))
                if gf: conv0(gf, 1, (0, 1, 2), before)
                if gf: quad_form(ng, 0)
                if gc: x_transposes(gc)
                if gf: conv0(gf, 1, (3,), None)
                if gb: spread(3, gb, 1, pM[0])
                if gf: conv0(gf, 1, (4, 5), None)
                if gc: qkv(gc, gd)
                if gb: f_transposes(gb)
                if gf: conv0(gf, 1, (6, 7), None)
                if gc: scores(gc)
                if gf: var0(ng, 0)
                if gf: conv2(gf, 0, (gf, 1))
                if gb: mlp1(gb, (0, 1))
                if gf: conv1(gf, 1, 0, range(0, 4))
                if gb: mlp1(gb, (2, 3))
                if gf: conv1(gf, 1, 0, range(4, 8))
                if gf: var(2, gf, 1)
                if gf: spread0(ng, 0)
                if gb: mlp2(gb, (0,))
                if gf: conv1(gf, 1, 1, range(0, 4))
                if gf: spread(2, gf, 1, pC[2])
                if gf: var(1, gf, 3, 0)
                if gb: mlp2(gb, (1,))
                if gf: conv1(gf, 1, 1, range(4, 8))
                if gb: mlp2(gb, (2,))
                if gf: spread(1, gf, 3, pC[0])
                if gf: var(1, gf, 4, 1)
                if gb: mlp2(gb, (3,))
                if gf: spread(1, gf, 4, pC[1])

            pe.wait_ge(s_dset, 5)
            quad_form(PRE, 0)
            var0(PRE, 0)
            spread0(PRE, 0)
            pe.wait_ge(s_dset, 8)
            pe.wait_ge(s_w0l, 1)
            body(PRE, None, None, None)
            pe.wait_ge(s_rest, 3)
            body(FIRST, PRE, None, None)
            body((None, 2), FIRST, PRE, None)
            with pe.Fori(0, LOOPS) as i:
                body((i, 3), (i, 2), (i, 1), (i, 0))
            middle_last((None, NG - 1), (None, NG - 2), (None, NG - 3))
            tail_last((None, NG - 1), (None, NG - 2))
            body(None, None, None, (None, NG - 1))

        @block.scalar
        def _(sc):
            def do(out, in_, func, **k):
                return nc.scalar.activation(out, in_, func, **k)

            def x_high(group, k):
                sc.wait_ge(s_xs, at(group, 2, k + 1))
                do(xh[0:KQ, :], xs[0:KQ, :], ACT.Copy).then_inc(s_xh, 1)

            def relu0(group, k, js):
                for j in js:
                    sc.wait_ge(s_c0, at(group, 2 * PH, PH * k + j + 1))
                    do(h0[:, 0, j, :, 1:1 + NW], pC[j % 3][:, :].rearrange("p (b w) -> p b w", b=2), ACT.Relu)\
                        .then_inc(s_h0h, 1)

            def squares(n, group, idx, src, buf=0, cols=512):
                sc.wait_ge(s_pool if n == 4 else s_conv[n], at(group, PER[n], idx))
                nb = len(y[n])
                if n < 3 and not (group[0] is None and group[1] * PER[n] + idx <= nb):
                    sc.wait_ge(ns[n]["lo"], at(group, PER[n], idx - nb))
                bias = {} if n == 4 else {"bias": cen[:, TAPS0 + n:TAPS0 + n + 1]}
                do(y[n][buf][:, 0:cols], src, ACT.Identity, **bias).then_inc(ns[n]["y"], 1)
                do(sq[n][buf][:, 0:cols], src, ACT.Square, **bias).then_inc(ns[n]["sq"], 1)

            def relu(n, group, idx, cols=512):
                sc.wait_ge(ns[n]["z"], at(group, PER[n], idx))
                x = y[n][(idx - 1) % len(y[n])][:, 0:cols]
                do(x, x, ACT.Relu, bias=vec[:, OFFS + n:OFFS + n + 1],
                   scale=vec[:, GAIN + n:GAIN + n + 1]).then_inc(ns[n]["act"], 1)

            def gelu1(group, ms):
                for m in ms:
                    sc.wait_ge(s_m1, at(group, MC, m + 1))
                    if m >= 2:
                        sc.wait_ge(s_g1l, at(group, MC, m - 1))
                    do(g1[m % 2][:, :], pM[m % 2][:, :], ACT.Gelu, bias=vec[:, MB1 + m:MB1 + m + 1]).then_inc(s_g1, 1)

            def gelu2(group, ms):
                for m in ms:
                    sc.wait_ge(s_m2, at(group, MC, m + 1))
                    do(g2[:, m, :], pM[m % 2][:, :], ACT.Gelu, bias=vec[:, MB2 + m:MB2 + m + 1]).then_inc(s_g2, 1)

            def exp3(group):
                sc.wait_ge(s_m3, at(group, 1, 1))
                do(sig[:, 0, :], pM[0][:, 0:GB], ACT.Exp, bias=neg3[:, :], scale=-1.0).then_inc(s_exp3, 1)

            def x_rows(group, second, banks=pT):
                sc.wait_ge(s_lxp[1 + second], at(group, 1, 1))
                do((l2t if second else lxt)[0:D, :], banks[second][0:D, :], ACT.Copy).then_inc(s_lxt[1 + second], 1)

            def q_rows(group, banks=pT):
                sc.wait_ge(s_qkvp, at(group, 2, 1))
                do(qT[:, :], banks[1][0:D + 1, :], ACT.Copy).then_inc(s_q, 1)

            def v_rows(group, banks=pT):
                sc.wait_ge(s_qkvp, at(group, 2, 2))
                do(v[:, :, :], banks[0][:, 0:GB * D].rearrange("p (b d) -> p b d", b=GB), ACT.Copy).then_inc(s_v, 1)

            def copy_scores(group, banks=pT):
                sc.wait_ge(s_sp, at(group, 1, 1))
                do(s[:, :, :], banks[1][:, :].rearrange("p (b d) -> p b d", b=GB), ACT.Copy, scale=float(D) ** -0.5)\
                    .then_inc(s_s, 1)

            def exps(group):
                sc.wait_ge(s_sm, at(group, 1, 1))
                for b in range(GB):
                    x = do(e[:, b, :], s[:, b, :], ACT.Exp, bias=nmax[:, b:b + 1], accum_out=den[:, b:b + 1])
                x.then_inc(s_e, 1)

            def e_rows(group):
                sc.wait_ge(s_etp, at(group, 1, 1))
                do(eT[:, :, :], pT[0][:, :].rearrange("p (b d) -> p b d", b=GB), ACT.Copy).then_inc(s_et, 1)

            def ffn_relu(group, l):
                sc.wait_ge(s_fp, at(group, 4, l + 1))
                b = vec[:, BI:BI + 1] if l == 0 else vec[:, BS + l - 1:BS + l]
                do(u[l][:, :], pT[l % 2][:, :], ACT.Relu, bias=b).then_inc(s_u, 1)

            def middle_last(gb, gc, gd):
                exps(gd)
                relu(1, gb, 4)
                squares(2, gb, 2, pC[2][:, :])
                exp3(gc)
                e_rows(gd)
                relu(2, gb, 2)
                squares(4, gc, 1, pM[1][:, 0:GB * TN], cols=GB * TN)
                x_rows(gd, 1)
                squares(3, gb, 1, late3[:, :])
                ffn_relu(gd, 0)
                relu(4, gc, 1, GB * TN)
                relu(3, gb, 1)
                ffn_relu(gd, 1)
                gelu1(gb, (0, 1))
                ffn_relu(gd, 2)
                gelu1(gb, (2, 3))
                x_rows(gc, 0)
                q_rows(gc)
                v_rows(gc)
                gelu2(gb, (0,))
                copy_scores(gc)
                gelu2(gb, (1, 2, 3))

            def tail_last(gc, gd):
                exp3(gc)
                squares(4, gc, 1, pM[1][:, 0:GB * TN], cols=GB * TN)
                exps(gd)
                relu(4, gc, 1, GB * TN)
                e_rows(gd)
                x_rows(gc, 0, lateT)
                q_rows(gc, lateT)
                v_rows(gc, lateT)
                copy_scores(gc, lateT)
                x_rows(gd, 1)
                for l in range(3):
                    ffn_relu(gd, l)

            def body(gf, gb, gc, gd):
                ng = gf and nxt(gf)
                if gd: exps(gd)
                if gf: relu0(gf, 0, (0, 1, 2))
                if gb: relu(1, gb, 4)
                if gc: exp3(gc)
                if gf: relu0(gf, 0, (3, 4, 5))
                if gd: e_rows(gd)
                if gf: relu0(gf, 0, (6, 7))
                if gb: squares(2, gb, 2, pC[2][:, :])
                if gd: x_rows(gd, 1)
                if gf: squares(1, gf, 1, pC[0][:, :], 0)
                if gc: squares(4, gc, 1, pM[1][:, 0:GB * TN], cols=GB * TN)
                if gf: x_high(gf, 1)
                if gb: relu(2, gb, 2)
                if gd: ffn_relu(gd, 0)
                if gc: relu(4, gc, 1, GB * TN)
                if gf: squares(1, gf, 2, pC[1][:, :], 1)
                if gf: relu(1, gf, 1)
                if gd: ffn_relu(gd, 1)
                if gb: squares(3, gb, 1, pM[0][:, :])
                if gd: ffn_relu(gd, 2)
                if gf: relu(1, gf, 2)

                if gf: relu0(gf, 1, (0, 1, 2))
                if gc: x_rows(gc, 0)
                if gb: relu(3, gb, 1)
                if gf: relu0(gf, 1, (3, 4, 5))
                if gc: q_rows(gc)
                if gc: v_rows(gc)
                if gf: relu0(gf, 1, (6, 7))
                if gc: copy_scores(gc)
                if gf: squares(2, gf, 1, pC[2][:, :])
                if gb: gelu1(gb, range(MC))
                if gf: squares(1, gf, 3, pC[0][:, :], 0)
                if gf: x_high(ng, 0)
                if gb: gelu2(gb, (0,))
                if gf: relu(2, gf, 1)
                if gb: gelu2(gb, (1,))
                if gf: squares(1, gf, 4, pC[1][:, :], 1)
                if gf: relu(1, gf, 3)
                if gb: gelu2(gb, (2, 3))

            def conv_high(n):
                sc.wait_ge(s_wcc, n + 1)
                t = slice(CT1 * n, CT1 * n + CT1)
                do(wch[:, t, :], wc_raw[:, t, :], ACT.Copy).then_inc(s_wch, 1)

            sc.wait_ge(s_const, 32)
            conv_high(0)
            sc.wait_ge(s_ready, 1)
            x_high(PRE, 0)
            conv_high(1)
            body(PRE, None, None, None)
            body(FIRST, PRE, None, None)
            body((None, 2), FIRST, PRE, None)
            with sc.Fori(0, LOOPS) as i:
                body((i, 3), (i, 2), (i, 1), (i, 0))
            middle_last((None, NG - 1), (None, NG - 2), (None, NG - 3))
            tail_last((None, NG - 1), (None, NG - 2))
            body(None, None, None, (None, NG - 1))

        @block.vector
        def _(ve):
            V = nc.vector
            count = [0]

            def step(ins):
                count[0] += 1
                ins.then_inc(s_dset, 1)
                ve.wait_ge(s_dset, count[0])

            def split(hi, lo, x):
                step(V.tensor_copy(hi, x))
                step(V.tensor_tensor(lo, x, hi.bitcast(F32), ALU.subtract))

            ve.wait_ge(s_const, 32)
            step(V.tensor_copy(w0gain[:, KQ:K0], vec[:, OFFS:OFFS + 1]))
            ve.wait_ge(s_setup, 1)
            step(V.tensor_tensor(cen[:, :], vec[:, 0:CEN], pM[0][:, 0:CEN], ALU.subtract))
            step(V.tensor_copy(w0rep[:, :].rearrange("p (t j) -> p t j", j=PH),
                               cen[:, 0:TAPS0 + 1].unsqueeze(2).to_broadcast([128, TAPS0 + 1, PH])))
            step(V.tensor_scalar(w0gain[:, 0:KQ], w0rep[:, :], vec[:, GAIN:GAIN + 1], None, ALU.mult))
            ve.wait_ge(s_setup, 2)
            step(V.tensor_tensor(gram[:, :], pF[0:KQ, 0:KQ], cst[0:KQ, SAME:SAME + KQ], ALU.mult))
            ve.wait_ge(s_setup, 3)
            split(w0th[:, :], w0tl[:, :], pC[0][0:K0, 0:128])
            step(V.tensor_tensor(w0h[:, :, :], w0th[:, :].bitcast(F32).unsqueeze(1).to_broadcast([K0, PH, 128]),
                                 cst[0:K0, PHASE:PHASE + PH].unsqueeze(2).to_broadcast([K0, PH, 128]), ALU.mult))

            def conv_means(n):
                ve.wait_ge(s_wcload, 16)
                t = slice(CT1 * n, CT1 * n + CT1)
                step(V.tensor_reduce(wc_mean[:, t], wc_raw[:, t, :], AX, ALU.add))
                step(V.tensor_scalar(wc_mean[:, t], wc_mean[:, t], 1.0 / C, None, ALU.mult))

            def conv_centre(n):
                t = slice(CT1 * n, CT1 * n + CT1)
                V.tensor_tensor(wc_raw[:, t, :], wc_raw[:, t, :],
                                wc_mean[:, t].unsqueeze(2).to_broadcast([128, CT1, 128]), ALU.subtract)\
                    .then_inc(s_wcc, 1)

            def later_small():
                step(V.tensor_scalar(neg3[:, :], vec[:, B3:B3 + 1], -1.0, None, ALU.mult))
                ve.wait_ge(s_setup, 4)
                step(V.tensor_copy(wqk[:, :], pT[0][0:D + 1, 0:D + 1]))
                step(V.tensor_copy(wvo[:, :], pT[1][0:D + 1, 0:D]))
                step(V.tensor_copy(route_f[:, :], route_i[:, :]))
                step(V.tensor_scalar(onehot[:, :], route_f[:, :], cst[0:E, ROWNO:ROWNO + 1], None, ALU.is_equal))
                step(V.tensor_scalar(route_in[:, :], route_f[0:1, :], 0.0, None, ALU.is_ge))
                step(V.tensor_scalar(route_c[:, :], route_f[0:1, :], float(E), None, ALU.is_lt))
                step(V.tensor_tensor(route_in[:, :], route_in[:, :], route_c[:, :], ALU.mult))
                step(V.tensor_scalar(route_c[:, :], route_f[0:1, :], 0.0, float(E), ALU.max, ALU.min))
                step(V.tensor_scalar(route_c[:, :], route_c[:, :], -float(E), None, ALU.add))
                step(V.tensor_tensor(route_c[:, :], route_c[:, :], route_in[:, :], ALU.mult))
                step(V.tensor_scalar(pick[:, :], route_c[:, :], float(E), None, ALU.add))
                for l in range(2):
                    step(V.tensor_tensor(ws[:, l, :], ws[:, l, :], ident, ALU.add))
                split(brh[:, :, :], brl[:, :, :], brt[:, :, :])
                V.memset(lv[:, :], 1.0).then_inc(s_rest, 1)

            def later_mlp():
                ve.wait_ge(s_mlpw, 32)
                for hi, lo, raw in ((m1h[:, :], m1l[:, :], m1raw[:, :]), (m2h[:, :, :], m2l[:, :, :], m2raw[:, :, :])):
                    step(V.tensor_copy(hi, raw))
                    V.tensor_tensor(lo, raw, hi.bitcast(F32), ALU.subtract).then_inc(s_rest, 1)

            def add_shared(n):
                ve.wait_ge(s_raw, 16 * n + 16)
                w = wr[:, :, :, :].rearrange("p n l o -> p n (l o)")
                V.tensor_tensor(w, w, ws[:, :, :].rearrange("p l o -> p (l o)").unsqueeze(1).to_broadcast([128, NR, 256]),
                                ALU.add).then_inc(s_sum, 1)

            def quad_x(group, k):
                ve.wait_ge(s_quad, at(group, 2, k + 1))
                V.tensor_tensor(quad[:, :], pF[0:KQ, :], xt[k][:, :], ALU.mult).then_inc(s_quadx, 1)

            def eps_0(group, k):
                ve.wait_ge(s_var0, at(group, 2, k + 1))
                V.tensor_scalar(eps0[:, :], pF[:, 0:32], 1.0 / (C - 1), EPS, ALU.mult, ALU.add)\
                    .then_inc(s_eps0, 1)
                root0(group, k)

            STEPS = 10

            def root0(group, k):
                n = [k * STEPS]

                def link(ins):
                    n[0] += 1
                    ins.then_inc(s_rstd0, 1)
                    ve.wait_ge(s_rstd0, at(group, 2 * STEPS, n[0]))

                ve.wait_ge(s_eps0, at(group, 2, k + 1))
                link(V.tensor_scalar(rstd0[:, :].bitcast(I32), eps0[:, :].bitcast(I32), -0.5, float(0x5f3759df),
                                     ALU.mult, ALU.add))
                for _ in range(3):
                    link(V.tensor_tensor(newt[:, :], rstd0[:, :], rstd0[:, :], ALU.mult))
                    link(V.scalar_tensor_tensor(out=newt[:, :], in0=newt[:, :], scalar=-0.5, in1=eps0[:, :],
                                                op0=ALU.mult, op1=ALU.mult))
                    link(V.scalar_tensor_tensor(out=rstd0[:, :], in0=newt[:, :], scalar=1.5, in1=rstd0[:, :],
                                                op0=ALU.add, op1=ALU.mult))

            def spread_0(group, k):
                V.tensor_copy(rst0w[:, :, :].rearrange("p b (t j) -> p b t j", j=PH),
                              rstd0[:, :].rearrange("p (b j) -> p b j", j=PH).unsqueeze(2)
                              .to_broadcast([128, 4, TAPS0 + 1, PH])).then_inc(s_rst0w, 1)

            def scale_x(group, k):
                ve.wait_ge(s_rb0, at(group, 2, k + 1))
                V.tensor_tensor(xs[0:KQ, :], xt[k][:, :], pF[0:KQ, :], ALU.mult).then_inc(s_xs, 1)

            def low0(group, k, js):
                for j in js:
                    ve.wait_ge(s_h0h, at(group, 2 * PH, PH * k + j + 1))
                    V.scalar_tensor_tensor(out=h0[:, 1, j, :, 1:1 + NW],
                                           in0=pC[j % 3][:, :].rearrange("p (b w) -> p b w", b=2), scalar=0.0,
                                           in1=h0[:, 0, j, :, 1:1 + NW].bitcast(F32), op0=ALU.max,
                                           op1=ALU.subtract).then_inc(s_h0l, 1)

            def eps(n, group, idx, buf=0, blocks=4, bank=None):
                bank = bank or var_bank[n][buf]
                ve.wait_ge(ns[n]["var"], at(group, PER[n], idx))
                V.tensor_scalar(vare[n][:, 0:blocks], bank[:, 0:blocks], 1.0 / (C - 1), EPS, ALU.mult, ALU.add)\
                    .then_inc(ns[n]["eps"], 1)

            def norm(n, group, idx, bank, buf=0, cols=512):
                ve.wait_ge(ns[n]["rb"], at(group, PER[n], idx))
                V.tensor_tensor(y[n][buf][:, 0:cols], y[n][buf][:, 0:cols], bank[:, 0:cols], ALU.mult)\
                    .then_inc(ns[n]["z"], 1)

            def centre_f(group):
                ve.wait_ge(s_ft, at(group, 1, 1))
                p = pM[1][:, :].rearrange("p (b c) -> p b c", b=GB)
                V.tensor_reduce(fsum[:, :], p, AX, ALU.add).then_inc(s_fsum, 1)
                ve.wait_ge(s_fsum, at(group, 1, 1))
                V.tensor_scalar(fmean[:, :], fsum[:, :], 1.0 / C, None, ALU.mult).then_inc(s_fmean, 1)
                ve.wait_ge(s_fmean, at(group, 1, 1))
                V.tensor_tensor(ftc[:, :, :], p, fmean[:, :].unsqueeze(2).to_broadcast([128, GB, 128]),
                                ALU.subtract).then_inc(s_ftc, 1)

            def low1(group, ms):
                for m in ms:
                    ve.wait_ge(s_g1h, at(group, MC, m + 1))
                    V.tensor_tensor(g1l[:, m, :], g1[m % 2][:, :], g1h[:, m, :].bitcast(F32), ALU.subtract)\
                        .then_inc(s_g1l, 1)

            def sum_g2(group, ms):
                for m in ms:
                    ve.wait_ge(s_g2, at(group, MC, m + 1))
                    w = vec[:, MW3 + m:MW3 + m + 1]
                    if m == 0:
                        V.tensor_scalar(g2sum[:, :], g2[:, m, :], w, None, ALU.mult).then_inc(s_g2sum, 1)
                    else:
                        ve.wait_ge(s_g2sum, at(group, MC, m))
                        V.scalar_tensor_tensor(out=g2sum[:, :], in0=g2[:, m, :], scalar=w, in1=g2sum[:, :],
                                               op0=ALU.mult, op1=ALU.add).then_inc(s_g2sum, 1)

            def chain(s_done, per):
                k = [0]

                def link(group, ins, wait=True):
                    k[0] += 1
                    ins.then_inc(s_done, 1)
                    if wait:
                        ve.wait_ge(s_done, at(group, per, k[0]))
                return link

            def sigmoid(group):
                ve.wait_ge(s_exp3, at(group, 1, 1))
                link = chain(s_chain["sigmoid"], 2)
                link(group, V.tensor_scalar(sig[:, 1, :], sig[:, 0, :], 1.0, None, ALU.add))
                link(group, V.reciprocal(sig[:, 2, :], sig[:, 1, :]))
                V.tensor_scalar(imp[:, :], sig[:, 2, :], TEMP, None, ALU.add).then_inc(s_sig, 1)

            def normalise(group):
                ve.wait_ge(s_tot, at(group, 1, 1))
                link = chain(s_chain["total"], 1)
                link(group, V.reciprocal(rtot[:, :], pM[1][:, 0:GB]))
                V.scalar_tensor_tensor(out=impn[:, :], in0=imp[:, :], scalar=float(TN), in1=rtot[:, :],
                                       op0=ALU.mult, op1=ALU.mult).then_inc(s_impn, 1)

            def overs(group):
                ve.wait_ge(s_cum, at(group, 1, 1))
                link = chain(s_chain["over"], 1 + GB)
                link(group, V.tensor_copy(cums[:, :], pM[1][:, 0:GB]))
                for b in range(GB):
                    link(group, V.tensor_scalar(over[:, b, :], cst[:, RAMP:RAMP + TN + 1], cums[:, b:b + 1], 0.0,
                                                ALU.add, ALU.max), b == GB - 1)
                V.tensor_tensor(diff[:, :, :], over[:, :, 0:TN], over[:, :, 1:TN + 1], ALU.subtract)\
                    .then_inc(s_over, 1)

            def copy_shares(group):
                ve.wait_ge(s_wm, at(group, 1, 1))
                V.tensor_copy(wmat[:, :, :], pM[0][:, 0:GB * TN].rearrange("p (b n) -> p b n", b=GB))\
                    .then_inc(s_wmat, 1)

            def ln_stats(group, src, which):
                link = chain(s_chain[f"ln{which}"], 2 * GB)
                for b in range(GB):
                    link(group, V.bn_stats(bn[:, b, :], src[:, b, :]), False)
                wait_apart(ve, s_chain[f"ln{which}"], at(group, 2 * GB, GB))
                for b in range(GB):
                    link(group, V.bn_aggr(mv[:, b, :], bn[:, b, :]), b == GB - 1)
                V.tensor_scalar(lv[:, :], mv[:, :, 1], EPS, None, ALU.add).then_inc(s_ln[which], 1)

            def ln_apply(group, src, dst, which):
                ve.wait_ge(s_lr[which], at(group, 1, 1))
                for b in range(GB):
                    x = V.tensor_scalar(dst[:, b, :], src[:, b, :], mv[:, b, 0:1], lr[:, b:b + 1],
                                        ALU.subtract, ALU.mult)
                x.then_inc(s_lx[which], 1)

            h_rows = h[:, 0:GB * D].rearrange("p (b n) -> p b n", b=GB)

            def ln1_stats(group):
                ve.wait_ge(ns[4]["act"], at(group, 1, 1))
                ln_stats(group, h_rows, 1)

            def ln2_stats(group):
                ve.wait_ge(s_ha, at(group, 1, 1))
                ln_stats(group, ha[:, :, :], 2)

            NTOP = TOPK // 8

            def topk(group, rounds):
                for r in rounds:
                    if r == 0:
                        wait_apart(ve, s_s, at(group, 1, 1))
                    src = s if r == 0 else swork
                    for b in range(GB):
                        if r:
                            wait_apart(ve, s_top, at(group, TOPS, (2 * r - 1) * GB + b + 1))
                        V.max(top[:, b, :], src[:, b, :]).then_inc(s_top, 1)
                    if r < NTOP - 1:
                        for b in range(GB):
                            wait_apart(ve, s_top, at(group, TOPS, 2 * r * GB + b + 1))
                            V.match_replace(swork[:, b, :], top[:, b, :], src[:, b, :], NEG).then_inc(s_top, 1)
            TOPS = (2 * NTOP - 1) * GB

            def mask(group):
                ve.wait_ge(s_top, at(group, TOPS, TOPS))
                link = chain(s_chain["mask"], GB + 1)
                for b in range(GB):
                    link(group, V.scalar_tensor_tensor(out=s[:, b, :], in0=s[:, b, :], scalar=top[:, b, 7:8],
                                                       in1=s[:, b, :], op0=ALU.is_ge, op1=ALU.mult), b == GB - 1)
                link(group, V.tensor_reduce(smax[:, :], s[:, :, :], AX, ALU.max))
                V.tensor_scalar(nmax[:, :], smax[:, :], -1.0, None, ALU.mult).then_inc(s_sm, 1)

            def add_attn(group):
                ve.wait_ge(s_e, at(group, 1, 1))
                link = chain(s_chain["den"], 1)
                link(group, V.reciprocal(rden[:, :], den[:, :]), False)
                ve.wait_ge(s_hb, at(group, 1, 1))
                ve.wait_ge(s_op, at(group, 1, 1))
                ve.wait_ge(s_chain["den"], at(group, 1, 1))
                for b in range(GB):
                    x = V.scalar_tensor_tensor(out=ha[:, b, :], in0=pT[0][:, D * b:D * b + D], scalar=rden[:, b:b + 1],
                                               in1=hb[:, b, :], op0=ALU.mult, op1=ALU.add)
                x.then_inc(s_ha, 1)

            def result(group):
                ve.wait_ge(s_hc, at(group, 1, 1))
                ve.wait_ge(s_fp, at(group, 4, 4))
                V.tensor_tensor(res[:, :, :], pT[1][:, 0:GB * D].rearrange("p (b d) -> p b d", b=GB), hc[:, :, :],
                                ALU.add).then_inc(s_res, 1)

            def middle_last(gb, gc, gd):
                sigmoid(gc)
                normalise(gc)
                eps(2, gb, 2)
                overs(gc)
                norm(2, gb, 2, pC[2])
                copy_shares(gc)
                add_attn(gd)
                ln2_stats(gd)
                ln_apply(gd, ha, l2x, 2)
                eps(4, gc, 1, blocks=2)
                eps(3, gb, 1, bank=late3)
                norm(4, gc, 1, pM[0], cols=GB * TN)
                norm(3, gb, 1, late3)
                ln1_stats(gc)
                centre_f(gb)
                ln_apply(gc, h_rows, lx, 1)
                low1(gb, range(MC))
                result(gd)
                sum_g2(gb, (0,))
                topk(gc, range(0, 2))
                sum_g2(gb, (1,))
                topk(gc, range(2, 3))
                sum_g2(gb, (2,))
                topk(gc, range(3, 4))
                sum_g2(gb, (3,))

            def tail_last(gc, gd):
                topk(gd, range(4, 5))
                sigmoid(gc)
                topk(gd, range(5, 6))
                normalise(gc)
                overs(gc)
                topk(gd, range(6, 7))
                copy_shares(gc)
                topk(gd, range(7, 8))
                mask(gd)
                eps(4, gc, 1, blocks=2)
                norm(4, gc, 1, pM[0], cols=GB * TN)
                ln1_stats(gc)
                ln_apply(gc, h_rows, lx, 1)
                add_attn(gd)
                ln2_stats(gd)
                ln_apply(gd, ha, l2x, 2)
                topk(gc, range(0, 8))
                mask(gc)
                result(gd)

            def body(gf, gb, gc, gd):
                ng = gf and nxt(gf)
                if gf: low0(gf, 0, (0, 1, 2))
                if gf: quad_x(gf, 1)
                if gc: sigmoid(gc)
                if gf: low0(gf, 0, (3, 4, 5))
                if gc: normalise(gc)
                if gf: low0(gf, 0, (6, 7))
                if gc: overs(gc)
                if gd: add_attn(gd)
                if gd: ln2_stats(gd)
                if gf: eps_0(gf, 1)
                if gd: ln_apply(gd, ha, l2x, 2)
                if gc: copy_shares(gc)
                if gf: spread_0(gf, 1)
                if gb: eps(2, gb, 2)
                if gf is PRE: later_small()
                if gf is FIRST: add_shared(0)
                if gf: scale_x(gf, 1)
                if gb: norm(2, gb, 2, pC[2])
                if gc: eps(4, gc, 1, blocks=2)
                if gf: eps(1, gf, 1, 0)
                if gc: norm(4, gc, 1, pM[0], cols=GB * TN)
                if gf: norm(1, gf, 1, pC[0], 0)
                if gc: ln1_stats(gc)
                if gc: ln_apply(gc, h_rows, lx, 1)
                if gf: eps(1, gf, 2, 1)
                if gf: norm(1, gf, 2, pC[1], 1)
                if gb: eps(3, gb, 1)
                if gd: result(gd)

                if gf: low0(gf, 1, (0, 1, 2))
                if gf: quad_x(ng, 0)
                if gb: norm(3, gb, 1, pM[0])
                if gf: low0(gf, 1, (3, 4, 5))
                if gb: centre_f(gb)
                if gf: low0(gf, 1, (6, 7))
                if gf: eps_0(ng, 0)
                if gf: spread_0(ng, 0)
                if gf is PRE: later_mlp()
                if gf is FIRST: add_shared(1)
                if gc: topk(gc, range(0, 2))
                if gb: low1(gb, range(MC))
                if gc: topk(gc, range(2, 4))
                if gf: eps(2, gf, 1)
                if gf: scale_x(ng, 0)
                if gb: sum_g2(gb, (0,))
                if gc: topk(gc, range(4, 5))
                if gf: norm(2, gf, 1, pC[2])
                if gb: sum_g2(gb, (1,))
                if gf: eps(1, gf, 3, 0)
                if gc: topk(gc, range(5, 7))
                if gf: norm(1, gf, 3, pC[0], 0)
                if gf: eps(1, gf, 4, 1)
                if gc: topk(gc, range(7, 8))
                if gc: mask(gc)
                if gb: sum_g2(gb, (2,))
                if gf: norm(1, gf, 4, pC[1], 1)
                if gb: sum_g2(gb, (3,))

            quad_x(PRE, 0)
            conv_means(0)
            eps_0(PRE, 0)
            spread_0(PRE, 0)
            conv_centre(0)
            ve.wait_ge(s_ready, 1)
            scale_x(PRE, 0)
            conv_means(1)
            conv_centre(1)
            body(PRE, None, None, None)
            body(FIRST, PRE, None, None)
            body((None, 2), FIRST, PRE, None)
            with ve.Fori(0, LOOPS) as i:
                body((i, 3), (i, 2), (i, 1), (i, 0))
            middle_last((None, NG - 1), (None, NG - 2), (None, NG - 3))
            tail_last((None, NG - 1), (None, NG - 2))
            body(None, None, None, (None, NG - 1))

        @block.gpsimd
        def _(po):
            G = nc.gpsimd

            def root(out, in_):
                return G.tensor_tensor(out, in_, cst[:, HALF:HALF + in_.shape[1]], ALU.pow)

            def keep(out, in_):
                return G.tensor_scalar(out, in_, 1.0, 0.0, ALU.mult, ALU.add)

            def x_low(group, k):
                po.wait_ge(s_xh, at(group, 2, k + 1))
                G.tensor_tensor(xl[0:KQ, :], xs[0:KQ, :], xh[0:KQ, :].bitcast(F32), ALU.subtract).then_inc(s_xl, 1)

            def rootn(n, group, idx, blocks=4):
                po.wait_ge(ns[n]["eps"], at(group, PER[n], idx))
                root(rstd[n][:, 0:blocks], vare[n][:, 0:blocks]).then_inc(ns[n]["rstd"], 1)

            def pads0(group, k):
                wait_apart(po, s_h0l, at(group, 2 * PH, PH * k + PH))
                for dj, dw, sj, sw in ((6, 0, 2, 1), (7, 0, 1, 1), (0, NW + 1, 6, NW), (1, NW + 1, 5, NW)):
                    x = keep(h0[:, :, dj, :, dw:dw + 1], h0[:, :, sj, :, sw:sw + 1].bitcast(F32))
                x.then_inc(s_pad0, 1)

            def splitn(n, group, idx, hi, lo, src):
                wait_apart(po, ns[n]["act"], at(group, PER[n], idx))
                keep(hi, src).then_inc(ns[n]["hi"], 1)
                po.wait_ge(ns[n]["hi"], at(group, PER[n], idx))
                G.tensor_tensor(lo, src, hi.bitcast(F32), ALU.subtract).then_inc(ns[n]["lo"], 1)

            def split1(group, k, r):
                splitn(1, group, 2 * k + r + 1, h1[:, 0, r, :, 1:1 + T2], h1[:, 1, r, :, 1:1 + T2],
                       y[1][r][:, :].rearrange("p (b w) -> p b w", b=2))

            def pads1(group, k):
                wait_apart(po, ns[1]["lo"], at(group, 4, 2 * k + 2))
                for dr, dw, sr, sw in ((1, 0, 1, 1), (0, T2 + 1, 0, T2)):
                    x = keep(h1[:, :, dr, :, dw:dw + 1], h1[:, :, sr, :, sw:sw + 1].bitcast(F32))
                x.then_inc(s_pad1, 1)

            def split2(group, k):
                b = slice(2 * k, 2 * k + 2)
                splitn(2, group, k + 1, h2[:, 0, b, 1:1 + T2], h2[:, 1, b, 1:1 + T2],
                       y[2][0][:, :].rearrange("p (b w) -> p b w", b=2))
                wait_apart(po, ns[2]["lo"], at(group, 2, k + 1))
                for dw, sw in ((0, 2), (T2 + 1, T2 - 1)):
                    x = keep(h2[:, :, b, dw:dw + 1], h2[:, :, b, sw:sw + 1].bitcast(F32))
                x.then_inc(s_pad2, 1)

            def split3(group):
                splitn(3, group, 1, fh[:, :], fl[:, :], f[:, :])

            def high1(group, ms):
                for m in ms:
                    wait_apart(po, s_g1, at(group, MC, m + 1))
                    keep(g1h[:, m, :], g1[m % 2][:, :]).then_inc(s_g1h, 1)

            def add_bout(group, gd):
                po.wait_ge(ns[4]["act"], at(group, 1, 1))
                if gd:
                    po.wait_ge(s_ha, at(gd, 1, 1))
                G.tensor_tensor(hb[:, :, :], h[:, 0:GB * D].rearrange("p (b n) -> p b n", b=GB),
                                bout[:, :].unsqueeze(1).to_broadcast([128, GB, D]), ALU.add).then_inc(s_hb, 1)

            def add_bo(group):
                po.wait_ge(s_ha, at(group, 1, 1))
                G.tensor_tensor(hc[:, :, :], ha[:, :, :], bo[:, :].unsqueeze(1).to_broadcast([128, GB, D]),
                                ALU.add).then_inc(s_hc, 1)

            def ln_root(group, which):
                po.wait_ge(s_ln[which], at(group, 1, 1))
                root(lr[:, :], lv[:, :]).then_inc(s_lr[which], 1)

            def middle_last(gb, gc, gd):
                rootn(2, gb, 2)
                split2(gb, 1)
                ln_root(gd, 2)
                rootn(4, gc, 1, 2)
                rootn(3, gb, 1)
                add_bo(gd)
                split3(gb)
                ln_root(gc, 1)
                add_bout(gc, gd)
                high1(gb, range(MC))

            def tail_last(gc, gd):
                rootn(4, gc, 1, 2)
                ln_root(gc, 1)
                ln_root(gd, 2)
                add_bo(gd)
                add_bout(gc, gd)

            def body(gf, gb, gc, gd):
                ng = gf and nxt(gf)
                if gf: pads0(gf, 0)
                if gd: ln_root(gd, 2)
                if gb: rootn(2, gb, 2)
                if gf: x_low(gf, 1)
                if gb: split2(gb, 1)
                if gc: rootn(4, gc, 1, 2)
                if gf: rootn(1, gf, 1)
                if gd: add_bo(gd)
                if gc: ln_root(gc, 1)
                if gc: add_bout(gc, gd)
                if gf: split1(gf, 0, 0)
                if gf: rootn(1, gf, 2)
                if gf: split1(gf, 0, 1)
                if gf: pads1(gf, 0)
                if gb: rootn(3, gb, 1)

                if gb: split3(gb)
                if gf: pads0(gf, 1)
                if gb: high1(gb, range(MC))
                if gf: rootn(2, gf, 1)
                if gf: x_low(ng, 0)
                if gf: split2(gf, 0)
                if gf: rootn(1, gf, 3)
                if gf: rootn(1, gf, 4)
                if gf: split1(gf, 1, 0)
                if gf: split1(gf, 1, 1)
                if gf: pads1(gf, 1)

            G.memset(xt[0][64:KQ, :], 1.0).then_inc(s_rows, 1)
            G.memset(xt[1][64:KQ, :], 1.0).then_inc(s_rows, 1)
            po.wait_ge(s_rows, 2)
            G.memset(xs[:, :], 1.0).then_inc(s_rows, 1)
            po.wait_ge(s_rows, 3)
            keep(xh[:, :], xs[:, :]).then_inc(s_rows, 1)
            po.wait_ge(s_rows, 4)
            G.memset(xs[:, :], 0.0).then_inc(s_rows, 1)
            po.wait_ge(s_rows, 5)
            keep(xl[:, :], xs[:, :]).then_inc(s_rows, 1)
            po.wait_ge(s_rows, 6)
            G.memset(lxt[D:D + 1, :], 1.0).then_inc(s_ready, 1)

            def conv_low(n):
                po.wait_ge(s_wch, n + 1)
                t = slice(CT1 * n, CT1 * n + CT1)
                G.tensor_tensor(wcl[:, t, :], wc_raw[:, t, :], wch[:, t, :].bitcast(F32), ALU.subtract)\
                    .then_inc(s_wcl, 1)

            po.wait_ge(s_ready, 1)
            po.wait_ge(s_dset, 7)
            G.tensor_tensor(w0l[:, :, :], w0tl[:, :].bitcast(F32).unsqueeze(1).to_broadcast([K0, PH, 128]),
                            cst[0:K0, PHASE:PHASE + PH].unsqueeze(2).to_broadcast([K0, PH, 128]), ALU.mult)\
                .then_inc(s_w0l, 1)
            x_low(PRE, 0)
            conv_low(0)
            conv_low(1)
            body(PRE, None, None, None)
            body(FIRST, PRE, None, None)
            body((None, 2), FIRST, PRE, None)
            with po.Fori(0, LOOPS) as i:
                body((i, 3), (i, 2), (i, 1), (i, 0))
            middle_last((None, NG - 1), (None, NG - 2), (None, NG - 3))
            tail_last((None, NG - 1), (None, NG - 2))
            body(None, None, None, (None, NG - 1))


def shape_constants():
    c = np.zeros((128, NCONST), np.float32)
    r = np.arange(128)
    c[:, IDENT:IDENT + 128] = np.eye(128)
    c[:, TRI:TRI + 128] = r[:, None] <= r[None, :]
    c[:, SHIFT:SHIFT + 128] = np.eye(128) - np.eye(128, k=1)
    c[:, MEANS:MEANS + 128] = 1.0 / C
    c[:, ONES:ONES + 128] = 1.0
    c[:, RAMP:RAMP + TN] = -np.arange(TN)
    c[:, RAMP + TN] = -1e30
    c[:, PHASE:PHASE + PH] = (r[:, None] % PH == np.arange(PH)) | (r[:, None] == KQ)
    c[:, SAME:SAME + KQ] = r[:, None] % PH == np.arange(KQ)[None, :] % PH
    c[:, HALF:HALF + 32] = -0.5
    c[:, ROWNO] = r
    return c


def kernel(**inputs):
    import concourse.bacc as bacc
    from concourse.bass_utils import run_bass_kernel_spmd

    p = {k.replace("L0_", ""): np.asarray(x) for k, x in inputs.items()}
    x = np.pad(p["x"][:, 0, :], ((0, 0), (PAD0, PAD0)), mode="reflect")
    at_ = (STRIDE0 * PH * np.arange(NW)[None, None, :] + STRIDE0 * np.arange(PH)[None, :, None]
           + np.arange(TAPS0)[:, None, None])
    win = x[:, at_].reshape(B // 2, 2, KX, NW).transpose(0, 2, 1, 3).reshape(B // 2, KX, N)
    win = np.pad(win, ((0, 2), (0, 0), (0, 0)))
    col = lambda v: v.reshape(-1, 128).T
    vecs = np.concatenate(
        [p["tok_conv0_w"][:, 0, :]] + [p[f"tok_conv{n}_b"][:, None] for n in range(4)]
        + [p[f"tok_n{n}_w"][:, None] for n in range(5)] + [p[f"tok_n{n}_b"][:, None] for n in range(5)]
        + [col(p["tok_mlp_b1"]), col(p["tok_mlp_b2"]), col(p["tok_mlp_w3"]), col(p["ffn_bs"][0, 0]),
           col(p["ffn_bs"][1, 0]), col(p["ffn_bi"]), np.broadcast_to(p["tok_mlp_b3"][None, :], (128, 1))], axis=1)
    wconv = np.concatenate([p[f"tok_conv{n}_w"].transpose(1, 2, 0) for n in (1, 2, 3)], axis=1)
    arrays = {
        "consts": shape_constants(),
        "vecs": vecs,
        "wconv": wconv,
        "m1": p["tok_mlp_w1"],
        "m2": p["tok_mlp_w2"].reshape(MC, 128, DM).transpose(1, 0, 2),
        "wqkvt": np.concatenate([p["attn_W_qkv"], p["attn_b_qkv"][None, :]]).T.reshape(3, D, D + 1).transpose(1, 0, 2),
        "wout": p["attn_W_out"],
        "bout": np.broadcast_to(p["attn_b_out"][None, :], (128, D)),
        "wi": p["ffn_Wi"].T,
        "ws": p["ffn_Ws"][:, 0].transpose(2, 0, 1),
        "brt": p["ffn_br"].transpose(1, 0, 2),
        "wo": p["ffn_Wo"].T,
        "bo": np.broadcast_to(p["ffn_bo"][None, :], (128, D)),
        "route": np.broadcast_to(p["ffn_route_id"][None, :], (E, B * RG)),
        "wr": p["ffn_Wr"].transpose(1, 3, 0, 2),
        "x": win,
    }
    arrays = {k: np.ascontiguousarray(v) for k, v in arrays.items()}
    nc = bacc.Bacc("TRN2", target_bir_lowering=False, num_devices=1)
    a = {k: nc.dram_tensor(f"in_{k}", v.shape, mybir.dt.from_np(v.dtype), kind="ExternalInput").ap()
         for k, v in arrays.items()}
    a["sums"] = nc.dram_tensor("sums", (E + 1, 128, 2, 128), F32).ap()
    a["out"] = nc.dram_tensor("out", (B, C, TN), F32, kind="ExternalOutput").ap()
    build(nc, a)
    r = run_bass_kernel_spmd(nc, [{f"in_{k}": v for k, v in arrays.items()}], core_ids=[0])
    return r.results[0]["out"]
```
